# Optimizing a Trainium2 kernel written in Bass

```python
import numpy as np
import jax
import jax.numpy as jnp

def _softmax(x, axis=-1):
    return jax.nn.softmax(x, axis=axis)

def _gelu(x):
    return jax.nn.gelu(x, approximate=True)

def _silu(x):
    return jax.nn.silu(x)

def _sigmoid(x):
    return jax.nn.sigmoid(x)

def _layernorm(x, axis=-1, eps=1e-05):
    m = jnp.mean(x, axis=axis, keepdims=True)
    v = jnp.var(x, axis=axis, keepdims=True)
    return (x - m) / jnp.sqrt(v + eps)

def _scatter_add(tgt, idx, src, axis=0):
    return tgt.at[idx].add(src)

def _segment_sum(src, seg, n):
    return jax.ops.segment_sum(src, seg, n)
kernel_name = 'mk_decoder_postln_d1_seqx_r4_206200'

def setup_inputs(seed: int=0):
    np.random.seed(seed)
    _w = jnp.asarray

    def _rec_inputs():
        import jax
        import jax.numpy as jnp
        _rk = jax.random.key(seed)
        x = -0.0002928 + 1 * jax.random.normal(jax.random.fold_in(_rk, 1), (32, 128, 256), jnp.float32)
        _lenS = 128 - jax.random.randint(jax.random.fold_in(_rk, 7), (32,), 0, max(1, 128 // 4) + 1, jnp.int32)
        _lenS2 = 128 - jax.random.randint(jax.random.fold_in(_rk, 8), (32,), 0, max(1, 128 // 4) + 1, jnp.int32)
        _ctx_1024P = jax.random.normal(jax.random.fold_in(_rk, 11), (32, 16, 256), jnp.float32)
        _ctx_1024c = jax.random.dirichlet(jax.random.fold_in(_rk, 511), 0.3 * jnp.ones((16,), jnp.float32), (32, 128))
        _ctx_1024t = jnp.einsum('bsk,bkd->bsd', _ctx_1024c, _ctx_1024P)
        _ctx_1024t = _ctx_1024t * jax.lax.rsqrt(jnp.mean(jnp.square(_ctx_1024t)) + 1e-12) * 0.953939
        ctx_1024 = -1.39393e-06 + 0.999914 * (_ctx_1024t + 0.3 * jax.random.normal(jax.random.fold_in(_rk, 611), (32, 128, 256), jnp.float32))
        _validS = jnp.arange(128)[None, :] < _lenS[:, None]
        _validS2 = jnp.arange(128)[None, :] < _lenS2[:, None]
        _causal = jnp.tril(jnp.ones((128, 128), dtype=bool))
        mask_BxS2_bf1 = jnp.ones((32, 128), dtype=bool)
        return (x, ctx_1024, mask_BxS2_bf1)
    x, ctx_1024, mask_BxS2_bf1 = _rec_inputs()

    def _L0_attn_setup():
        import jax, jax.numpy as jnp
        import numpy as np
        HID = 256
        HK, HV = (4, 8)
        DK, DV = (128, 128)
        KEY_DIM = HK * DK
        VAL_DIM = HV * DV
        CONV_DIM = 2 * KEY_DIM + VAL_DIM
        KCONV = 4
        NEXP, TOPK, INTER = (8, 2, 128)
        EPS = 1e-06

        def zrms(x, w):
            v = jnp.mean(x * x, axis=-1, keepdims=True)
            return x * jax.lax.rsqrt(v + EPS) * (1.0 + w)

        def causal_dwconv(x, w):
            xp = jnp.pad(x, ((0, 0), (KCONV - 1, 0), (0, 0)))
            kern = w.T[:, None, :]
            return jax.lax.conv_general_dilated(xp, kern, (1,), 'VALID', dimension_numbers=('NHC', 'HIO', 'NHC'), feature_group_count=CONV_DIM)

        def gated_delta_rule(q, k, v, g, beta):
            B = q.shape[0]
            S0 = jnp.zeros((B, HV, DK, DV), q.dtype)

            def step(S, inp):
                qt, kt, vt, gt, bt = inp
                S = S * jnp.exp(gt)[..., None, None]
                kv = jnp.einsum('bhk,bhkv->bhv', kt, S)
                delta = (vt - kv) * bt[..., None]
                S = S + jnp.einsum('bhk,bhv->bhkv', kt, delta)
                o = jnp.einsum('bhk,bhkv->bhv', qt, S)
                return (S, o)
            xs = tuple((jnp.moveaxis(a, 1, 0) for a in (q, k, v, g, beta)))
            _, o = jax.lax.scan(step, S0, xs)
            return jnp.moveaxis(o, 0, 1)

        def _reference_tuple_inner(hidden_states, w_ln1, w_ln2, W_qkvz, W_ba, conv_w, dt_bias, A_log, gate_norm_w, W_out, W_router, W_gate_e, W_up_e, W_down_e):
            B, S, _ = hidden_states.shape
            resid = hidden_states
            x = zrms(hidden_states, w_ln1)
            qkvz = x @ W_qkvz
            q, k, v, z = jnp.split(qkvz, [KEY_DIM, 2 * KEY_DIM, 2 * KEY_DIM + VAL_DIM], axis=-1)
            b, a = jnp.split(x @ W_ba, 2, axis=-1)
            beta = jax.nn.sigmoid(b)
            g = -jnp.exp(A_log) * jax.nn.softplus(a + dt_bias)
            mixed = jnp.concatenate([q, k, v], axis=-1)
            mixed = jax.nn.silu(causal_dwconv(mixed, conv_w))
            q, k, v = jnp.split(mixed, [KEY_DIM, 2 * KEY_DIM], axis=-1)
            q = q.reshape(B, S, HK, DK)
            k = k.reshape(B, S, HK, DK)
            v = v.reshape(B, S, HV, DV)
            rep = HV // HK
            q = jnp.repeat(q, rep, axis=2)
            k = jnp.repeat(k, rep, axis=2)
            q = q * jax.lax.rsqrt(jnp.sum(q * q, -1, keepdims=True) + EPS)
            k = k * jax.lax.rsqrt(jnp.sum(k * k, -1, keepdims=True) + EPS)
            q = q * DK ** (-0.5)
            core = gated_delta_rule(q, k, v, g, beta)
            core = core * jax.lax.rsqrt(jnp.mean(core * core, -1, keepdims=True) + EPS) * gate_norm_w
            core = core * jax.nn.silu(z.reshape(B, S, HV, DV))
            h = resid + core.reshape(B, S, VAL_DIM) @ W_out
            resid = h
            x = zrms(h, w_ln2)
            probs = jax.nn.softmax(x @ W_router, axis=-1)
            topv, topi = jax.lax.top_k(probs, TOPK)
            topv = topv / jnp.sum(topv, -1, keepdims=True)
            route = jnp.sum(jax.nn.one_hot(topi, NEXP, dtype=x.dtype) * topv[..., None], axis=-2)
            gate_h = jnp.einsum('bsh,ehi->bsei', x, W_gate_e)
            up_h = jnp.einsum('bsh,ehi->bsei', x, W_up_e)
            exp_out = jnp.einsum('bsei,eih->bseh', jax.nn.silu(gate_h) * up_h, W_down_e)
            moe_out = jnp.einsum('bseh,bse->bsh', exp_out, route)
            return (resid + moe_out, topi)
        key = jax.random.key(seed)
        ks = jax.random.split(key, 12)

        def lin(k, shape, fan_in):
            return jax.random.normal(k, shape, jnp.float32) * fan_in ** (-0.5)
        return {'hidden_states': jax.random.normal(ks[0], (1, 512, HID), jnp.float32), 'w_ln1': jnp.zeros((HID,), jnp.float32), 'w_ln2': jnp.zeros((HID,), jnp.float32), 'W_qkvz': lin(ks[1], (HID, 2 * KEY_DIM + 2 * VAL_DIM), HID), 'W_ba': lin(ks[2], (HID, 2 * HV), HID), 'conv_w': jax.random.normal(ks[3], (CONV_DIM, KCONV), jnp.float32) * KCONV ** (-0.5), 'dt_bias': jax.random.normal(ks[4], (HV,), jnp.float32) * 0.1, 'A_log': jnp.log(jax.random.uniform(ks[5], (HV,), jnp.float32, 1.0, 16.0)), 'gate_norm_w': jnp.ones((DV,), jnp.float32), 'W_out': lin(ks[6], (VAL_DIM, HID), VAL_DIM), 'W_router': lin(ks[7], (HID, NEXP), HID), 'W_gate_e': lin(ks[8], (NEXP, HID, INTER), HID), 'W_up_e': lin(ks[9], (NEXP, HID, INTER), HID), 'W_down_e': lin(ks[10], (NEXP, INTER, HID), INTER)}
    _L0_attn_all = _L0_attn_setup()
    _L0_attn_in = {k: v for k, v in _L0_attn_all.items() if k in ('w_ln1', 'w_ln2', 'W_qkvz', 'W_ba', 'conv_w', 'dt_bias', 'A_log', 'gate_norm_w', 'W_out', 'W_router', 'W_gate_e', 'W_up_e', 'W_down_e')}
    del _L0_attn_all

    def _L0_xattn_setup():
        import jax, jax.numpy as jnp
        import numpy as np
        N_HEADS = 16
        D_MODEL = 256
        HEAD_DIM = D_MODEL // N_HEADS
        MASK_FILL = -100000000.0

        def _split_heads(x):
            B, S, _ = x.shape
            return x.reshape(B, S, N_HEADS, HEAD_DIM).transpose(0, 2, 1, 3)
        key = jax.random.key(seed)
        ks = jax.random.split(key, 12)
        B, L, P = (2, 512, 512)
        s = 1.0 / np.sqrt(D_MODEL).astype(np.float32)
        inp = {'q': jax.random.normal(ks[0], (B, L, D_MODEL), dtype=jnp.float32), 'k': jax.random.normal(ks[1], (B, P, D_MODEL), dtype=jnp.float32), 'v': jax.random.normal(ks[2], (B, P, D_MODEL), dtype=jnp.float32), 'attention_mask': jnp.ones((B, P), dtype=bool), 'Wq': jax.random.normal(ks[3], (D_MODEL, D_MODEL), dtype=jnp.float32) * s, 'bq': jnp.zeros((D_MODEL,), dtype=jnp.float32), 'Wk': jax.random.normal(ks[4], (D_MODEL, D_MODEL), dtype=jnp.float32) * s, 'bk': jnp.zeros((D_MODEL,), dtype=jnp.float32), 'Wv': jax.random.normal(ks[5], (D_MODEL, D_MODEL), dtype=jnp.float32) * s, 'bv': jnp.zeros((D_MODEL,), dtype=jnp.float32), 'Wo': jax.random.normal(ks[6], (D_MODEL, D_MODEL), dtype=jnp.float32) * s, 'bo': jnp.zeros((D_MODEL,), dtype=jnp.float32)}
        return inp
    _L0_xattn_all = _L0_xattn_setup()
    _L0_xattn_in = {k: v for k, v in _L0_xattn_all.items() if k in ('Wq', 'bq', 'Wk', 'bk', 'Wv', 'bv', 'Wo', 'bo')}
    del _L0_xattn_all

    def _L0_ffn_setup():
        import jax, jax.numpy as jnp
        import numpy as np
        NUM_COLUMNS = 16
        INPUT_DIM = 256
        NUM_NEURONS = 64
        SPARSITY = 0.05
        B, S = (4, 512)

        def _l2norm(v, axis=-1, eps=1e-12):
            n = jnp.sqrt(jnp.sum(v * v, axis=axis, keepdims=True))
            return v / jnp.maximum(n, eps)
        key = jax.random.key(seed)
        ks = jax.random.split(key, 12)
        D, C, N = (INPUT_DIM, NUM_COLUMNS, NUM_NEURONS)
        inp = {'x': jax.random.normal(ks[0], (B, S, D), dtype=jnp.float32), 'col_emb': jax.random.normal(ks[1], (C, D), dtype=jnp.float32) * 0.02, 'gate_w1': jax.random.normal(ks[2], (D, D // 2), dtype=jnp.float32) / np.sqrt(D), 'gate_b1': jnp.zeros((D // 2,), dtype=jnp.float32), 'gate_w2': jax.random.normal(ks[3], (D // 2, C), dtype=jnp.float32) / np.sqrt(D // 2), 'gate_b2': jnp.zeros((C,), dtype=jnp.float32), 'W_cols': jax.random.normal(ks[4], (C, D, N), dtype=jnp.float32) / np.sqrt(D), 'b_cols': jnp.zeros((C, N), dtype=jnp.float32), 'proj_w': jax.random.normal(ks[5], (C * N, D), dtype=jnp.float32) / np.sqrt(C * N), 'proj_b': jnp.zeros((D,), dtype=jnp.float32), 'ln_g': jnp.ones((D,), dtype=jnp.float32), 'ln_b': jnp.zeros((D,), dtype=jnp.float32)}
        return inp
    _L0_ffn_all = _L0_ffn_setup()
    _L0_ffn_in = {k: v for k, v in _L0_ffn_all.items() if k in ('col_emb', 'gate_w1', 'gate_b1', 'gate_w2', 'gate_b2', 'W_cols', 'b_cols', 'proj_w', 'proj_b', 'ln_g', 'ln_b')}
    del _L0_ffn_all
    return {'x': x, 'ctx_1024': ctx_1024, 'mask_BxS2_bf1': mask_BxS2_bf1, 'L0_attn_w_ln1': _L0_attn_in['w_ln1'], 'L0_attn_w_ln2': _L0_attn_in['w_ln2'], 'L0_attn_W_qkvz': _L0_attn_in['W_qkvz'], 'L0_attn_W_ba': _L0_attn_in['W_ba'], 'L0_attn_conv_w': _L0_attn_in['conv_w'], 'L0_attn_dt_bias': _L0_attn_in['dt_bias'], 'L0_attn_A_log': _L0_attn_in['A_log'], 'L0_attn_gate_norm_w': _L0_attn_in['gate_norm_w'], 'L0_attn_W_out': _L0_attn_in['W_out'], 'L0_attn_W_router': _L0_attn_in['W_router'], 'L0_attn_W_gate_e': _L0_attn_in['W_gate_e'], 'L0_attn_W_up_e': _L0_attn_in['W_up_e'], 'L0_attn_W_down_e': _L0_attn_in['W_down_e'], 'L0_xattn_Wq': _L0_xattn_in['Wq'], 'L0_xattn_bq': _L0_xattn_in['bq'], 'L0_xattn_Wk': _L0_xattn_in['Wk'], 'L0_xattn_bk': _L0_xattn_in['bk'], 'L0_xattn_Wv': _L0_xattn_in['Wv'], 'L0_xattn_bv': _L0_xattn_in['bv'], 'L0_xattn_Wo': _L0_xattn_in['Wo'], 'L0_xattn_bo': _L0_xattn_in['bo'], 'L0_ffn_col_emb': _L0_ffn_in['col_emb'], 'L0_ffn_gate_w1': _L0_ffn_in['gate_w1'], 'L0_ffn_gate_b1': _L0_ffn_in['gate_b1'], 'L0_ffn_gate_w2': _L0_ffn_in['gate_w2'], 'L0_ffn_gate_b2': _L0_ffn_in['gate_b2'], 'L0_ffn_W_cols': _L0_ffn_in['W_cols'], 'L0_ffn_b_cols': _L0_ffn_in['b_cols'], 'L0_ffn_proj_w': _L0_ffn_in['proj_w'], 'L0_ffn_proj_b': _L0_ffn_in['proj_b'], 'L0_ffn_ln_g': _L0_ffn_in['ln_g'], 'L0_ffn_ln_b': _L0_ffn_in['ln_b']}

def reference(x, ctx_1024, mask_BxS2_bf1, L0_attn_w_ln1, L0_attn_w_ln2, L0_attn_W_qkvz, L0_attn_W_ba, L0_attn_conv_w, L0_attn_dt_bias, L0_attn_A_log, L0_attn_gate_norm_w, L0_attn_W_out, L0_attn_W_router, L0_attn_W_gate_e, L0_attn_W_up_e, L0_attn_W_down_e, L0_xattn_Wq, L0_xattn_bq, L0_xattn_Wk, L0_xattn_bk, L0_xattn_Wv, L0_xattn_bv, L0_xattn_Wo, L0_xattn_bo, L0_ffn_col_emb, L0_ffn_gate_w1, L0_ffn_gate_b1, L0_ffn_gate_w2, L0_ffn_gate_b2, L0_ffn_W_cols, L0_ffn_b_cols, L0_ffn_proj_w, L0_ffn_proj_b, L0_ffn_ln_g, L0_ffn_ln_b):
    import jax
    import jax.numpy as jnp

    def _L0_attn_ref(hidden_states, w_ln1, w_ln2, W_qkvz, W_ba, conv_w, dt_bias, A_log, gate_norm_w, W_out, W_router, W_gate_e, W_up_e, W_down_e):
        import jax, jax.numpy as jnp
        import numpy as np
        HID = 256
        HK, HV = (4, 8)
        DK, DV = (128, 128)
        KEY_DIM = HK * DK
        VAL_DIM = HV * DV
        CONV_DIM = 2 * KEY_DIM + VAL_DIM
        KCONV = 4
        NEXP, TOPK, INTER = (8, 2, 128)
        EPS = 1e-06

        def zrms(x, w):
            v = jnp.mean(x * x, axis=-1, keepdims=True)
            return x * jax.lax.rsqrt(v + EPS) * (1.0 + w)

        def causal_dwconv(x, w):
            xp = jnp.pad(x, ((0, 0), (KCONV - 1, 0), (0, 0)))
            kern = w.T[:, None, :]
            return jax.lax.conv_general_dilated(xp, kern, (1,), 'VALID', dimension_numbers=('NHC', 'HIO', 'NHC'), feature_group_count=CONV_DIM)

        def gated_delta_rule(q, k, v, g, beta):
            B = q.shape[0]
            S0 = jnp.zeros((B, HV, DK, DV), q.dtype)

            def step(S, inp):
                qt, kt, vt, gt, bt = inp
                S = S * jnp.exp(gt)[..., None, None]
                kv = jnp.einsum('bhk,bhkv->bhv', kt, S)
                delta = (vt - kv) * bt[..., None]
                S = S + jnp.einsum('bhk,bhv->bhkv', kt, delta)
                o = jnp.einsum('bhk,bhkv->bhv', qt, S)
                return (S, o)
            xs = tuple((jnp.moveaxis(a, 1, 0) for a in (q, k, v, g, beta)))
            _, o = jax.lax.scan(step, S0, xs)
            return jnp.moveaxis(o, 0, 1)

        def _reference_tuple_inner(hidden_states, w_ln1, w_ln2, W_qkvz, W_ba, conv_w, dt_bias, A_log, gate_norm_w, W_out, W_router, W_gate_e, W_up_e, W_down_e):
            B, S, _ = hidden_states.shape
            resid = hidden_states
            x = zrms(hidden_states, w_ln1)
            qkvz = x @ W_qkvz
            q, k, v, z = jnp.split(qkvz, [KEY_DIM, 2 * KEY_DIM, 2 * KEY_DIM + VAL_DIM], axis=-1)
            b, a = jnp.split(x @ W_ba, 2, axis=-1)
            beta = jax.nn.sigmoid(b)
            g = -jnp.exp(A_log) * jax.nn.softplus(a + dt_bias)
            mixed = jnp.concatenate([q, k, v], axis=-1)
            mixed = jax.nn.silu(causal_dwconv(mixed, conv_w))
            q, k, v = jnp.split(mixed, [KEY_DIM, 2 * KEY_DIM], axis=-1)
            q = q.reshape(B, S, HK, DK)
            k = k.reshape(B, S, HK, DK)
            v = v.reshape(B, S, HV, DV)
            rep = HV // HK
            q = jnp.repeat(q, rep, axis=2)
            k = jnp.repeat(k, rep, axis=2)
            q = q * jax.lax.rsqrt(jnp.sum(q * q, -1, keepdims=True) + EPS)
            k = k * jax.lax.rsqrt(jnp.sum(k * k, -1, keepdims=True) + EPS)
            q = q * DK ** (-0.5)
            core = gated_delta_rule(q, k, v, g, beta)
            core = core * jax.lax.rsqrt(jnp.mean(core * core, -1, keepdims=True) + EPS) * gate_norm_w
            core = core * jax.nn.silu(z.reshape(B, S, HV, DV))
            h = resid + core.reshape(B, S, VAL_DIM) @ W_out
            resid = h
            x = zrms(h, w_ln2)
            probs = jax.nn.softmax(x @ W_router, axis=-1)
            topv, topi = jax.lax.top_k(probs, TOPK)
            topv = topv / jnp.sum(topv, -1, keepdims=True)
            route = jnp.sum(jax.nn.one_hot(topi, NEXP, dtype=x.dtype) * topv[..., None], axis=-2)
            gate_h = jnp.einsum('bsh,ehi->bsei', x, W_gate_e)
            up_h = jnp.einsum('bsh,ehi->bsei', x, W_up_e)
            exp_out = jnp.einsum('bsei,eih->bseh', jax.nn.silu(gate_h) * up_h, W_down_e)
            moe_out = jnp.einsum('bseh,bse->bsh', exp_out, route)
            return (resid + moe_out, topi)
        return _reference_tuple_inner(hidden_states, w_ln1, w_ln2, W_qkvz, W_ba, conv_w, dt_bias, A_log, gate_norm_w, W_out, W_router, W_gate_e, W_up_e, W_down_e)[0]

    def _L0_xattn_ref(q, k, v, attention_mask, Wq, bq, Wk, bk, Wv, bv, Wo, bo):
        import jax, jax.numpy as jnp
        import numpy as np
        N_HEADS = 16
        D_MODEL = 256
        HEAD_DIM = D_MODEL // N_HEADS
        MASK_FILL = -100000000.0

        def _split_heads(x):
            B, S, _ = x.shape
            return x.reshape(B, S, N_HEADS, HEAD_DIM).transpose(0, 2, 1, 3)
        qm = _split_heads(q @ Wq.T + bq)
        km = _split_heads(k @ Wk.T + bk)
        vm = _split_heads(v @ Wv.T + bv)
        scores = jnp.einsum('bnlh,bnph->bnlp', qm, km) / np.sqrt(HEAD_DIM).astype(np.float32)
        mask = attention_mask[:, None, None, :]
        scores = jnp.where(mask, scores, MASK_FILL)
        attn = jax.nn.softmax(scores, axis=-1)
        out = jnp.einsum('bnlp,bnph->bnlh', attn, vm)
        B, _, L, _ = out.shape
        out = out.transpose(0, 2, 1, 3).reshape(B, L, D_MODEL)
        return out @ Wo.T + bo

    def _L0_ffn_ref(x, col_emb, gate_w1, gate_b1, gate_w2, gate_b2, W_cols, b_cols, proj_w, proj_b, ln_g, ln_b):
        import jax, jax.numpy as jnp
        import numpy as np
        NUM_COLUMNS = 16
        INPUT_DIM = 256
        NUM_NEURONS = 64
        SPARSITY = 0.05
        B, S = (4, 512)

        def _l2norm(v, axis=-1, eps=1e-12):
            n = jnp.sqrt(jnp.sum(v * v, axis=axis, keepdims=True))
            return v / jnp.maximum(n, eps)
        Bq, Sq, D = x.shape
        C = col_emb.shape[0]
        similarity = jnp.einsum('bsd,cd->bsc', _l2norm(x), _l2norm(col_emb))
        h = jax.nn.gelu(x @ gate_w1 + gate_b1, approximate=False)
        gate_values = jax.nn.sigmoid(h @ gate_w2 + gate_b2)
        logits = similarity + gate_values
        k = max(1, int(C * SPARSITY))
        _, top_idx = jax.lax.top_k(logits, k)
        mask = jnp.sum(jax.nn.one_hot(top_idx, C, dtype=logits.dtype), axis=-2)
        weights = mask * jax.nn.softmax(logits, axis=-1)
        cols = jax.nn.gelu(jnp.einsum('bsd,cdn->bscn', x, W_cols) + b_cols, approximate=False)
        cols = cols * weights[..., None]
        combined = cols.reshape(Bq, Sq, -1)
        y = combined @ proj_w + proj_b + x
        mu = jnp.mean(y, axis=-1, keepdims=True)
        var = jnp.mean((y - mu) ** 2, axis=-1, keepdims=True)
        out = (y - mu) * jax.lax.rsqrt(var + 1e-05) * ln_g + ln_b
        return out
    x = _layernorm(x + _L0_attn_ref(x, L0_attn_w_ln1, L0_attn_w_ln2, L0_attn_W_qkvz, L0_attn_W_ba, L0_attn_conv_w, L0_attn_dt_bias, L0_attn_A_log, L0_attn_gate_norm_w, L0_attn_W_out, L0_attn_W_router, L0_attn_W_gate_e, L0_attn_W_up_e, L0_attn_W_down_e), axis=-1)
    x = _layernorm(x + _L0_xattn_ref(x, ctx_1024, ctx_1024, mask_BxS2_bf1, L0_xattn_Wq, L0_xattn_bq, L0_xattn_Wk, L0_xattn_bk, L0_xattn_Wv, L0_xattn_bv, L0_xattn_Wo, L0_xattn_bo), axis=-1)
    x = _layernorm(x + _L0_ffn_ref(x, L0_ffn_col_emb, L0_ffn_gate_w1, L0_ffn_gate_b1, L0_ffn_gate_w2, L0_ffn_gate_b2, L0_ffn_W_cols, L0_ffn_b_cols, L0_ffn_proj_w, L0_ffn_proj_b, L0_ffn_ln_g, L0_ffn_ln_b), axis=-1)
    return x

_drawn_inputs = setup_inputs


def setup_inputs(seed=0):
    import zlib

    import numpy as np

    out = dict(_drawn_inputs(seed))
    spreads = {'L0_attn_w_ln1': (0.0, 0.1),
     'L0_attn_w_ln2': (0.0, 0.1),
     'L0_attn_gate_norm_w': (1.0, 0.2),
     'L0_xattn_bq': (0.0, 0.389),
     'L0_xattn_bk': (0.0, 0.8),
     'L0_xattn_bv': (0.0, 0.1),
     'L0_xattn_bo': (0.0, 0.1),
     'L0_ffn_gate_b1': (0.0, 0.8),
     'L0_ffn_gate_b2': (0.0, 0.8),
     'L0_ffn_b_cols': (0.0, 0.8),
     'L0_ffn_proj_b': (0.0, 0.1),
     'L0_ffn_ln_g': (1.0, 0.2),
     'L0_ffn_ln_b': (0.0, 0.1)}
    factors = {'L0_attn_dt_bias': 4.012,
     'L0_ffn_col_emb': 8.0,
     'L0_ffn_gate_w1': 8.0,
     'L0_ffn_gate_w2': 8.0,
     'L0_ffn_W_cols': 8.0,
     'L0_ffn_proj_w': 8.0}
    for name, (base, spread) in spreads.items():
        noise = np.random.default_rng([zlib.crc32(name.encode()), seed]).standard_normal(out[name].shape)
        drawn = base * np.exp(spread * noise) if base else spread * noise
        out[name] = jnp.asarray(drawn.astype(out[name].dtype))
    for name, factor in factors.items():
        out[name] = (out[name] * factor).astype(out[name].dtype)
    return out
```

```python
from contextlib import ExitStack

import numpy as np

import concourse.bass as bass
import concourse.mybir as mybir

F32 = mybir.dt.float32
BF16 = mybir.dt.bfloat16
U8 = mybir.dt.uint8
U32 = mybir.dt.uint32
ALU = mybir.AluOpType
ACT = mybir.ActivationFunctionType
AX_X = mybir.AxisListType.X

P = 128
D = 256
KC = D // P
HK, HV = 4, 8
DK = 128
QK_BLOCKS = 2 * HK
CONV_BLOCKS = QK_BLOCKS + HV
TAPS = 4
CONV_DIM = CONV_BLOCKS * P
NEXP = 8
NH, HD = 16, 16
NCOL = 16
BLK = 32
NBLK = P // BLK
LEVELS = (2, 4, 8, 16)
EPS_RMS = 1e-6
EPS_LN = 1e-5
FILL = 1e8 * HD ** 0.5

CONST = {}
_at = 0
for _name, _width in (("ident", P), ("upto", P), ("later", P), ("above", P), ("outside", P),
                      ("level1", BLK), ("levels", len(LEVELS) * BLK), ("eye_blocks", BLK),
                      ("iota", NCOL), ("mask_row", 1), ("spread", 8 * P)):
    CONST[_name] = (_at, _at + _width)
    _at += _width
CONST_COLS = _at


def constants():
    c = np.zeros((P, CONST_COLS), np.float32)
    p = np.arange(P)[:, None]
    f = np.arange(P)[None, :]

    def put(name, a):
        c[:a.shape[0], CONST[name][0]:CONST[name][1]] = a

    put("ident", (p == f) * 1.0)
    put("upto", (p <= f) * 1.0)
    put("later", (p > f) * 1.0)
    put("above", (f > p) * -1e30)
    put("outside", (p // BLK < f // BLK) * -1.0)
    r, q = p % BLK, np.arange(BLK)[None, :]

    def sibling(s):
        return ((r // (2 * s) == q // (2 * s)) & ((r // s) % 2 == 0) & ((q // s) % 2 == 1)) * 1.0

    put("level1", -sibling(1))
    put("levels", np.concatenate([sibling(s) for s in LEVELS], 1))
    put("eye_blocks", (r == q) * 1.0)
    put("iota", np.tile(np.arange(NCOL)[None, :], (P, 1)))
    put("mask_row", (p % 32 == HD) * -1.0)
    put("spread", (np.arange(NCOL)[:, None] == np.arange(8 * P)[None, :] // 64) * 1.0)
    return c


class Signal:

    def __init__(self, ctx, nc, name, per=1):
        self.sem = ctx.enter_context(nc.semaphore(name))
        self.per = per

    def __call__(self, n, c=None):
        c = self.per if c is None else c
        return (self.sem, n * self.per if c == self.per else n * self.per - (self.per - c))


def first(n):
    return isinstance(n, int) and n == 1


SCHEDULE = (
    "a_norm", "b_ctx", "a_qkv", "b_norm", "a_z", "b_experts", "a_scales", "b_down", "a_values", "b_queries",
    "a_decay", "b_scores", "a_system", "b_probs", "a_level0", "b_attend", "a_level1", "b_proj", "a_level2",
    "b_gate", "a_level3", "b_route", "a_solve", "b_mix", "a_step0", "a_step1", "a_step2", "b_out",
    "a_read", "a_out",
)


def build(nc, x_d, ctx_d, mask_d, const_d, wqkvz_d, wba_d, convw_d, ln12_d, dt_d, alog_d, gnw_d, wout_d,
          wr_d, wg_d, wu_d, wd_d, wq_d, wk_d, wv_d, wo_d, bq_d, bk_d, bv_d, bo_d, ce_d, w1_d, b1_d, w2_d, b2_d,
          wc_d, bc_d, wp_d, bp_d, lng_d, lnb_d, out_d):
    B = x_d.shape[0]
    with ExitStack() as ctx:
        def sb(name, shape, dt=F32):
            return ctx.enter_context(nc.sbuf_tensor(name, shape, dt))

        def sig(name, per=1):
            return Signal(ctx, nc, name, per)

        const = sb("const", [P, CONST_COLS])
        wqkvz = sb("wqkvz", [P, KC, CONV_DIM + HV * P])
        wba = sb("wba", [P, KC, 2 * HV])
        convw = sb("convw", [P, CONV_BLOCKS, TAPS])
        ln12 = sb("ln12", [P, 2, KC])
        dtb = sb("dtb", [P, HV])
        negA = sb("negA", [P, HV])
        gnw = sb("gnw", [P, 1])
        wout = sb("wout", [P, HV, D])
        wr = sb("wr", [P, KC, NEXP])
        wg = sb("wg", [P, KC, NEXP * P])
        wu = sb("wu", [P, KC, NEXP * P])
        wd = sb("wd", [P, NEXP, D])
        wq = sb("wq", [P, KC, 4 * P])
        wk = sb("wk", [P, KC, 4 * P])
        wv = sb("wv", [P, KC, D])
        wo = sb("wo", [P, KC, D])
        bq = sb("bq", [P, 4])
        bk = sb("bk", [P, 4])
        rows = sb("rows", [P, 5, D])
        BV, BO, BP, LG, LB = range(5)
        ce_stat = sb("ce_stat", [NCOL, 4])
        cenT = sb("cenT", [P, KC, NCOL])
        w1 = sb("w1", [P, KC, P])
        b1 = sb("b1", [P, 1])
        w2 = sb("w2", [P, NCOL])
        b2 = sb("b2", [P, NCOL])
        wc = sb("wc", [P, KC, NCOL * 64])
        bc = sb("bc", [P, 8])
        wp = sb("wp", [P, 8, D])
        ident_bf = sb("ident_bf", [P, P], BF16)
        above_bf = sb("above_bf", [P, 4 * P], BF16)
        ones = sb("ones", [P, 1])
        nhalf = sb("nhalf", [P, NCOL])

        def con(name, rows_=P):
            a, b = CONST[name]
            return const[0:rows_, a:b]

        ident = con("ident")

        xin = sb("xin", [P, D])
        xres = sb("xres", [P, D])
        junk_a = sb("junk_a", [P, D])
        st_a = sb("st_a", [P, 4])
        xn = sb("xn", [P, D])
        xnT = sb("xnT", [P, KC, P])
        ypad = sb("ypad", [P, CONV_BLOCKS, TAPS - 1 + P])
        acc = sb("acc", [P, CONV_BLOCKS, P])
        mixed = sb("mixed", [P, CONV_BLOCKS, P])
        zs = sb("zs", [P, HV, P])
        ba = sb("ba", [P, 2 * HV])
        gate = sb("gate", [P, 10, HV])
        TB, BETA, ADT, NABS, EABS, LNP, SPM, SP, G, MINA = range(10)
        sse = sb("sse", [P, QK_BLOCKS])
        rqk = sb("rqk", [P, QK_BLOCKS])
        krb = sb("krb", [P, HV])
        ckk = sb("ckk", [P, HV])
        u = sb("u", [P, HV, P])
        gseg = sb("gseg", [P, HV, P])
        decay = sb("decay", [P, HV, P])
        lower = sb("lower", [P, HV, P])
        scoreqk = sb("scoreqk", [P, HV, P])
        scoreT = sb("scoreT", [P, HV, P])
        sqk = scoreT
        diag = sb("diag", [P, HV, BLK])
        zblk = sb("zblk", [P, HV, BLK])
        xblk = sb("xblk", [P, HV, BLK])
        ablk = sb("ablk", [P, HV, BLK])
        diagT, zinit = xblk, ablk
        zfull = sb("zfull", [P, HV, P])
        nT = gseg
        rsol = acc[:, 0:HV, :]
        tsol = [acc[:, HV:2 * HV, :], scoreqk]
        junk_o = nT
        ostat = sb("ostat", [P, 7, HV])
        OSS, RQS, RQ2, OM, OV, OP, OSC = range(7)
        core, coreT = decay, lower
        hmid = sb("hmid", [P, D])
        xh = sb("xh", [P, D])

        cin = sb("cin", [P, D])
        m_u8 = sb("m_u8", [P, P], U8)
        madj = sb("madj", [P, P])
        cT = sb("cT", [P, KC, P])
        kTm = sb("kTm", [P, 4, P])
        vaug = sb("vaug", [P, NH, HD + 1])
        junk_b = sb("junk_b", [P, D])
        st_b = sb("st_b", [P, 4])
        x2 = sb("x2", [P, D])
        x2T = sb("x2T", [P, KC, P])
        rl = sb("rl", [P, NEXP])
        top8 = sb("top8", [P, 8])
        idx8 = sb("idx8", [P, 8], U32)
        idxf = sb("idxf", [P, 2])
        rmix = sb("rmix", [P, 4])
        r12 = sb("r12", [P, 2, NEXP])
        route = sb("route", [P, NEXP])
        y1p = sb("y1p", [P, D])
        y1 = sb("y1", [P, D])
        y1b = sb("y1b", [P, D])
        bn = sb("bn", [P, 4, 6])
        mv = sb("mv", [P, 4, 2])
        lnv = sb("lnv", [P, 4, 2])
        y1T = x2T
        qT = sb("qT", [P, 4, P])
        smax = sb("smax", [P, NH])
        nmax = sb("nmax", [P, NH])
        prob = sb("prob", [P, 4, 4, P])
        probT = sb("probT", [P, 4, 4, P])
        flat = prob[:, :, :, :].rearrange("p a b f -> p (a b) f")
        sg, act_ = flat[:, 0:NEXP, :], flat[:, NEXP:2 * NEXP, :]
        actT = probT[:, 0:2, :, :].rearrange("p a b f -> p (a b) f")
        rsum = sb("rsum", [P, NH])
        ao = sb("ao", [P, NH, HD])
        aoT = x2T
        y2p = y1p
        y2 = sb("y2", [P, D])
        y2pb = y1b
        y2lb = sb("y2lb", [P, D])
        rx = sb("rx", [P, 3])
        y2T = x2T
        hT = sb("hT", [P, P])
        gc, gcw = sg, act_
        lg = sb("lg", [P, 8, NCOL])
        LBIAS, LTANH, LSIG, LOGIT, LTE, LNUM, LDEN, LEXP = range(8)
        lrec = sb("lrec", [P, NCOL])
        lmax = sb("lmax", [P, 8])
        lidx = sb("lidx", [P, 8], U32)
        lsm = sb("lsm", [P, 4])
        w16 = sb("w16", [P, NCOL])
        wT = sb("wT", [NCOL, P])
        y3p = y1p
        y3 = sb("y3", [P, D])
        y3g = x2
        y4 = sb("y4", [P, D])
        yout = sb("yout", [P, D])
        ce, ce_junk, cen = yout[0:NCOL, :], junk_b[0:NCOL, :], y4[0:NCOL, :]

        A = [ctx.enter_context(nc.psum_tensor(f"bank_a{i}", [P, 512], F32)) for i in range(4)]
        Bk = [ctx.enter_context(nc.psum_tensor(f"bank_b{i}", [P, 512], F32)) for i in range(4)]

        def quad(bank):
            return bank[:, :].rearrange("p (a b) -> p a b", b=P)

        w_a, w_b = sig("weights_a"), sig("weights_b")
        prep = sig("prep")
        filled = sig("filled")
        ce_sumsq, alog_exp, ce_rnorm, cen_ok = sig("ce_sumsq"), sig("alog_exp"), sig("ce_rnorm", 2), sig("cen_ok")
        ce_ps = sig("ce_ps")
        x_loaded, c_loaded, m_loaded = sig("x_loaded", 16), sig("c_loaded", 16), sig("m_loaded", 16)
        stored = sig("stored", 16)
        pe_passed, dve_passed, pool_passed = sig("pe_passed"), sig("dve_passed"), sig("pool_passed")
        x_sumsq, x_rstd, x_res, x_norm = sig("x_sumsq"), sig("x_rstd", 2), sig("x_res"), sig("x_norm")
        xnT_ps, xnT_ok = sig("xnT_ps"), sig("xnT_ok")
        qkv_ps, y_ok, tap_last, conv = sig("qkv_ps", 4), sig("y_ok", 4), sig("tap_last", 16), sig("conv", 48)
        mixed_ok = sig("mixed_ok", 4)
        z_ps, ba_ps, zs_ok, ba_ok = sig("z_ps", 2), sig("ba_ps"), sig("zs_ok", 2), sig("ba_ok")
        tb_ok, eln, gates = sig("tb_ok"), sig("exp_ln", 2), sig("gates", 7)
        sq_ok, ss_ps, sse_ok, rqk_ok, kscale = sig("sq_ok"), sig("ss_ps"), sig("sse_ok"), sig("rqk_ok"), sig("kscale", 2)
        vT_ps, u_ok = sig("vT_ps", 2), sig("u_ok", 2)
        gseg_ok, decay_ps, decay_ok = sig("gseg_ok", 2), sig("decay_ps", 2), sig("decay_ok", 2)
        kk_ps, qk_ps, lower_ok, score_ok = sig("kk_ps"), sig("qk_ps"), sig("lower_ok"), sig("score_ok")
        diag_ok, init_ok = sig("diag_ok"), sig("init_ok", 2)
        z_ok, x_ok = sig("z_ok", 5), sig("x_ok", 4)
        la_ps, a_ok, lb_ps = sig("la_ps", 4), sig("a_ok", 4), sig("lb_ps", 4)
        scoreT_ps, scoreT_ok = sig("scoreT_ps", 2), sig("scoreT_ok", 2)
        zfull_ok, r_ps, r_ok, n_ps, n_ok = sig("zfull_ok"), sig("r_ps", 2), sig("r_ok", 2), sig("n_ps", 2), sig("n_ok", 2)
        step_ps, step_ok = sig("step_ps", 6), sig("step_ok", 6)
        o_ps, o_sumsq, o_scale, core_ok = sig("o_ps", 2), sig("o_sumsq"), sig("o_scale", 6), sig("core_ok", 2)
        coreT_ps, coreT_ok, out_ps, h_ok, xh_ok = sig("coreT_ps", 2), sig("coreT_ok", 2), sig("out_ps"), sig("h_ok"), sig("xh_ok")

        cT_ps, cT_ok, madj_ok, k_ps, v_ps, k_ok, v_ok = (sig("cT_ps"), sig("cT_ok"), sig("madj_ok"), sig("k_ps"),
                                                         sig("v_ps"), sig("k_ok"), sig("v_ok"))
        h_sumsq, h_rstd, x2_ok, x2T_ps, x2T_ok = sig("h_sumsq"), sig("h_rstd", 2), sig("x2_ok"), sig("x2T_ps"), sig("x2T_ok")
        rl_ps, rl_ok, gu_ps, sg_ok = sig("rl_ps"), sig("rl_ok"), sig("gu_ps", 4), sig("sg_ok", 2)
        top_ok, rtanh, routing = sig("top_ok", 3), sig("rtanh"), sig("routing", 6)
        act_ok, actT_ps, actT_ok, down_ps = sig("act_ok", 2), sig("actT_ps", 2), sig("actT_ok", 2), sig("down_ps")
        ysum, ln_bn, ln_rstd, yn = sig("ysum", 3), sig("ln_bn", 8), sig("ln_rstd", 8), sig("yn", 3)
        y1b_ok, y1T_ps, y1T_ok, q_ps, q_ok = sig("y1b_ok"), sig("y1T_ps"), sig("y1T_ok"), sig("q_ps"), sig("q_ok")
        s_ps, smax_ok, nmax_ok, prob_ok = sig("s_ps"), sig("smax_ok", 4), sig("nmax_ok", 4), sig("prob_ok", 4)
        probT_ps, pTa_ok, pTv_ok = sig("probT_ps", 4), sig("probT_act", 2), sig("probT_dve", 2)
        pv_ps, rsum_ok, ao_ok, aoT_ps, aoT_ok, xo_ps = (sig("pv_ps"), sig("rsum_ok"), sig("ao_ok"), sig("aoT_ps"),
                                                        sig("aoT_ok"), sig("xo_ps"))
        y2b_ok, rx_ok, y2T_ps, y2T_ok = sig("y2b_ok", 2), sig("rx_ok", 3), sig("y2T_ps"), sig("y2T_ok")
        hg_ps, hT_ok, c_ps, gc_ok, lg_ps = sig("hg_ps"), sig("hT_ok"), sig("c_ps", 2), sig("gc_ok", 2), sig("lg_ps")
        lb_ok, ltanh, lsig, lchain = sig("lb_ok"), sig("ltanh", 2), sig("lsig"), sig("lchain", 11)
        wT_ps, wT_ok, wb_ps, gcw_ok, pj_ps = sig("wT_ps"), sig("wT_ok"), sig("wb_ps", 2), sig("gcw_ok", 2), sig("pj_ps")
        y3_ok, y_out = sig("y3_ok", 2), sig("y_out")

        loads_a = [(const, const_d), (wqkvz, wqkvz_d), (wba, wba_d), (convw, convw_d), (wout, wout_d),
                   (ln12, ln12_d), (gnw, gnw_d)]
        loads_b = [(wr, wr_d), (wg, wg_d), (wu, wu_d), (wd, wd_d), (wq, wq_d), (wk, wk_d), (wv, wv_d), (wo, wo_d),
                   (bq, bq_d), (bk, bk_d), (w1, w1_d), (w2, w2_d), (wc, wc_d), (bc, bc_d), (wp, wp_d), (ce, ce_d), (b1, b1_d)]

        small_a = [(dtb[:, :], dt_d.partition_broadcast(P)), (negA[:, :], alog_d.partition_broadcast(P))]
        small_b = [(rows[:, BV, :], bv_d.partition_broadcast(P)), (rows[:, BO, :], bo_d.partition_broadcast(P)),
                   (rows[:, BP, :], bp_d.partition_broadcast(P)), (rows[:, LG, :], lng_d.partition_broadcast(P)),
                   (rows[:, LB, :], lnb_d.partition_broadcast(P)), (b2[:, :], b2_d.partition_broadcast(P))]
        W_A = 16 * (len(loads_a) + len(small_a))
        W_B = 16 * (len(loads_b) + len(small_b))
        FILLS = 5
        PREP_A, PREP_B = 9, 13

        def heads(t, half):
            return t[:, 4 * half:4 * half + 4, :]

        def cols(ap, n):
            return ap.unsqueeze(2).to_broadcast([ap.shape[0], ap.shape[1], n])

        block = ctx.enter_context(nc.Block())

        def run(parts, engine):
            def go(n_a, n_b):
                for name in SCHEDULE:
                    n = n_a if name[0] == "a" else n_b
                    if n is not None and name in parts:
                        parts[name](n)
            go(1, None)
            go(2, 1)
            with engine.Fori(3, B + 1) as i:
                go(i, i - 1)
            go(None, B)

        @block.sync
        def _(sp):
            def load_x(n):
                if not first(n):
                    sp.wait_ge(*x_norm(n - 1))
                    sp.wait_ge(*x_res(n - 1))
                sp.dma_start(xin[:, :], x_d[n - 1, :, :]).then_inc(x_loaded.sem, 16)

            def load_ctx(n):
                if not first(n):
                    sp.wait_ge(*cT_ps(n - 1))
                    sp.wait_ge(*madj_ok(n - 1))
                sp.dma_start(cin[:, :], ctx_d[n - 1, :, :]).then_inc(c_loaded.sem, 16)
                sp.dma_start(m_u8[:, :], mask_d[n - 1, :, :].broadcast_to([P, P])).then_inc(m_loaded.sem, 16)

            def store(n):
                sp.wait_ge(*y_out(n))
                sp.dma_start(out_d[n - 1, :, :], yout[:, :]).then_inc(stored.sem, 16)

            load_x(1)
            for dst, src in loads_a:
                sp.dma_start(dst[:], src).then_inc(w_a.sem, 16)
            for dst, src in small_a:
                sp.dma_start(dst, src).then_inc(w_a.sem, 16)
            for dst, src in loads_b:
                sp.dma_start(dst[:], src).then_inc(w_b.sem, 16)
            for dst, src in small_b:
                sp.dma_start(dst, src).then_inc(w_b.sem, 16)
            load_ctx(1)
            load_x(2)
            load_x(3)
            load_ctx(2)
            store(1)
            with sp.Fori(4, B + 1) as i:
                load_x(i)
                load_ctx(i - 1)
                store(i - 2)
            load_ctx(B)
            store(B - 1)
            store(B)
            sp.wait_ge(*stored(B))

        @block.tensor
        def _(pe):
            mm, tr = nc.tensor.matmul, nc.tensor.transpose

            def a_norm(n):
                pe.wait_ge(*x_norm(n))
                for c in range(KC):
                    last = tr(A[0][:, c * P:(c + 1) * P], xn[:, c * P:(c + 1) * P], ident)
                last.then_inc(xnT_ps.sem, 1)

            def a_qkv(n):
                pe.wait_ge(*xnT_ok(n))
                for g, bank in enumerate((1, 2, 3, 0)):
                    for b in range(4):
                        o = (4 * g + b) * P
                        for c in range(KC):
                            last = mm(A[bank][:, b * P:(b + 1) * P], wqkvz[:, c, o:o + P], xnT[:, c, :],
                                      start=(c == 0), stop=(c == KC - 1))
                    last.then_inc(qkv_ps.sem, 1)

            def a_z(n):
                for half in range(2):
                    pe.wait_ge(*tap_last(n, 4 * half + 4))
                    for c in range(KC):
                        o = CONV_DIM + 512 * half
                        last = mm(A[1 + half][:, :], xnT[:, c, :], wqkvz[:, c, o:o + 512],
                                  start=(c == 0), stop=(c == KC - 1))
                    last.then_inc(z_ps.sem, 1)
                pe.wait_ge(*tap_last(n, 12))
                for c in range(KC):
                    last = mm(A[3][:, 0:2 * HV], xnT[:, c, :], wba[:, c, :], start=(c == 0), stop=(c == KC - 1))
                last.then_inc(ba_ps.sem, 1)

            def a_scales(n):
                pe.wait_ge(*ba_ok(n))
                pe.wait_ge(*sq_ok(n))
                for b in range(QK_BLOCKS):
                    last = mm(A[3][:, 16 + b:17 + b], sqk[:, b, :], ones[:, :], start=True, stop=True)
                last.then_inc(ss_ps.sem, 1)

            def a_values(n):
                for half in range(2):
                    pe.wait_ge(*mixed_ok(n, 3 + half))
                    pe.wait_ge(*zs_ok(n, 1 + half))
                    for b in range(4):
                        last = tr(A[1 + half][:, b * P:(b + 1) * P], mixed[:, QK_BLOCKS + 4 * half + b, :], ident)
                    last.then_inc(vT_ps.sem, 1)

            def a_decay(n):
                for half, bank in enumerate((0, 3)):
                    if half == 0:
                        pe.wait_ge(*tap_last(n, 16))
                    else:
                        pe.wait_ge(*sse_ok(n))
                    mm(A[bank][:, :], ident_bf[:, :], above_bf[:, :], start=True, stop=False)
                    pe.wait_ge(*gseg_ok(n, 1 + half))
                    mm(A[bank][:, :], con("upto"), heads(gseg, half), start=False, stop=True)\
                        .then_inc(decay_ps.sem, 1)

            def a_system(n):
                pe.wait_ge(*u_ok(n, 1))
                for h in range(HK):
                    k = mixed[:, HK + h, :]
                    last = mm(A[1][:, h * P:(h + 1) * P], k, k, start=True, stop=True)
                last.then_inc(kk_ps.sem, 1)
                pe.wait_ge(*u_ok(n, 2))
                for h in range(HK):
                    last = mm(A[2][:, h * P:(h + 1) * P], mixed[:, h, :], mixed[:, HK + h, :], start=True, stop=True)
                last.then_inc(qk_ps.sem, 1)

            def blocks(out, lhsT, rhs):
                for h in range(HV):
                    for b in range(NBLK):
                        r = slice(BLK * b, BLK * (b + 1))
                        last = mm(out[r, BLK * h:BLK * (h + 1)], lhsT[r, h, :], rhs[r, h, :], start=True, stop=True)
                return last

            def level(n, k):
                if k == 0:
                    pe.wait_ge(*decay_ok(n, 2))
                pe.wait_ge(*z_ok(n, k + 1)).then_inc(pe_passed.sem, 1)
                blocks(A[0], diag, zblk).then_inc(la_ps.sem, 1)
                if k < 2:
                    if k == 0:
                        pe.wait_ge(*score_ok(n))
                        pe.wait_ge(*lower_ok(n))
                    for b in range(4):
                        last = tr(A[1 + k][:, b * P:(b + 1) * P], scoreqk[:, 4 * k + b, :], ident)
                    last.then_inc(scoreT_ps.sem, 1)
                pe.wait_ge(*a_ok(n, k + 1))
                pe.wait_ge(*x_ok(n, k + 1)).then_inc(pe_passed.sem, 1)
                blocks(A[3], xblk, ablk).then_inc(lb_ps.sem, 1)

            def a_solve(n):
                pe.wait_ge(*zfull_ok(n))
                for half in range(2):
                    pe.wait_ge(*scoreT_ok(n, 1 + half))
                    for b in range(4):
                        h = 4 * half + b
                        last = mm(A[1 + half][:, b * P:(b + 1) * P], zfull[:, h, :], u[:, h, :], start=True, stop=True)
                    last.then_inc(r_ps.sem, 1)
                pe.wait_ge(*z_ok(n, 5))
                for half, bank in enumerate((0, 3)):
                    for b in range(4):
                        h = 4 * half + b
                        last = mm(A[bank][:, b * P:(b + 1) * P], lower[:, h, :], zfull[:, h, :], start=True, stop=True)
                    last.then_inc(n_ps.sem, 1)

            def step(n, k):
                for half, bank in enumerate((0, 3)):
                    if k == 0:
                        pe.wait_ge(*n_ok(n, 1 + half))
                        pe.wait_ge(*r_ok(n, 1 + half))
                    else:
                        pe.wait_ge(*step_ok(n, 2 * k - 1 + half))
                    src = rsol if k == 0 else tsol[(k - 1) % 2]
                    for b in range(4):
                        h = 4 * half + b
                        last = mm(A[bank][:, b * P:(b + 1) * P], nT[:, h, :], src[:, h, :], start=True, stop=True)
                    last.then_inc(step_ps.sem, 1)

            def a_read(n):
                for half in range(2):
                    pe.wait_ge(*step_ok(n, 5 + half))
                    for b in range(4):
                        h = 4 * half + b
                        last = mm(A[1 + half][:, b * P:(b + 1) * P], scoreT[:, h, :], tsol[0][:, h, :],
                                  start=True, stop=True)
                    last.then_inc(o_ps.sem, 1)

            def a_out(n):
                for half, bank in enumerate((0, 3)):
                    pe.wait_ge(*core_ok(n, 1 + half))
                    for b in range(4):
                        last = tr(A[bank][:, b * P:(b + 1) * P], core[:, 4 * half + b, :], ident)
                    last.then_inc(coreT_ps.sem, 1)
                for h in range(HV):
                    if h % 4 == 0:
                        pe.wait_ge(*coreT_ok(n, 1 + h // 4))
                    last = mm(A[1][:, 0:D], coreT[:, h, :], wout[:, h, :], start=(h == 0), stop=(h == HV - 1))
                last.then_inc(out_ps.sem, 1)

            def b_ctx(n):
                pe.wait_ge(*c_loaded(n))
                if not first(n):
                    pe.wait_ge(*gcw_ok(n - 1))
                for c in range(KC):
                    last = tr(Bk[0][:, c * P:(c + 1) * P], cin[:, c * P:(c + 1) * P], ident)
                last.then_inc(cT_ps.sem, 1)
                pe.wait_ge(*cT_ok(n))
                for b in range(4):
                    for c in range(KC):
                        last = mm(Bk[1][:, b * P:(b + 1) * P], wk[:, c, b * P:(b + 1) * P], cT[:, c, :],
                                  start=(c == 0), stop=(c == KC - 1))
                last.then_inc(k_ps.sem, 1)
                if not first(n):
                    pe.wait_ge(*ysum(n - 1))
                for c in range(KC):
                    last = mm(Bk[2][:, 0:D], cT[:, c, :], wv[:, c, :], start=(c == 0), stop=(c == KC - 1))
                last.then_inc(v_ps.sem, 1)

            def b_norm(n):
                pe.wait_ge(*x2_ok(n))
                for c in range(KC):
                    last = tr(Bk[3][:, c * P:(c + 1) * P], x2[:, c * P:(c + 1) * P], ident)
                last.then_inc(x2T_ps.sem, 1)

            def b_experts(n):
                pe.wait_ge(*x2T_ok(n))
                for c in range(KC):
                    last = mm(Bk[0][:, 0:NEXP], x2T[:, c, :], wr[:, c, :], start=(c == 0), stop=(c == KC - 1))
                last.then_inc(rl_ps.sem, 1)
                for i, (w, half, bank) in enumerate(((wg, 0, 1), (wu, 0, 2), (wg, 1, 3), (wu, 1, 0))):
                    if i == 0:
                        pe.wait_ge(*k_ok(n))
                    if i == 1:
                        pe.wait_ge(*v_ok(n))
                    if i == 3:
                        pe.wait_ge(*rl_ok(n))
                    for c in range(KC):
                        last = mm(Bk[bank][:, :], x2T[:, c, :], w[:, c, 512 * half:512 * half + 512],
                                  start=(c == 0), stop=(c == KC - 1))
                    last.then_inc(gu_ps.sem, 1)

            def b_down(n):
                for half, bank in enumerate((1, 3)):
                    pe.wait_ge(*act_ok(n, 1 + half))
                    for b in range(4):
                        last = tr(Bk[bank][:, b * P:(b + 1) * P], act_[:, 4 * half + b, :], ident)
                    last.then_inc(actT_ps.sem, 1)
                for e in range(NEXP):
                    if e % 4 == 0:
                        pe.wait_ge(*actT_ok(n, 1 + e // 4))
                    last = mm(Bk[2][:, 0:D], actT[:, e, :], wd[:, e, :], start=(e == 0), stop=(e == NEXP - 1))
                last.then_inc(down_ps.sem, 1)

            def b_queries(n):
                pe.wait_ge(*yn(n, 1))
                for c in range(KC):
                    last = tr(Bk[0][:, c * P:(c + 1) * P], y1[:, c * P:(c + 1) * P], ident)
                last.then_inc(y1T_ps.sem, 1)
                pe.wait_ge(*y1T_ok(n))
                for b in range(4):
                    for c in range(KC):
                        last = mm(Bk[1][:, b * P:(b + 1) * P], wq[:, c, b * P:(b + 1) * P], y1T[:, c, :],
                                  start=(c == 0), stop=(c == KC - 1))
                last.then_inc(q_ps.sem, 1)

            def b_scores(n):
                pe.wait_ge(*q_ok(n))
                for b in range(4):
                    for j in range(4):
                        r = slice(32 * j, 32 * j + 32)
                        last = mm(Bk[j][:, b * P:(b + 1) * P], qT[r, b, :], kTm[r, b, :], start=True, stop=True)
                last.then_inc(s_ps.sem, 1)

            def b_probs(n):
                for j in range(4):
                    pe.wait_ge(*prob_ok(n, j + 1))
                    for b in range(4):
                        last = tr(Bk[j][:, b * P:(b + 1) * P], prob[:, j, b, :], ident)
                    last.then_inc(probT_ps.sem, 1)

            def b_attend(n):
                pe.wait_ge(*pTa_ok(n, 2))
                pe.wait_ge(*pTv_ok(n, 2))
                for j in range(4):
                    for b in range(4):
                        h = 4 * b + j
                        last = mm(Bk[0][:, (HD + 1) * h:(HD + 1) * (h + 1)], probT[:, j, b, :], vaug[:, h, :],
                                  start=True, stop=True)
                last.then_inc(pv_ps.sem, 1)

            def b_proj(n):
                pe.wait_ge(*ao_ok(n))
                for c in range(KC):
                    last = tr(Bk[1][:, c * P:(c + 1) * P], ao[:, 8 * c:8 * c + 8, :], ident)
                last.then_inc(aoT_ps.sem, 1)
                pe.wait_ge(*aoT_ok(n))
                for c in range(KC):
                    last = mm(Bk[2][:, 0:D], aoT[:, c, :], wo[:, c, :], start=(c == 0), stop=(c == KC - 1))
                last.then_inc(xo_ps.sem, 1)

            def b_gate(n):
                pe.wait_ge(*yn(n, 2))
                for c in range(KC):
                    last = tr(Bk[3][:, c * P:(c + 1) * P], y2[:, c * P:(c + 1) * P], ident)
                last.then_inc(y2T_ps.sem, 1)
                pe.wait_ge(*y2T_ok(n))
                for c in range(KC):
                    last = mm(Bk[0][:, 0:P], w1[:, c, :], y2T[:, c, :], start=(c == 0), stop=(c == KC - 1))
                last.then_inc(hg_ps.sem, 1)
                for c in range(KC):
                    mm(Bk[1][:, 0:NCOL], y2T[:, c, :], cenT[:, c, :], start=(c == 0), stop=(c == KC - 1))
                for half in range(2):
                    for b in range(4):
                        o = (4 * half + b) * P
                        for c in range(KC):
                            last = mm(Bk[2 + half][:, b * P:(b + 1) * P], wc[:, c, o:o + P], y2T[:, c, :],
                                      start=(c == 0), stop=(c == KC - 1))
                    last.then_inc(c_ps.sem, 1)
                    if half == 0:
                        pe.wait_ge(*hT_ok(n))
                        mm(Bk[1][:, 32:32 + NCOL], hT[:, :], w2[:, :], start=True, stop=True).then_inc(lg_ps.sem, 1)

            def b_mix(n):
                pe.wait_ge(*lchain(n, 11))
                tr(Bk[0][0:NCOL, 0:P], w16[:, :], ident).then_inc(wT_ps.sem, 1)
                pe.wait_ge(*wT_ok(n))
                for half in range(2):
                    for b in range(4):
                        o = CONST["spread"][0] + (4 * half + b) * P
                        last = mm(Bk[half][:, b * P:(b + 1) * P], const[0:NCOL, o:o + P], wT[:, :], start=True, stop=True)
                    last.then_inc(wb_ps.sem, 1)
                for b in range(8):
                    if b % 4 == 0:
                        pe.wait_ge(*gcw_ok(n, 1 + b // 4))
                    last = mm(Bk[2][:, 0:D], gcw[:, b, :], wp[:, b, :], start=(b == 0), stop=(b == 7))
                last.then_inc(pj_ps.sem, 1)

            pe.wait_ge(w_a.sem, W_A)
            pe.wait_ge(filled.sem, FILLS)
            pe.wait_ge(prep.sem, PREP_A)
            pe.wait_ge(cen_ok.sem, 1)
            for c in range(KC):
                last = tr(Bk[1][:, c * P:c * P + NCOL], cen[:, c * P:(c + 1) * P], const[0:NCOL, 0:NCOL])
            last.then_inc(ce_ps.sem, 1)
            pe.wait_ge(w_b.sem, W_B)
            pe.wait_ge(prep.sem, PREP_B)
            run(dict(a_norm=a_norm, a_qkv=a_qkv, a_z=a_z, a_scales=a_scales, a_values=a_values, a_decay=a_decay,
                     a_system=a_system, a_level0=lambda n: level(n, 0), a_level1=lambda n: level(n, 1),
                     a_level2=lambda n: level(n, 2), a_level3=lambda n: level(n, 3), a_solve=a_solve,
                     a_step0=lambda n: step(n, 0), a_step1=lambda n: step(n, 1), a_step2=lambda n: step(n, 2),
                     a_read=a_read, a_out=a_out, b_ctx=b_ctx, b_norm=b_norm, b_experts=b_experts, b_down=b_down,
                     b_queries=b_queries, b_scores=b_scores, b_probs=b_probs, b_attend=b_attend, b_proj=b_proj,
                     b_gate=b_gate, b_mix=b_mix), pe)

        @block.scalar
        def _(act):
            fn = nc.scalar.activation

            def a_norm(n):
                act.wait_ge(*x_loaded(n))
                fn(junk_a[:, :], xin[:, :], ACT.Square, accum_out=st_a[:, 0:1]).then_inc(x_sumsq.sem, 1)
                act.wait_ge(*xnT_ps(n))
                fn(xnT[:, :, :], A[0][:, 0:D], ACT.Copy).then_inc(xnT_ok.sem, 1)

            def a_qkv(n):
                for g, bank in enumerate((1, 2, 3, 0)):
                    act.wait_ge(*qkv_ps(n, g + 1))
                    fn(ypad[:, 4 * g:4 * g + 4, TAPS - 1:], quad(A[bank]), ACT.Copy).then_inc(y_ok.sem, 1)
                    for b in range(4):
                        c = 4 * g + b
                        fn(acc[:, c, :], A[bank][:, b * P:(b + 1) * P], ACT.Copy, scale=convw[:, c, TAPS - 1:TAPS])\
                            .then_inc(tap_last.sem, 1)

            def a_z(n):
                for half in range(2):
                    act.wait_ge(*z_ps(n, 1 + half))
                    fn(heads(zs, half), quad(A[1 + half]), ACT.Silu).then_inc(zs_ok.sem, 1)
                act.wait_ge(*ba_ps(n))
                fn(ba[:, :], A[3][:, 0:2 * HV], ACT.Copy).then_inc(ba_ok.sem, 1)
                act.wait_ge(*ba_ok(n))
                fn(gate[:, TB, :], ba[:, 0:HV], ACT.Tanh, scale=0.5).then_inc(tb_ok.sem, 1)
                for g in range(4):
                    act.wait_ge(*conv(n, 12 * g + 12))
                    fn(mixed[:, 4 * g:4 * g + 4, :], acc[:, 4 * g:4 * g + 4, :], ACT.Silu).then_inc(mixed_ok.sem, 1)
                    if g == 1:
                        act.wait_ge(*mixed_ok(n, 2))
                        fn(sqk[:, :, :], mixed[:, 0:QK_BLOCKS, :], ACT.Square).then_inc(sq_ok.sem, 1)

            def a_decay(n):
                act.wait_ge(*gates(n, 4))
                fn(gate[:, EABS, :], gate[:, NABS, :], ACT.Exp).then_inc(eln.sem, 1)
                act.wait_ge(*eln(n, 1))
                fn(gate[:, LNP, :], gate[:, EABS, :], ACT.Ln, bias=ones[:, 0:1]).then_inc(eln.sem, 1)
                for half, bank in enumerate((0, 3)):
                    act.wait_ge(*decay_ps(n, 1 + half))
                    fn(heads(decay, half), quad(A[bank]), ACT.Exp).then_inc(decay_ok.sem, 1)

            def a_system(n):
                act.wait_ge(*lower_ok(n))
                for b in range(NBLK):
                    r = slice(BLK * b, BLK * (b + 1))
                    last = fn(diag[r, :, :], lower[r, :, r], ACT.Copy)
                last.then_inc(diag_ok.sem, 1)

            def level(n, k):
                if k < 2:
                    act.wait_ge(*scoreT_ps(n, k + 1))
                    fn(heads(scoreT, k), quad(A[1 + k]), ACT.Copy).then_inc(scoreT_ok.sem, 1)

            def a_solve(n):
                act.wait_ge(*z_ok(n, 5))
                for b in range(NBLK):
                    r = slice(BLK * b, BLK * (b + 1))
                    last = fn(zfull[r, :, r], zblk[r, :, :], ACT.Copy)
                last.then_inc(zfull_ok.sem, 1)
                for half in range(2):
                    act.wait_ge(*r_ps(n, 1 + half))
                    fn(heads(rsol, half), quad(A[1 + half]), ACT.Copy).then_inc(r_ok.sem, 1)

            def a_read(n):
                for h in range(HV):
                    if h % 4 == 0:
                        act.wait_ge(*o_ps(n, 1 + h // 4))
                    last = fn(junk_o[:, h, :], A[1 + h // 4][:, (h % 4) * P:(h % 4 + 1) * P], ACT.Square,
                              accum_out=ostat[:, OSS, h:h + 1])
                last.then_inc(o_sumsq.sem, 1)

            def a_out(n):
                for half, bank in enumerate((0, 3)):
                    act.wait_ge(*coreT_ps(n, 1 + half))
                    fn(heads(coreT, half), quad(A[bank]), ACT.Copy).then_inc(coreT_ok.sem, 1)

            def b_ctx(n):
                act.wait_ge(*cT_ps(n))
                fn(cT[:, :, :], Bk[0][:, 0:D], ACT.Copy).then_inc(cT_ok.sem, 1)
                act.wait_ge(*h_ok(n))
                fn(junk_b[:, :], hmid[:, :], ACT.Square, accum_out=st_b[:, 0:1]).then_inc(h_sumsq.sem, 1)

            def b_norm(n):
                act.wait_ge(*x2T_ps(n))
                fn(x2T[:, :, :], Bk[3][:, 0:D], ACT.Copy).then_inc(x2T_ok.sem, 1)

            def b_experts(n):
                act.wait_ge(*rl_ps(n))
                fn(rl[:, :], Bk[0][:, 0:NEXP], ACT.Copy).then_inc(rl_ok.sem, 1)
                act.wait_ge(*gu_ps(n, 1))
                fn(heads(sg, 0), quad(Bk[1]), ACT.Silu).then_inc(sg_ok.sem, 1)
                act.wait_ge(*routing(n, 1))
                fn(rmix[:, 1:2], rmix[:, 0:1], ACT.Tanh, scale=0.5).then_inc(rtanh.sem, 1)
                act.wait_ge(*gu_ps(n, 3))
                fn(heads(sg, 1), quad(Bk[3]), ACT.Silu).then_inc(sg_ok.sem, 1)

            def b_down(n):
                for half, bank in enumerate((1, 3)):
                    act.wait_ge(*actT_ps(n, 1 + half))
                    fn(heads(actT, half), quad(Bk[bank]), ACT.Copy).then_inc(actT_ok.sem, 1)

            def b_queries(n):
                act.wait_ge(*y1T_ps(n))
                fn(y1T[:, :, :], Bk[0][:, 0:D], ACT.Copy).then_inc(y1T_ok.sem, 1)
                act.wait_ge(*q_ps(n))
                for b in range(4):
                    last = fn(qT[:, b, :], Bk[1][:, b * P:(b + 1) * P], ACT.Identity, bias=bq[:, b:b + 1])
                last.then_inc(q_ok.sem, 1)

            def b_scores(n):
                for j in range(4):
                    act.wait_ge(*nmax_ok(n, j + 1))
                    for b in range(4):
                        last = fn(prob[:, j, b, :], Bk[j][:, b * P:(b + 1) * P], ACT.Exp, scale=HD ** -0.5,
                                  bias=nmax[:, 4 * j + b:4 * j + b + 1])
                    last.then_inc(prob_ok.sem, 1)

            def b_probs(n):
                for j in (0, 2):
                    act.wait_ge(*probT_ps(n, j + 1))
                    fn(probT[:, j, :, :], quad(Bk[j]), ACT.Copy).then_inc(pTa_ok.sem, 1)

            def b_proj(n):
                act.wait_ge(*aoT_ps(n))
                fn(aoT[:, :, :], Bk[1][:, 0:D], ACT.Copy).then_inc(aoT_ok.sem, 1)

            def b_gate(n):
                act.wait_ge(*y2T_ps(n))
                fn(y2T[:, :, :], Bk[3][:, 0:D], ACT.Copy).then_inc(y2T_ok.sem, 1)
                act.wait_ge(*hg_ps(n))
                fn(hT[:, :], Bk[0][:, 0:P], ACT.Gelu, bias=b1[:, 0:1]).then_inc(hT_ok.sem, 1)
                for half in range(2):
                    act.wait_ge(*c_ps(n, 1 + half))
                    for b in range(4):
                        last = fn(gc[:, 4 * half + b, :], Bk[2 + half][:, b * P:(b + 1) * P], ACT.Gelu,
                                  bias=bc[:, 4 * half + b:4 * half + b + 1])
                    last.then_inc(gc_ok.sem, 1)
                    if half == 0:
                        act.wait_ge(*lb_ok(n))
                        fn(lg[:, LTANH, :], lg[:, LBIAS, :], ACT.Tanh, scale=0.5).then_inc(ltanh.sem, 1)

            def b_route(n):
                act.wait_ge(*lchain(n, 5))
                fn(lg[:, LTE, :], lg[:, LOGIT, :], ACT.Tanh, scale=0.5, bias=lsm[:, 1:2]).then_inc(ltanh.sem, 1)

            def b_mix(n):
                act.wait_ge(*wT_ps(n))
                fn(wT[:, :], Bk[0][0:NCOL, 0:P], ACT.Copy).then_inc(wT_ok.sem, 1)

            act.wait_ge(w_b.sem, W_B)
            fn(ce_junk[:, :], ce[:, :], ACT.Square, accum_out=ce_stat[:, 0:1]).then_inc(ce_sumsq.sem, 1)
            act.wait_ge(w_a.sem, W_A)
            fn(negA[:, :], negA[:, :], ACT.Exp).then_inc(alog_exp.sem, 1)
            act.wait_ge(filled.sem, FILLS)
            run(dict(a_norm=a_norm, a_qkv=a_qkv, a_z=a_z, a_decay=a_decay, a_system=a_system,
                     a_level0=lambda n: level(n, 0), a_level1=lambda n: level(n, 1), a_solve=a_solve, a_read=a_read,
                     a_out=a_out, b_ctx=b_ctx, b_norm=b_norm, b_experts=b_experts, b_down=b_down,
                     b_queries=b_queries, b_scores=b_scores, b_probs=b_probs, b_proj=b_proj, b_gate=b_gate,
                     b_route=b_route, b_mix=b_mix), act)

        @block.vector
        def _(dve):
            tt, ts, stt = nc.vector.tensor_tensor, nc.vector.tensor_scalar, nc.vector.scalar_tensor_tensor

            def a_norm(n):
                dve.wait_ge(*x_rstd(n))
                dve.wait_ge(*x_loaded(n))
                ts(xn[:, :], xin[:, :], st_a[:, 2:3], None, ALU.mult).then_inc(x_norm.sem, 1)

            def a_qkv(n):
                for g in range(4):
                    dve.wait_ge(*y_ok(n, g + 1))
                    for k in range(TAPS - 1):
                        for b in range(4):
                            c = 4 * g + b
                            if k == 0:
                                dve.wait_ge(*tap_last(n, c + 1))
                            else:
                                dve.wait_ge(*conv(n, 12 * g + 4 * (k - 1) + b + 1))
                            stt(acc[:, c, :], ypad[:, c, k:k + P], convw[:, c, k:k + 1], acc[:, c, :],
                                ALU.mult, ALU.add).then_inc(conv.sem, 1)

            def a_scales(n):
                dve.wait_ge(*ss_ps(n))
                ts(sse[:, :], A[3][:, 16:16 + QK_BLOCKS], EPS_RMS, None, ALU.add).then_inc(sse_ok.sem, 1)

            def a_values(n):
                dve.wait_ge(*kscale(n, 1))
                for half in range(2):
                    dve.wait_ge(*vT_ps(n, 1 + half))
                    tt(heads(u, half), quad(A[1 + half]), cols(krb[:, 4 * half:4 * half + 4], P), ALU.mult)\
                        .then_inc(u_ok.sem, 1)

            def a_system(n):
                dve.wait_ge(*kk_ps(n))
                dve.wait_ge(*decay_ok(n))
                dve.wait_ge(*kscale(n, 2))
                for h in range(HV):
                    last = stt(lower[:, h, :], A[1][:, (h // 2) * P:(h // 2 + 1) * P], ckk[:, h:h + 1], decay[:, h, :],
                               ALU.mult, ALU.mult)
                last.then_inc(lower_ok.sem, 1)
                dve.wait_ge(*qk_ps(n))
                tt(scoreqk[:, :, :].rearrange("p (a b) f -> p a b f", b=2),
                   quad(A[2]).unsqueeze(2).to_broadcast([P, 4, 2, P]),
                   decay[:, :, :].rearrange("p (a b) f -> p a b f", b=2), ALU.mult).then_inc(score_ok.sem, 1)
                dve.wait_ge(*diag_ok(n))
                nc.vector.transpose(diagT[:, :, :], diag[:, :, :]).then_inc(init_ok.sem, 1)
                dve.wait_ge(*init_ok(n, 1))
                tt(zinit[:, :, :], diagT[:, :, :], con("level1").unsqueeze(1).to_broadcast([P, HV, BLK]), ALU.mult)\
                    .then_inc(init_ok.sem, 1)
                dve.wait_ge(*init_ok(n, 2))
                tt(zblk[:, :, :], zinit[:, :, :], con("eye_blocks").unsqueeze(1).to_broadcast([P, HV, BLK]), ALU.add)\
                    .then_inc(z_ok.sem, 1)
                dve.wait_ge(*z_ok(n, 1))
                nc.vector.transpose(xblk[:, :, :], zblk[:, :, :]).then_inc(x_ok.sem, 1)

            def level(n, k):
                o = CONST["levels"][0] + BLK * k
                dve.wait_ge(*la_ps(n, k + 1))
                tt(ablk[:, :, :], A[0][:, 0:HV * BLK].rearrange("p (h c) -> p h c", c=BLK),
                   const[:, o:o + BLK].unsqueeze(1).to_broadcast([P, HV, BLK]), ALU.mult).then_inc(a_ok.sem, 1)
                dve.wait_ge(*lb_ps(n, k + 1))
                tt(zblk[:, :, :], zblk[:, :, :], A[3][:, 0:HV * BLK].rearrange("p (h c) -> p h c", c=BLK),
                   ALU.subtract).then_inc(z_ok.sem, 1)
                if k < 3:
                    dve.wait_ge(*z_ok(n, k + 2))
                    nc.vector.transpose(xblk[:, :, :], zblk[:, :, :]).then_inc(x_ok.sem, 1)

            def a_solve(n):
                for half, bank in enumerate((0, 3)):
                    dve.wait_ge(*n_ps(n, 1 + half))
                    tt(heads(nT, half), quad(A[bank]), con("outside").unsqueeze(1).to_broadcast([P, 4, P]), ALU.mult)\
                        .then_inc(n_ok.sem, 1)

            def step(n, k):
                for half, bank in enumerate((0, 3)):
                    dve.wait_ge(*step_ps(n, 2 * k + 1 + half))
                    if k == 0:
                        dve.wait_ge(*r_ok(n, 1 + half))
                    tt(heads(tsol[k % 2], half), heads(rsol, half), quad(A[bank]), ALU.add).then_inc(step_ok.sem, 1)

            def a_read(n):
                dve.wait_ge(*o_scale(n))
                for h in range(HV):
                    last = stt(core[:, h, :], A[1 + h // 4][:, (h % 4) * P:(h % 4 + 1) * P], ostat[:, OSC, h:h + 1],
                               zs[:, h, :], ALU.mult, ALU.mult)
                    if h % 4 == 3:
                        last.then_inc(core_ok.sem, 1)

            def a_out(n):
                dve.wait_ge(*out_ps(n))
                dve.wait_ge(*x_res(n))
                tt(hmid[:, :], xres[:, :], A[1][:, 0:D], ALU.add).then_inc(h_ok.sem, 1)

            def stats(n, k, y):
                nc.vector.bn_stats(bn[:, k, :], y[:, :]).then_inc(ln_bn.sem, 1)
                dve.wait_ge(*ln_bn(n, 2 * k + 1)).then_inc(dve_passed.sem, 1)
                nc.vector.bn_aggr(mv[:, k, :], bn[:, k, :]).then_inc(ln_bn.sem, 1)

            def normalize(n, k, out, y):
                dve.wait_ge(*ln_rstd(n, 2 * k + 2))
                return ts(out[:, :], y[:, :], mv[:, k, 0:1], lnv[:, k, 1:2], ALU.subtract, ALU.mult)

            def b_ctx(n):
                dve.wait_ge(*k_ps(n))
                dve.wait_ge(*madj_ok(n))
                for b in range(4):
                    last = stt(kTm[:, b, :], Bk[1][:, b * P:(b + 1) * P], bk[:, b:b + 1], madj[:, :], ALU.add, ALU.mult)
                last.then_inc(k_ok.sem, 1)
                dve.wait_ge(*v_ps(n))
                tt(vaug[:, :, 0:HD], Bk[2][:, 0:D].rearrange("p (h d) -> p h d", d=HD),
                   rows[:, BV, :].rearrange("p (h d) -> p h d", d=HD), ALU.add).then_inc(v_ok.sem, 1)

            def b_norm(n):
                dve.wait_ge(*h_rstd(n))
                ts(x2[:, :], hmid[:, :], st_b[:, 2:3], None, ALU.mult).then_inc(x2_ok.sem, 1)

            def b_experts(n):
                dve.wait_ge(*rl_ok(n)).then_inc(dve_passed.sem, 1)
                nc.vector.max(top8[:, :], rl[:, :]).then_inc(top_ok.sem, 1)
                dve.wait_ge(*top_ok(n, 1)).then_inc(dve_passed.sem, 1)
                nc.vector.max_index(idx8[:, :], top8[:, :], rl[:, :]).then_inc(top_ok.sem, 1)
                dve.wait_ge(*top_ok(n, 2))
                nc.vector.tensor_copy(idxf[:, :], idx8[:, 0:2]).then_inc(top_ok.sem, 1)
                dve.wait_ge(*routing(n))
                for half, bank in enumerate((2, 0)):
                    dve.wait_ge(*gu_ps(n, 2 + 2 * half))
                    dve.wait_ge(*sg_ok(n, 1 + half))
                    for b in range(4):
                        e = 4 * half + b
                        last = stt(act_[:, e, :], Bk[bank][:, b * P:(b + 1) * P], route[:, e:e + 1], sg[:, e, :],
                                   ALU.mult, ALU.mult)
                    last.then_inc(act_ok.sem, 1)

            def b_down(n):
                dve.wait_ge(*down_ps(n))
                dve.wait_ge(*xh_ok(n))
                tt(y1p[:, :], xh[:, :], Bk[2][:, 0:D], ALU.add).then_inc(ysum.sem, 1)
                dve.wait_ge(*ysum(n, 1))
                stats(n, 0, y1p)

            def b_queries(n):
                normalize(n, 0, y1, y1p).then_inc(yn.sem, 1)

            def b_scores(n):
                dve.wait_ge(*s_ps(n))

                def scaled(j):
                    dve.wait_ge(*smax_ok(n, j + 1))
                    ts(nmax[:, 4 * j:4 * j + 4], smax[:, 4 * j:4 * j + 4], -HD ** -0.5, None, ALU.mult)\
                        .then_inc(nmax_ok.sem, 1)
                for j in range(4):
                    nc.vector.tensor_reduce(smax[:, 4 * j:4 * j + 4], quad(Bk[j]), AX_X, ALU.max).then_inc(smax_ok.sem, 1)
                    if j:
                        scaled(j - 1)
                scaled(3)

            def b_probs(n):
                for j in (1, 3):
                    dve.wait_ge(*probT_ps(n, j + 1))
                    nc.vector.tensor_copy(probT[:, j, :, :], quad(Bk[j])).then_inc(pTv_ok.sem, 1)

            def b_attend(n):
                pv = Bk[0][:, 0:NH * (HD + 1)].rearrange("p (h d) -> p h d", d=HD + 1)
                dve.wait_ge(*pv_ps(n))
                nc.vector.reciprocal(rsum[:, :].unsqueeze(2), pv[:, :, HD:HD + 1]).then_inc(rsum_ok.sem, 1)
                dve.wait_ge(*rsum_ok(n))
                tt(ao[:, :, :], pv[:, :, 0:HD], cols(rsum[:, :], HD), ALU.mult).then_inc(ao_ok.sem, 1)

            def b_proj(n):
                dve.wait_ge(*xo_ps(n))
                dve.wait_ge(*y1b_ok(n))
                tt(y2p[:, :], y1b[:, :], Bk[2][:, 0:D], ALU.add).then_inc(ysum.sem, 1)
                dve.wait_ge(*ysum(n, 2))
                stats(n, 1, y2p)

            def b_gate(n):
                normalize(n, 1, y2, y2p).then_inc(yn.sem, 1)
                dve.wait_ge(*lg_ps(n))
                tt(lg[:, LBIAS, :], Bk[1][:, 32:32 + NCOL], b2[:, :], ALU.add).then_inc(lb_ok.sem, 1)

            def b_route(n):
                dve.wait_ge(*lsig(n))
                dve.wait_ge(*rx_ok(n))
                stt(lg[:, LOGIT, :], Bk[1][:, 0:NCOL], rx[:, 2:3], lg[:, LSIG, :], ALU.mult, ALU.add)\
                    .then_inc(lchain.sem, 1)
                dve.wait_ge(*lchain(n, 1)).then_inc(dve_passed.sem, 1)
                nc.vector.max(lmax[:, :], lg[:, LOGIT, :]).then_inc(lchain.sem, 1)
                dve.wait_ge(*lchain(n, 2)).then_inc(dve_passed.sem, 1)
                nc.vector.max_index(lidx[:, :], lmax[:, :], lg[:, LOGIT, :]).then_inc(lchain.sem, 1)
                dve.wait_ge(*lchain(n, 3))
                nc.vector.tensor_copy(lsm[:, 0:1], lidx[:, 0:1]).then_inc(lchain.sem, 1)
                ts(lsm[:, 1:2], lmax[:, 0:1], -0.5, None, ALU.mult).then_inc(lchain.sem, 1)
                dve.wait_ge(*ltanh(n, 2))
                ts(lg[:, LNUM, :], lg[:, LTE, :], 1.0, None, ALU.add).then_inc(lchain.sem, 1)
                ts(lg[:, LDEN, :], lg[:, LTE, :], -1.0, 1.0, ALU.mult, ALU.add).then_inc(lchain.sem, 1)
                dve.wait_ge(*lchain(n, 7))
                nc.vector.reciprocal(lrec[:, :], lg[:, LDEN, :]).then_inc(lchain.sem, 1)
                dve.wait_ge(*lchain(n, 8))
                nc.vector.tensor_tensor_reduce(out=lg[:, LEXP, :], in0=lg[:, LNUM, :], in1=lrec[:, :], scale=1.0,
                                               scalar=0.0, op0=ALU.mult, op1=ALU.add, accum_out=lsm[:, 2:3])\
                    .then_inc(lchain.sem, 1)
                dve.wait_ge(*lchain(n, 9))
                nc.vector.reciprocal(lsm[:, 3:4], lsm[:, 2:3]).then_inc(lchain.sem, 1)
                dve.wait_ge(*lchain(n, 10))
                ts(w16[:, :], con("iota"), lsm[:, 0:1], lsm[:, 3:4], ALU.is_equal, ALU.mult).then_inc(lchain.sem, 1)

            def b_mix(n):
                for half in range(2):
                    dve.wait_ge(*wb_ps(n, 1 + half))
                    dve.wait_ge(*gc_ok(n, 1 + half))
                    tt(heads(gcw, half), heads(gc, half), quad(Bk[half]), ALU.mult).then_inc(gcw_ok.sem, 1)

            def b_out(n):
                dve.wait_ge(*pj_ps(n))
                dve.wait_ge(*y2b_ok(n))
                tt(y3p[:, :], y2pb[:, :], Bk[2][:, 0:D], ALU.add).then_inc(ysum.sem, 1)
                dve.wait_ge(*ysum(n, 3))
                stats(n, 2, y3p)
                normalize(n, 2, y3, y3p).then_inc(yn.sem, 1)
                dve.wait_ge(*yn(n, 3))
                tt(y3g[:, :], y3[:, :], rows[:, LG, :], ALU.mult).then_inc(y3_ok.sem, 1)
                dve.wait_ge(*y3_ok(n, 1))
                tt(y4[:, :], y3g[:, :], y2lb[:, :], ALU.add).then_inc(y3_ok.sem, 1)
                dve.wait_ge(*y3_ok(n, 2))
                stats(n, 3, y4)
                if not first(n):
                    dve.wait_ge(*stored(n - 1))
                normalize(n, 3, yout, y4).then_inc(y_out.sem, 1)

            dve.wait_ge(w_a.sem, W_A)
            dve.wait_ge(filled.sem, FILLS)
            ts(ln12[:, :, :], ln12[:, :, :], 1.0, None, ALU.add).then_inc(prep.sem, 1)
            nc.vector.tensor_copy(ident_bf[:, :], ident).then_inc(prep.sem, 1)
            nc.vector.tensor_copy(quad(above_bf), con("above").unsqueeze(1).to_broadcast([P, 4, P])).then_inc(prep.sem, 1)
            ts(wout[:, :, :], wout[:, :, :], gnw[:, 0:1], None, ALU.mult).then_inc(prep.sem, 1)
            dve.wait_ge(prep.sem, 4)
            for c in range(KC):
                ts(wqkvz[:, c, :], wqkvz[:, c, :], ln12[:, 0, c:c + 1], None, ALU.mult).then_inc(prep.sem, 1)
                ts(wba[:, c, :], wba[:, c, :], ln12[:, 0, c:c + 1], None, ALU.mult).then_inc(prep.sem, 1)
            dve.wait_ge(alog_exp.sem, 1)
            ts(negA[:, :], negA[:, :], -1.0, None, ALU.mult).then_inc(prep.sem, 1)
            dve.wait_ge(w_b.sem, W_B)
            for c in range(KC):
                ts(wr[:, c, :], wr[:, c, :], ln12[:, 1, c:c + 1], None, ALU.mult)
                ts(wg[:, c, :], wg[:, c, :], ln12[:, 1, c:c + 1], None, ALU.mult)
                ts(wu[:, c, :], wu[:, c, :], ln12[:, 1, c:c + 1], None, ALU.mult).then_inc(prep.sem, 1)
            dve.wait_ge(ce_rnorm.sem, 2)
            ts(cen[:, :], ce[:, :], ce_stat[:, 2:3], None, ALU.mult).then_inc(cen_ok.sem, 1)
            dve.wait_ge(ce_ps.sem, 1)
            for c in range(KC):
                nc.vector.tensor_copy(cenT[:, c, :], Bk[1][:, c * P:c * P + NCOL]).then_inc(prep.sem, 1)
            run(dict(a_norm=a_norm, a_qkv=a_qkv, a_scales=a_scales, a_values=a_values, a_system=a_system,
                     a_level0=lambda n: level(n, 0), a_level1=lambda n: level(n, 1),
                     a_level2=lambda n: level(n, 2), a_level3=lambda n: level(n, 3), a_solve=a_solve,
                     a_step0=lambda n: step(n, 0), a_step1=lambda n: step(n, 1), a_step2=lambda n: step(n, 2),
                     a_read=a_read, a_out=a_out, b_ctx=b_ctx, b_norm=b_norm, b_experts=b_experts, b_down=b_down,
                     b_queries=b_queries, b_scores=b_scores, b_probs=b_probs, b_attend=b_attend, b_proj=b_proj,
                     b_gate=b_gate, b_route=b_route, b_mix=b_mix, b_out=b_out), dve)

        @block.gpsimd
        def _(pool):
            tt, ts = nc.gpsimd.tensor_tensor, nc.gpsimd.tensor_scalar

            def power(out, base):
                return tt(out, base, nhalf[:, 0:base.shape[-1]], ALU.pow)

            def a_norm(n):
                pool.wait_ge(*x_loaded(n))
                pool.wait_ge(*x_sumsq(n)).then_inc(pool_passed.sem, 1)
                ts(st_a[:, 1:2], st_a[:, 0:1], 1.0 / D, EPS_RMS, ALU.mult, ALU.add).then_inc(x_rstd.sem, 1)
                pool.wait_ge(*x_rstd(n, 1))
                power(st_a[:, 2:3], st_a[:, 1:2]).then_inc(x_rstd.sem, 1)
                ts(xres[:, :], xin[:, :], 1.0, 0.0, ALU.mult, ALU.add).then_inc(x_res.sem, 1)

            def a_z(n):
                pool.wait_ge(*ba_ok(n))
                tt(gate[:, ADT, :], ba[:, HV:2 * HV], dtb[:, :], ALU.add).then_inc(gates.sem, 1)
                pool.wait_ge(*gates(n, 1)).then_inc(pool_passed.sem, 1)
                ts(gate[:, SPM, :], gate[:, ADT, :], 0.0, 0.0, ALU.max, ALU.add).then_inc(gates.sem, 1)
                ts(gate[:, MINA, :], gate[:, ADT, :], 0.0, 0.0, ALU.min, ALU.add).then_inc(gates.sem, 1)
                pool.wait_ge(*gates(n, 3))
                tt(gate[:, NABS, :], gate[:, MINA, :], gate[:, SPM, :], ALU.subtract).then_inc(gates.sem, 1)

            def pairs(ap):
                return ap.rearrange("p (a b) -> p a b", b=HV // HK)

            def a_scales(n):
                pool.wait_ge(*tb_ok(n)).then_inc(pool_passed.sem, 1)
                ts(gate[:, BETA, :], gate[:, TB, :], 0.5, 0.5, ALU.mult, ALU.add).then_inc(gates.sem, 1)
                pool.wait_ge(*sse_ok(n))
                power(rqk[:, :], sse[:, :]).then_inc(rqk_ok.sem, 1)
                pool.wait_ge(*rqk_ok(n))
                pool.wait_ge(*gates(n, 5))
                rk = cols(rqk[:, HK:2 * HK], HV // HK)
                tt(pairs(krb[:, :]), pairs(gate[:, BETA, :]), rk, ALU.mult).then_inc(kscale.sem, 1)
                pool.wait_ge(*kscale(n, 1))
                tt(pairs(ckk[:, :]), pairs(krb[:, :]), rk, ALU.mult).then_inc(kscale.sem, 1)

            def a_decay(n):
                pool.wait_ge(*eln(n))
                tt(gate[:, SP, :], gate[:, SPM, :], gate[:, LNP, :], ALU.add).then_inc(gates.sem, 1)
                pool.wait_ge(*gates(n, 6))
                tt(gate[:, G, :], gate[:, SP, :], negA[:, :], ALU.mult).then_inc(gates.sem, 1)
                pool.wait_ge(*gates(n, 7)).then_inc(pool_passed.sem, 1)
                for h in range(HV):
                    last = ts(gseg[:, h, :], con("later"), gate[:, G, h:h + 1], None, ALU.mult)
                    if h % 4 == 3:
                        last.then_inc(gseg_ok.sem, 1)

            def a_read(n):
                ts(ostat[:, RQS, 0:HK], rqk[:, 0:HK], DK ** -0.5, 0.0, ALU.mult, ALU.add).then_inc(o_scale.sem, 1)
                pool.wait_ge(*o_scale(n, 1))
                rq = cols(ostat[:, RQS, 0:HK], HV // HK)
                tt(pairs(ostat[:, RQ2, :]), rq, rq, ALU.mult).then_inc(o_scale.sem, 1)
                pool.wait_ge(*o_scale(n, 2))
                pool.wait_ge(*o_sumsq(n))
                tt(ostat[:, OM, :], ostat[:, OSS, :], ostat[:, RQ2, :], ALU.mult).then_inc(o_scale.sem, 1)
                pool.wait_ge(*o_scale(n, 3)).then_inc(pool_passed.sem, 1)
                ts(ostat[:, OV, :], ostat[:, OM, :], 1.0 / P, EPS_RMS, ALU.mult, ALU.add).then_inc(o_scale.sem, 1)
                pool.wait_ge(*o_scale(n, 4))
                power(ostat[:, OP, :], ostat[:, OV, :]).then_inc(o_scale.sem, 1)
                pool.wait_ge(*o_scale(n, 5))
                tt(pairs(ostat[:, OSC, :]), pairs(ostat[:, OP, :]), rq, ALU.mult).then_inc(o_scale.sem, 1)

            def a_out(n):
                pool.wait_ge(*h_ok(n))
                tt(xh[:, :], hmid[:, :], xres[:, :], ALU.add).then_inc(xh_ok.sem, 1)

            def b_ctx(n):
                pool.wait_ge(*m_loaded(n)).then_inc(pool_passed.sem, 1)
                ts(madj[:, :], m_u8[:, :], con("mask_row"), None, ALU.add).then_inc(madj_ok.sem, 1)

            def b_norm(n):
                pool.wait_ge(*h_sumsq(n)).then_inc(pool_passed.sem, 1)
                ts(st_b[:, 1:2], st_b[:, 0:1], 1.0 / D, EPS_RMS, ALU.mult, ALU.add).then_inc(h_rstd.sem, 1)
                pool.wait_ge(*h_rstd(n, 1))
                power(st_b[:, 2:3], st_b[:, 1:2]).then_inc(h_rstd.sem, 1)

            def b_experts(n):
                pool.wait_ge(*top_ok(n))
                tt(rmix[:, 0:1], top8[:, 0:1], top8[:, 1:2], ALU.subtract).then_inc(routing.sem, 1)
                pool.wait_ge(*rtanh(n)).then_inc(pool_passed.sem, 1)
                for i, sign in enumerate((0.5, -0.5)):
                    ts(rmix[:, 2 + i:3 + i], rmix[:, 1:2], sign, 0.5, ALU.mult, ALU.add).then_inc(routing.sem, 1)
                pool.wait_ge(*routing(n, 3)).then_inc(pool_passed.sem, 1)
                for i in range(2):
                    ts(r12[:, i, :], const[:, CONST["iota"][0]:CONST["iota"][0] + NEXP], idxf[:, i:i + 1],
                       rmix[:, 2 + i:3 + i], ALU.is_equal, ALU.mult).then_inc(routing.sem, 1)
                pool.wait_ge(*routing(n, 5))
                tt(route[:, :], r12[:, 0, :], r12[:, 1, :], ALU.add).then_inc(routing.sem, 1)

            def rstd(n, k):
                pool.wait_ge(*ln_bn(n, 2 * k + 2)).then_inc(pool_passed.sem, 1)
                ts(lnv[:, k, 0:1], mv[:, k, 1:2], 1.0, EPS_LN, ALU.mult, ALU.add).then_inc(ln_rstd.sem, 1)
                pool.wait_ge(*ln_rstd(n, 2 * k + 1))
                power(lnv[:, k, 1:2], lnv[:, k, 0:1]).then_inc(ln_rstd.sem, 1)

            def b_queries(n):
                pool.wait_ge(*yn(n, 1))
                tt(y1b[:, :], y1[:, :], rows[:, BO, :], ALU.add).then_inc(y1b_ok.sem, 1)

            def b_gate(n):
                pool.wait_ge(*ln_rstd(n, 4)).then_inc(pool_passed.sem, 1)
                ts(rx[:, 0:1], mv[:, 1, 1:2], lnv[:, 1, 1:2], lnv[:, 1, 1:2], ALU.mult, ALU.mult).then_inc(rx_ok.sem, 1)
                pool.wait_ge(*rx_ok(n, 1)).then_inc(pool_passed.sem, 1)
                ts(rx[:, 1:2], rx[:, 0:1], float(D), 1e-24, ALU.mult, ALU.max).then_inc(rx_ok.sem, 1)
                pool.wait_ge(*rx_ok(n, 2))
                power(rx[:, 2:3], rx[:, 1:2]).then_inc(rx_ok.sem, 1)
                pool.wait_ge(*yn(n, 2))
                for out, row in ((y2pb, BP), (y2lb, LB)):
                    tt(out[:, :], y2[:, :], rows[:, row, :], ALU.add).then_inc(y2b_ok.sem, 1)
                pool.wait_ge(*ltanh(n, 1)).then_inc(pool_passed.sem, 1)
                ts(lg[:, LSIG, :], lg[:, LTANH, :], 0.5, 0.5, ALU.mult, ALU.add).then_inc(lsig.sem, 1)

            def b_out(n):
                rstd(n, 2)
                rstd(n, 3)

            nc.gpsimd.memset(nhalf[:, :], -0.5).then_inc(filled.sem, 1)
            nc.gpsimd.memset(ones[:, :], 1.0).then_inc(filled.sem, 1)
            nc.gpsimd.memset(ypad[:, :, 0:TAPS - 1], 0.0).then_inc(filled.sem, 1)
            nc.gpsimd.memset(zfull[:, :, :], 0.0).then_inc(filled.sem, 1)
            nc.gpsimd.memset(vaug[:, :, :], 1.0).then_inc(filled.sem, 1)
            pool.wait_ge(filled.sem, FILLS)
            pool.wait_ge(ce_sumsq.sem, 1)
            ts(ce_stat[:, 1:2], ce_stat[:, 0:1], 1.0, 1e-24, ALU.mult, ALU.max).then_inc(ce_rnorm.sem, 1)
            pool.wait_ge(ce_rnorm.sem, 1)
            tt(ce_stat[:, 2:3], ce_stat[:, 1:2], nhalf[0:NCOL, 0:1], ALU.pow).then_inc(ce_rnorm.sem, 1)
            pool.wait_ge(w_a.sem, W_A)
            pool.wait_ge(w_b.sem, W_B)
            pool.wait_ge(prep.sem, PREP_A)
            run(dict(a_norm=a_norm, a_z=a_z, a_scales=a_scales, a_decay=a_decay, a_read=a_read, a_out=a_out,
                     b_ctx=b_ctx, b_norm=b_norm, b_experts=b_experts, b_down=lambda n: rstd(n, 0),
                     b_queries=b_queries, b_proj=lambda n: rstd(n, 1), b_gate=b_gate, b_out=b_out), pool)


def kernel(**inputs):
    import concourse.bacc as bacc
    from concourse.bass_utils import run_bass_kernel_spmd

    a = {k.split("_", 2)[2] if k.startswith("L0") else k: np.asarray(v) for k, v in inputs.items()}

    def rows_first(w):
        return w.reshape(-1, P, w.shape[-1]).transpose(1, 0, 2)

    def experts(w):
        e, d, i = w.shape
        return w.reshape(e, KC, P, i).transpose(2, 1, 0, 3).reshape(P, KC, e * i)

    def head_rows(w):
        out = np.zeros((4, 4, 32, D), w.dtype)
        out[:, :, :HD] = w.reshape(4, 4, HD, D)
        return rows_first(out.reshape(4 * P, D).T)

    def head_bias(b, extra):
        out = np.zeros((4, 4, 32), b.dtype)
        out[:, :, :HD] = b.reshape(4, 4, HD)
        out[:, :, HD] = extra
        return out.transpose(1, 2, 0).reshape(P, 4)

    arrays = dict(
        x=a["x"], ctx=a["ctx_1024"], mask=a["mask_BxS2_bf1"].astype(np.uint8)[:, None, :], const=constants(),
        wqkvz=rows_first(a["W_qkvz"]), wba=rows_first(a["W_ba"]),
        convw=a["conv_w"].reshape(CONV_BLOCKS, P, TAPS).transpose(1, 0, 2),
        ln12=np.stack([a["w_ln1"].reshape(KC, P).T, a["w_ln2"].reshape(KC, P).T], 1),
        dt=a["dt_bias"], alog=a["A_log"], gnw=a["gate_norm_w"][:, None], wout=rows_first(a["W_out"]),
        wr=rows_first(a["W_router"]), wg=experts(a["W_gate_e"]), wu=experts(a["W_up_e"]),
        wd=a["W_down_e"].transpose(1, 0, 2),
        wq=head_rows(a["Wq"]), wk=head_rows(a["Wk"]), wv=rows_first(a["Wv"].T), wo=rows_first(a["Wo"].T),
        bq=head_bias(a["bq"], 1.0), bk=head_bias(a["bk"], FILL), bv=a["bv"], bo=a["bo"],
        ce=a["col_emb"], w1=rows_first(a["gate_w1"]), b1=a["gate_b1"][:, None], w2=a["gate_w2"], b2=a["gate_b2"],
        wc=experts(a["W_cols"]), bc=a["b_cols"].reshape(8, P).T, wp=rows_first(a["proj_w"]), bp=a["proj_b"],
        lng=a["ln_g"], lnb=a["ln_b"])
    nc = bacc.Bacc("TRN2", target_bir_lowering=False, num_devices=1)
    data, args = {}, []
    for name, v in arrays.items():
        v = np.ascontiguousarray(v)
        data[f"in_{name}_dram"] = v
        args.append(nc.dram_tensor(f"in_{name}_dram", v.shape, mybir.dt.from_np(v.dtype), kind="ExternalInput").ap())
    args.append(nc.dram_tensor("out_0_dram", a["x"].shape, F32, kind="ExternalOutput").ap())
    build(nc, *args)
    r = run_bass_kernel_spmd(nc, [data], core_ids=[0])
    return r.results[0]["out_0_dram"]
```

```python
from contextlib import ExitStack

import numpy as np

import concourse.bass as bass
import concourse.mybir as mybir

F32 = mybir.dt.float32
BF16 = mybir.dt.bfloat16
U8 = mybir.dt.uint8
U32 = mybir.dt.uint32
ALU = mybir.AluOpType
ACT = mybir.ActivationFunctionType
AX_X = mybir.AxisListType.X

P = 128
D = 256
KC = D // P
HK, HV = 4, 8
DK = 128
QK_BLOCKS = 2 * HK
CONV_BLOCKS = QK_BLOCKS + HV
TAPS = 4
CONV_DIM = CONV_BLOCKS * P
NEXP = 8
NH, HD = 16, 16
NCOL = 16
BLK = 32
NBLK = P // BLK
LEVELS = (2, 4, 8, 16)
EPS_RMS = 1e-6
EPS_LN = 1e-5
FILL = 1e8 * HD ** 0.5

CONST = {}
_at = 0
for _name, _width in (("ident", P), ("upto", P), ("later", P), ("above", P), ("outside", P),
                      ("level1", BLK), ("levels", len(LEVELS) * BLK), ("eye_blocks", BLK),
                      ("iota", NCOL), ("mask_row", 1), ("quadrant", 4)):
    CONST[_name] = (_at, _at + _width)
    _at += _width
CONST_COLS = _at


def constants():
    c = np.zeros((P, CONST_COLS), np.float32)
    p = np.arange(P)[:, None]
    f = np.arange(P)[None, :]

    def put(name, a):
        c[:a.shape[0], CONST[name][0]:CONST[name][1]] = a

    put("ident", (p == f) * 1.0)
    put("upto", (p <= f) * 1.0)
    put("later", (p > f) * 1.0)
    put("above", (f > p) * -1e30)
    put("outside", (p // BLK < f // BLK) * -1.0)
    r, q = p % BLK, np.arange(BLK)[None, :]

    def sibling(s):
        return ((r // (2 * s) == q // (2 * s)) & ((r // s) % 2 == 0) & ((q // s) % 2 == 1)) * 1.0

    put("level1", -sibling(1))
    put("levels", np.concatenate([sibling(s) for s in LEVELS], 1))
    put("eye_blocks", (r == q) * 1.0)
    put("iota", np.tile(np.arange(NCOL)[None, :], (P, 1)))
    put("mask_row", (p % 32 == HD) * -1.0)
    put("quadrant", (p // 32 == np.arange(4)[None, :]) * 1.0)
    return c


def spread():
    return ((np.arange(NCOL)[:, None] == np.arange(8 * P)[None, :] // 64) * 1.0).astype(np.float32)


class Signal:

    def __init__(self, ctx, nc, name, per=1):
        self.sem = ctx.enter_context(nc.semaphore(name))
        self.per = per

    def __call__(self, n, c=None):
        c = self.per if c is None else c
        return (self.sem, n * self.per if c == self.per else n * self.per - (self.per - c))


def first(n):
    return isinstance(n, int) and n == 1


ORDER = dict(
    pe="b_cT b_v a_xT a_qkv0 a_qkv1 a_qkv2 b_x2T a_qkv3 b_router b_gu0 a_z0 b_gu1 b_gu2 b_gu3 b_aT0 a_z1 "
       "b_aT1 b_dn0 a_ba b_dn1 b_k a_ss b_y1T a_vT0 b_q a_vT1 b_s0 b_s1 b_s2 b_s3 a_dec0 a_dec1 a_kk b_pT0 "
       "a_qk b_pT1 b_pT2 b_pT3 b_pv a_la0 a_sT0 a_lb0 b_xo a_la1 a_sT1 a_lb1 b_y2T a_la2 b_h a_lb2 b_c0 a_la3 "
       "a_lb3 b_lg b_c1 a_r0 a_r1 a_n0 a_n1 a_step00 a_step01 a_step10 a_step11 a_step20 b_wT a_step21 a_o0 "
       "a_o1 b_spread b_pj0 b_pj1 a_cT0 a_cT1 a_w0 a_w1".split(),
    act="a_sum b_cT b_sum a_xT a_qkv0 a_qkv1 b_x2T a_qkv2 b_rl a_qkv3 a_z0 b_sg0 b_rt b_sg1 b_aT0 b_aT1 a_z1 "
       "a_ba a_mix0 a_mix1 a_sq a_mix2 a_mix3 a_ln b_y1T b_q b_exp0 b_exp1 a_dec0 a_dec1 b_exp2 b_exp3 b_pT0 "
       "b_pT1 a_diag a_sT0 b_y2T b_h a_sT1 b_c0 a_zf b_lt b_c1 a_r0 a_r1 b_te b_wT a_o0 a_o1 a_cT0 a_cT1".split(),
    dve="a_xn b_v b_x2 a_conv0 b_top a_conv1 a_conv2 b_act0 b_act1 a_conv3 b_sum1 b_k b_y1 a_ss b_max0 a_u0 "
       "b_max1 b_max2 b_max3 a_u1 a_lower b_pT0 b_pT1 a_score a_init a_la0 b_ao a_lb0 a_la1 b_sum2 b_y2 a_lb1 "
       "a_la2 a_lb2 a_la3 a_lb3 b_lb b_route a_n0 a_n1 a_step00 a_step01 a_step10 a_step11 a_step20 a_step21 "
       "b_weight b_gc0 b_gc1 a_core0 a_core1 b_sum3 b_y3 a_h b_y4".split(),
    pool="a_x b_mask b_rs b_rt b_ln0 a_ga a_sc a_g b_y1b b_ln1 b_rx b_y2b b_sig a_osc b_ln2 b_ln3 a_xh".split(),
)


def build(nc, x_d, ctx_d, mask_d, const_d, spread_d, wqkvz_d, wba_d, convw_d, ln12_d, dt_d, alog_d, gnw_d, wout_d,
          wr_d, wg_d, wu_d, wd_d, wq_d, wk_d, wv_d, wo_d, bq_d, bk_d, bv_d, bo_d, ce_d, w1_d, b1_d, w2_d, b2_d,
          wc_d, bc_d, wp_d, bp_d, lng_d, lnb_d, out_d):
    B = x_d.shape[0]
    with ExitStack() as ctx:
        def sb(name, shape, dt=F32):
            return ctx.enter_context(nc.sbuf_tensor(name, shape, dt))

        def sig(name, per=1):
            return Signal(ctx, nc, name, per)

        const = sb("const", [P, CONST_COLS])
        wqkvz = sb("wqkvz", [P, KC, CONV_DIM + HV * P])
        wba = sb("wba", [P, KC, 2 * HV])
        convw = sb("convw", [P, CONV_BLOCKS, TAPS])
        ln12 = sb("ln12", [P, 2, KC])
        dtb = sb("dtb", [P, HV])
        negA = sb("negA", [P, HV])
        gnw = sb("gnw", [P, 1])
        wout = sb("wout", [P, HV, D])
        wr = sb("wr", [P, KC, NEXP])
        wg = sb("wg", [P, KC, NEXP * P])
        wu = sb("wu", [P, KC, NEXP * P])
        wd = sb("wd", [P, NEXP, D])
        wq = sb("wq", [P, KC, 4 * P])
        wk = sb("wk", [P, KC, 4 * P])
        wv = sb("wv", [P, KC, D])
        wo = sb("wo", [P, 4, D])
        bq = sb("bq", [P, 4])
        bk = sb("bk", [P, 4])
        rows = sb("rows", [P, 5, D])
        BV, BO, BP, LG, LB = range(5)
        ce_stat = sb("ce_stat", [NCOL, 4])
        cenT = sb("cenT", [P, KC, NCOL])
        w1 = sb("w1", [P, KC, P])
        b1 = sb("b1", [P, 1])
        w2 = sb("w2", [P, NCOL])
        b2 = sb("b2", [P, NCOL])
        wc = sb("wc", [P, KC, NCOL * 64])
        bc = sb("bc", [P, 8])
        wp = sb("wp", [P, 8, D])
        ident_bf = sb("ident_bf", [P, P], BF16)
        above_bf = sb("above_bf", [P, 4 * P], BF16)
        spread_bf = sb("spread_bf", [NCOL, 8 * P], BF16)
        ones = sb("ones", [P, 32])
        nhalf = sb("nhalf", [P, NCOL])

        def con(name, rows_=P):
            a, b = CONST[name]
            return const[0:rows_, a:b]

        ident = con("ident")

        xin = sb("xin", [P, D])
        xres = sb("xres", [P, D])
        junk_a = sb("junk_a", [P, D])
        st_a = sb("st_a", [P, 4])
        xn = sb("xn", [P, D])
        xnT = sb("xnT", [P, KC, P])
        ypad = sb("ypad", [P, CONV_BLOCKS, TAPS - 1 + P])
        acc = sb("acc", [P, CONV_BLOCKS, P])
        mixed = sb("mixed", [P, CONV_BLOCKS, P])
        zs = sb("zs", [P, HV, P])
        ba = sb("ba", [P, 2 * HV])
        gate = sb("gate", [P, 10, HV])
        TB, BETA, ADT, NABS, EABS, LNP, SPM, SP, G, MINA = range(10)
        sse = sb("sse", [P, QK_BLOCKS])
        rqk = sb("rqk", [P, QK_BLOCKS])
        krb = sb("krb", [P, HV])
        ckk = sb("ckk", [P, HV])
        u = sb("u", [P, HV, P])
        gseg = sb("gseg", [P, HV, P])
        decay = sb("decay", [P, HV, P])
        lower = sb("lower", [P, HV, P])
        scoreqk = sb("scoreqk", [P, HV, P])
        scoreT = sb("scoreT", [P, HV, P])
        sqk = scoreT
        diag = sb("diag", [P, HV, BLK])
        zblk = sb("zblk", [P, HV, BLK])
        xblk = sb("xblk", [P, HV, BLK])
        ablk = sb("ablk", [P, HV, BLK])
        diagT, zinit = xblk, ablk
        zfull = sb("zfull", [P, HV, P])
        nT = gseg
        rsol = acc[:, 0:HV, :]
        tsol = [acc[:, HV:2 * HV, :], scoreqk]
        junk_o = nT
        ostat = sb("ostat", [P, 7, HV])
        OSS, RQS, RQ2, OM, OV, OP, OSC = range(7)
        core, coreT = decay, lower
        hmid = sb("hmid", [P, D])
        xh = sb("xh", [P, D])

        cin = sb("cin", [P, D])
        m_u8 = sb("m_u8", [P, P], U8)
        madj = sb("madj", [P, 4, P])
        cT = sb("cT", [P, KC, P])
        vpad = sb("vpad", [P, NH, 32])
        junk_b = sb("junk_b", [P, D])
        st_b = sb("st_b", [P, 4])
        x2 = sb("x2", [P, D])
        x2T = sb("x2T", [P, KC, P])
        rl = sb("rl", [P, NEXP])
        top8 = sb("top8", [P, 8])
        idx8 = sb("idx8", [P, 8], U32)
        idxf = sb("idxf", [P, 2])
        rmix = sb("rmix", [P, 4])
        r12 = sb("r12", [P, 2, NEXP])
        route = sb("route", [P, NEXP])
        y1p = sb("y1p", [P, D])
        y1 = sb("y1", [P, D])
        y1b = sb("y1b", [P, D])
        bn = sb("bn", [P, 4, 6])
        mv = sb("mv", [P, 4, 2])
        lnv = sb("lnv", [P, 4, 2])
        y1T = x2T
        qT = sb("qT", [P, 4, P])
        smax = sb("smax", [P, NH])
        nmax = sb("nmax", [P, NH])
        prob = sb("prob", [P, 4, 4, P])
        probT = sb("probT", [P, 4, 4, P])
        flat = prob[:, :, :, :].rearrange("p a b f -> p (a b) f")
        sg, act_ = flat[:, 0:NEXP, :], flat[:, NEXP:2 * NEXP, :]
        actT = probT[:, 0:2, :, :].rearrange("p a b f -> p (a b) f")
        keys = probT
        rsum, aoT = prob[:, 0, :, :], prob[:, 1, :, :]
        spread_in = flat[0:NCOL, 0:8, :].rearrange("p a f -> p (a f)")
        y2p = y1p
        y2 = sb("y2", [P, D])
        y2pb = y1b
        y2lb = sb("y2lb", [P, D])
        rx = sb("rx", [P, 3])
        y2T = x2T
        hT = sb("hT", [P, P])
        gc, gcw = sg, act_
        lg = sb("lg", [P, 8, NCOL])
        LBIAS, LTANH, LSIG, LOGIT, LTE, LNUM, LDEN, LEXP = range(8)
        lrec = sb("lrec", [P, NCOL])
        lmax = sb("lmax", [P, 8])
        lidx = sb("lidx", [P, 8], U32)
        lsm = sb("lsm", [P, 4])
        onehot = sb("onehot", [P, NCOL])
        wT = sb("wT", [NCOL, P], BF16)
        y3p = y1p
        y3 = sb("y3", [P, D])
        y3g = x2
        y4 = sb("y4", [P, D])
        yout = sb("yout", [P, D])
        ce, ce_junk, cen = yout[0:NCOL, :], junk_b[0:NCOL, :], y4[0:NCOL, :]

        A = [ctx.enter_context(nc.psum_tensor(f"bank_a{i}", [P, 512], F32)) for i in range(4)]
        Bk = [ctx.enter_context(nc.psum_tensor(f"bank_b{i}", [P, 512], F32)) for i in range(4)]

        def quad(bank):
            return bank[:, :].rearrange("p (a b) -> p a b", b=P)

        w_a, w_b = sig("weights_a"), sig("weights_b")
        prep = sig("prep")
        filled = sig("filled")
        ce_sumsq, alog_exp, ce_rnorm, cen_ok = sig("ce_sumsq"), sig("alog_exp"), sig("ce_rnorm", 2), sig("cen_ok")
        ce_ps = sig("ce_ps")
        x_loaded, c_loaded, m_loaded = sig("x_loaded", 16), sig("c_loaded", 16), sig("m_loaded", 16)
        stored = sig("stored", 16)
        pe_passed, dve_passed, pool_passed = sig("pe_passed"), sig("dve_passed"), sig("pool_passed")
        x_sumsq, x_rstd, x_res, x_norm = sig("x_sumsq"), sig("x_rstd", 2), sig("x_res"), sig("x_norm")
        xnT_ps, xnT_ok = sig("xnT_ps"), sig("xnT_ok")
        qkv_ps, y_ok, tap_last, conv = sig("qkv_ps", 4), sig("y_ok", 4), sig("tap_last", 16), sig("conv", 48)
        mixed_ok = sig("mixed_ok", 4)
        z_ps, ba_ps, zs_ok, ba_ok = sig("z_ps", 2), sig("ba_ps"), sig("zs_ok", 2), sig("ba_ok")
        tb_ok, eln, gates = sig("tb_ok"), sig("exp_ln", 2), sig("gates", 7)
        sq_ok, ss_ps, sse_ok, rqk_ok, kscale = sig("sq_ok"), sig("ss_ps"), sig("sse_ok"), sig("rqk_ok"), sig("kscale", 2)
        vT_ps, u_ok = sig("vT_ps", 2), sig("u_ok", 2)
        gseg_ok, decay_ps, decay_ok = sig("gseg_ok", 2), sig("decay_ps", 2), sig("decay_ok", 2)
        kk_ps, qk_ps, lower_ok, score_ok = sig("kk_ps"), sig("qk_ps"), sig("lower_ok"), sig("score_ok")
        diag_ok, init_ok = sig("diag_ok"), sig("init_ok", 2)
        z_ok, x_ok = sig("z_ok", 5), sig("x_ok", 4)
        la_ps, a_ok, lb_ps = sig("la_ps", 4), sig("a_ok", 4), sig("lb_ps", 4)
        scoreT_ps, scoreT_ok = sig("scoreT_ps", 2), sig("scoreT_ok", 2)
        zfull_ok, r_ps, r_ok, n_ps, n_ok = sig("zfull_ok"), sig("r_ps", 2), sig("r_ok", 2), sig("n_ps", 2), sig("n_ok", 2)
        step_ps, step_ok = sig("step_ps", 6), sig("step_ok", 6)
        o_ps, o_sumsq, o_scale, core_ok = sig("o_ps", 2), sig("o_sumsq", 2), sig("o_scale", 6), sig("core_ok", 2)
        coreT_ps, coreT_ok, out_ps, h_ok, xh_ok = sig("coreT_ps", 2), sig("coreT_ok", 2), sig("out_ps"), sig("h_ok"), sig("xh_ok")

        cT_ps, cT_ok, madj_ok, k_ps, v_ps, k_ok, v_ok = (sig("cT_ps"), sig("cT_ok"), sig("madj_ok"), sig("k_ps"),
                                                         sig("v_ps"), sig("k_ok"), sig("v_ok"))
        h_sumsq, h_rstd, x2_ok, x2T_ps, x2T_ok = sig("h_sumsq"), sig("h_rstd", 2), sig("x2_ok"), sig("x2T_ps"), sig("x2T_ok")
        rl_ps, rl_ok, gu_ps, sg_ok = sig("rl_ps"), sig("rl_ok"), sig("gu_ps", 4), sig("sg_ok", 2)
        top_ok, rtanh, routing = sig("top_ok", 3), sig("rtanh"), sig("routing", 6)
        act_ok, actT_ps, actT_ok, down_ps = sig("act_ok", 2), sig("actT_ps", 2), sig("actT_ok", 2), sig("down_ps")
        ysum, ln_bn, ln_rstd, yn = sig("ysum", 3), sig("ln_bn", 8), sig("ln_rstd", 8), sig("yn", 3)
        y1b_ok, y1T_ps, y1T_ok, q_ps, q_ok = sig("y1b_ok"), sig("y1T_ps"), sig("y1T_ok"), sig("q_ps"), sig("q_ok")
        s_ps, smax_ok, nmax_ok, prob_ok = sig("s_ps", 4), sig("smax_ok", 4), sig("nmax_ok", 4), sig("prob_ok", 4)
        probT_ps, pTa_ok, pTv_ok = sig("probT_ps", 4), sig("probT_act", 2), sig("probT_dve", 2)
        sum_ps, pv_ps, rsum_ok, ao_ok, xo_ps = sig("sum_ps"), sig("pv_ps"), sig("rsum_ok"), sig("ao_ok"), sig("xo_ps")
        y2b_ok, rx_ok, y2T_ps, y2T_ok = sig("y2b_ok", 2), sig("rx_ok", 3), sig("y2T_ps"), sig("y2T_ok")
        hg_ps, hT_ok, c_ps, gc_ok, lg_ps = sig("hg_ps"), sig("hT_ok"), sig("c_ps", 2), sig("gc_ok", 2), sig("lg_ps")
        lb_ok, ltanh, lsig, lchain = sig("lb_ok"), sig("ltanh", 2), sig("lsig"), sig("lchain", 11)
        wT_ps, wT_ok, wb_ps, gcw_ok, pj_ps = sig("wT_ps"), sig("wT_ok"), sig("wb_ps", 2), sig("gcw_ok", 2), sig("pj_ps")
        y3_ok, y_out = sig("y3_ok", 2), sig("y_out")

        loads_a = [(const, const_d), (wqkvz, wqkvz_d), (wba, wba_d), (convw, convw_d), (wout, wout_d),
                   (ln12, ln12_d), (gnw, gnw_d)]
        loads_b = [(wr, wr_d), (wg, wg_d), (wu, wu_d), (wd, wd_d), (wq, wq_d), (wk, wk_d), (wv, wv_d), (wo, wo_d),
                   (bq, bq_d), (bk, bk_d), (w1, w1_d), (w2, w2_d), (wc, wc_d), (bc, bc_d), (wp, wp_d), (ce, ce_d), (b1, b1_d), (spread_in, spread_d)]

        small_a = [(dtb[:, :], dt_d.partition_broadcast(P)), (negA[:, :], alog_d.partition_broadcast(P))]
        small_b = [(rows[:, BV, :], bv_d.partition_broadcast(P)), (rows[:, BO, :], bo_d.partition_broadcast(P)),
                   (rows[:, BP, :], bp_d.partition_broadcast(P)), (rows[:, LG, :], lng_d.partition_broadcast(P)),
                   (rows[:, LB, :], lnb_d.partition_broadcast(P)), (b2[:, :], b2_d.partition_broadcast(P))]
        W_A = 16 * (len(loads_a) + len(small_a))
        W_B = 16 * (len(loads_b) + len(small_b))
        FILLS = 5
        PREP_A, PREP_B = 9, 14

        def heads(t, half):
            return t[:, 4 * half:4 * half + 4, :]

        def cols(ap, n):
            return ap.unsqueeze(2).to_broadcast([ap.shape[0], ap.shape[1], n])

        block = ctx.enter_context(nc.Block())

        def run(steps, order, engine):
            assert sorted(steps) == sorted(order)

            def go(n_a, n_b):
                for name in order:
                    n = n_a if name[0] == "a" else n_b
                    if n is not None:
                        steps[name](n)
            go(1, None)
            go(2, 1)
            with engine.Fori(3, B + 1) as i:
                go(i, i - 1)
            go(None, B)

        @block.sync
        def _(sp):
            def load_x(n):
                if not first(n):
                    sp.wait_ge(*x_norm(n - 1))
                    sp.wait_ge(*x_res(n - 1))
                sp.dma_start(xin[:, :], x_d[n - 1, :, :]).then_inc(x_loaded.sem, 16)

            def load_ctx(n):
                if not first(n):
                    sp.wait_ge(*cT_ps(n - 1))
                    sp.wait_ge(*madj_ok(n - 1))
                sp.dma_start(cin[:, :], ctx_d[n - 1, :, :]).then_inc(c_loaded.sem, 16)
                sp.dma_start(m_u8[:, :], mask_d[n - 1, :, :].broadcast_to([P, P])).then_inc(m_loaded.sem, 16)

            def store(n):
                sp.wait_ge(*y_out(n))
                sp.dma_start(out_d[n - 1, :, :], yout[:, :]).then_inc(stored.sem, 16)

            load_x(1)
            for dst, src in loads_a:
                sp.dma_start(dst[:], src).then_inc(w_a.sem, 16)
            for dst, src in small_a:
                sp.dma_start(dst, src).then_inc(w_a.sem, 16)
            for dst, src in loads_b:
                sp.dma_start(dst if dst is spread_in else dst[:], src).then_inc(w_b.sem, 16)
            for dst, src in small_b:
                sp.dma_start(dst, src).then_inc(w_b.sem, 16)
            load_ctx(1)
            load_x(2)
            load_x(3)
            load_ctx(2)
            store(1)
            with sp.Fori(4, B + 1) as i:
                load_x(i)
                load_ctx(i - 1)
                store(i - 2)
            load_ctx(B)
            store(B - 1)
            store(B)
            sp.wait_ge(*stored(B))

        @block.tensor
        def _(pe):
            mm, tr = nc.tensor.matmul, nc.tensor.transpose

            def a_xT(n):
                pe.wait_ge(*x_norm(n))
                for c in range(KC):
                    last = tr(A[0][:, c * P:(c + 1) * P], xn[:, c * P:(c + 1) * P], ident)
                last.then_inc(xnT_ps.sem, 1)

            def qkv(n, g):
                bank = (1, 2, 3, 0)[g]
                if g == 0:
                    pe.wait_ge(*xnT_ok(n))
                for b in range(4):
                    o = (4 * g + b) * P
                    for c in range(KC):
                        last = mm(A[bank][:, b * P:(b + 1) * P], wqkvz[:, c, o:o + P], xnT[:, c, :],
                                  start=(c == 0), stop=(c == KC - 1))
                last.then_inc(qkv_ps.sem, 1)

            def zgate(n, half):
                pe.wait_ge(*tap_last(n, 4 * half + 4))
                for c in range(KC):
                    o = CONV_DIM + 512 * half
                    last = mm(A[1 + half][:, :], xnT[:, c, :], wqkvz[:, c, o:o + 512],
                              start=(c == 0), stop=(c == KC - 1))
                last.then_inc(z_ps.sem, 1)

            def a_ba(n):
                pe.wait_ge(*tap_last(n, 12))
                for c in range(KC):
                    last = mm(A[3][:, 0:2 * HV], xnT[:, c, :], wba[:, c, :], start=(c == 0), stop=(c == KC - 1))
                last.then_inc(ba_ps.sem, 1)

            def a_ss(n):
                pe.wait_ge(*ba_ok(n))
                pe.wait_ge(*sq_ok(n))
                for b in range(QK_BLOCKS):
                    last = mm(A[3][:, 16 + b:17 + b], sqk[:, b, :], ones[:, 0:1], start=True, stop=True)
                last.then_inc(ss_ps.sem, 1)

            def values(n, half):
                pe.wait_ge(*mixed_ok(n, 3 + half))
                pe.wait_ge(*zs_ok(n, 1 + half))
                for b in range(4):
                    last = tr(A[1 + half][:, b * P:(b + 1) * P], mixed[:, QK_BLOCKS + 4 * half + b, :], ident)
                last.then_inc(vT_ps.sem, 1)

            def exponents(n, half):
                if half == 0:
                    pe.wait_ge(*tap_last(n, 16))
                else:
                    pe.wait_ge(*sse_ok(n))
                bank = (0, 3)[half]
                pe.wait_ge(*gseg_ok(n, 1 + half))
                mm(A[bank][:, :], ident_bf[:, :], above_bf[:, :], start=True, stop=False)
                mm(A[bank][:, :], con("upto"), heads(gseg, half), start=False, stop=True).then_inc(decay_ps.sem, 1)

            def a_kk(n):
                pe.wait_ge(*u_ok(n, 1))
                for h in range(HK):
                    k = mixed[:, HK + h, :]
                    last = mm(A[1][:, h * P:(h + 1) * P], k, k, start=True, stop=True)
                last.then_inc(kk_ps.sem, 1)

            def a_qk(n):
                pe.wait_ge(*u_ok(n, 2))
                for h in range(HK):
                    last = mm(A[2][:, h * P:(h + 1) * P], mixed[:, h, :], mixed[:, HK + h, :], start=True, stop=True)
                last.then_inc(qk_ps.sem, 1)

            def blocks(out, lhsT, rhs):
                for h in range(HV):
                    for b in range(NBLK):
                        r = slice(BLK * b, BLK * (b + 1))
                        last = mm(out[r, BLK * h:BLK * (h + 1)], lhsT[r, h, :], rhs[r, h, :], start=True, stop=True)
                return last

            def level_a(n, k):
                if k == 0:
                    pe.wait_ge(*decay_ok(n, 2))
                pe.wait_ge(*z_ok(n, k + 1)).then_inc(pe_passed.sem, 1)
                blocks(A[0], diag, zblk).then_inc(la_ps.sem, 1)

            def level_b(n, k):
                pe.wait_ge(*a_ok(n, k + 1))
                pe.wait_ge(*x_ok(n, k + 1)).then_inc(pe_passed.sem, 1)
                blocks(A[3], xblk, ablk).then_inc(lb_ps.sem, 1)

            def scores_T(n, half):
                if half == 0:
                    pe.wait_ge(*score_ok(n))
                    pe.wait_ge(*lower_ok(n))
                for b in range(4):
                    last = tr(A[1 + half][:, b * P:(b + 1) * P], scoreqk[:, 4 * half + b, :], ident)
                last.then_inc(scoreT_ps.sem, 1)

            def solve_r(n, half):
                pe.wait_ge(*zfull_ok(n))
                pe.wait_ge(*scoreT_ok(n, 1 + half))
                for b in range(4):
                    h = 4 * half + b
                    last = mm(A[1 + half][:, b * P:(b + 1) * P], zfull[:, h, :], u[:, h, :], start=True, stop=True)
                last.then_inc(r_ps.sem, 1)

            def solve_n(n, half):
                bank = (0, 3)[half]
                pe.wait_ge(*zfull_ok(n))
                for b in range(4):
                    h = 4 * half + b
                    last = mm(A[bank][:, b * P:(b + 1) * P], lower[:, h, :], zfull[:, h, :], start=True, stop=True)
                last.then_inc(n_ps.sem, 1)

            def horner(n, k, half):
                bank = (0, 3)[half]
                if k == 0:
                    pe.wait_ge(*n_ok(n, 1 + half))
                    pe.wait_ge(*r_ok(n, 1 + half))
                else:
                    pe.wait_ge(*step_ok(n, 2 * k - 1 + half))
                src = rsol if k == 0 else tsol[(k - 1) % 2]
                for b in range(4):
                    h = 4 * half + b
                    last = mm(A[bank][:, b * P:(b + 1) * P], nT[:, h, :], src[:, h, :], start=True, stop=True)
                last.then_inc(step_ps.sem, 1)

            def read(n, half):
                pe.wait_ge(*step_ok(n, 5 + half))
                for b in range(4):
                    h = 4 * half + b
                    last = mm(A[1 + half][:, b * P:(b + 1) * P], scoreT[:, h, :], tsol[0][:, h, :],
                              start=True, stop=True)
                last.then_inc(o_ps.sem, 1)

            def core_T(n, half):
                bank = (0, 3)[half]
                pe.wait_ge(*core_ok(n, 1 + half))
                for b in range(4):
                    last = tr(A[bank][:, b * P:(b + 1) * P], core[:, 4 * half + b, :], ident)
                last.then_inc(coreT_ps.sem, 1)

            def project(n, half):
                pe.wait_ge(*coreT_ok(n, 1 + half))
                for h in range(4 * half, 4 * half + 4):
                    last = mm(A[1][:, 0:D], coreT[:, h, :], wout[:, h, :], start=(h == 0), stop=(h == HV - 1))
                if half == 1:
                    last.then_inc(out_ps.sem, 1)

            def b_cT(n):
                pe.wait_ge(*c_loaded(n))
                if not first(n):
                    pe.wait_ge(*gcw_ok(n - 1))
                for c in range(KC):
                    last = tr(Bk[0][:, c * P:(c + 1) * P], cin[:, c * P:(c + 1) * P], ident)
                last.then_inc(cT_ps.sem, 1)

            def b_v(n):
                pe.wait_ge(*cT_ok(n))
                if not first(n):
                    pe.wait_ge(*ysum(n - 1))
                for c in range(KC):
                    last = mm(Bk[2][:, 0:D], cT[:, c, :], wv[:, c, :], start=(c == 0), stop=(c == KC - 1))
                last.then_inc(v_ps.sem, 1)

            def b_x2T(n):
                pe.wait_ge(*x2_ok(n))
                for c in range(KC):
                    last = tr(Bk[3][:, c * P:(c + 1) * P], x2[:, c * P:(c + 1) * P], ident)
                last.then_inc(x2T_ps.sem, 1)

            def b_router(n):
                pe.wait_ge(*x2T_ok(n))
                for c in range(KC):
                    last = mm(Bk[0][:, 0:NEXP], x2T[:, c, :], wr[:, c, :], start=(c == 0), stop=(c == KC - 1))
                last.then_inc(rl_ps.sem, 1)

            def gate_up(n, i):
                w, half, bank = ((wg, 0, 1), (wu, 0, 2), (wg, 1, 3), (wu, 1, 0))[i]
                if i == 1:
                    pe.wait_ge(*v_ok(n))
                if i == 3:
                    pe.wait_ge(*rl_ok(n))
                for c in range(KC):
                    last = mm(Bk[bank][:, :], x2T[:, c, :], w[:, c, 512 * half:512 * half + 512],
                              start=(c == 0), stop=(c == KC - 1))
                last.then_inc(gu_ps.sem, 1)

            def act_T(n, half):
                bank = (1, 3)[half]
                pe.wait_ge(*act_ok(n, 1 + half))
                for b in range(4):
                    last = tr(Bk[bank][:, b * P:(b + 1) * P], act_[:, 4 * half + b, :], ident)
                last.then_inc(actT_ps.sem, 1)

            def down(n, half):
                pe.wait_ge(*actT_ok(n, 1 + half))
                for e in range(4 * half, 4 * half + 4):
                    last = mm(Bk[2][:, 0:D], actT[:, e, :], wd[:, e, :], start=(e == 0), stop=(e == NEXP - 1))
                if half == 1:
                    last.then_inc(down_ps.sem, 1)

            def b_k(n):
                for b in range(4):
                    for c in range(KC):
                        last = mm(Bk[3][:, b * P:(b + 1) * P], wk[:, c, b * P:(b + 1) * P], cT[:, c, :],
                                  start=(c == 0), stop=(c == KC - 1))
                last.then_inc(k_ps.sem, 1)

            def b_y1T(n):
                pe.wait_ge(*yn(n, 1))
                for c in range(KC):
                    last = tr(Bk[0][:, c * P:(c + 1) * P], y1[:, c * P:(c + 1) * P], ident)
                last.then_inc(y1T_ps.sem, 1)

            def b_q(n):
                pe.wait_ge(*y1T_ok(n))
                for b in range(4):
                    for c in range(KC):
                        last = mm(Bk[1][:, b * P:(b + 1) * P], wq[:, c, b * P:(b + 1) * P], y1T[:, c, :],
                                  start=(c == 0), stop=(c == KC - 1))
                last.then_inc(q_ps.sem, 1)

            def scores(n, b):
                if b == 0:
                    pe.wait_ge(*q_ok(n))
                    pe.wait_ge(*k_ok(n))
                mm(Bk[b][:, :], qT[:, b, :], keys[:, b, :, :], start=True, stop=True).then_inc(s_ps.sem, 1)

            def prob_T(n, b):
                pe.wait_ge(*prob_ok(n, b + 1))
                for j in range(4):
                    last = tr(Bk[b][:, j * P:(j + 1) * P], prob[:, b, j, :], ident)
                last.then_inc(probT_ps.sem, 1)

            def b_pv(n):
                pe.wait_ge(*pTa_ok(n, 2))
                pe.wait_ge(*pTv_ok(n, 2)).then_inc(pe_passed.sem, 1)
                for j in range(4):
                    for b in range(4):
                        last = mm(Bk[1][32 * j:32 * j + 32, b * P:(b + 1) * P], ones[:, :], probT[:, b, j, :],
                                  start=True, stop=True)
                last.then_inc(sum_ps.sem, 1)
                for j in range(4):
                    for b in range(4):
                        last = mm(Bk[0][32 * j:32 * j + 32, b * P:(b + 1) * P], vpad[:, 4 * b + j, :],
                                  probT[:, b, j, :], start=True, stop=True)
                last.then_inc(pv_ps.sem, 1)

            def b_xo(n):
                pe.wait_ge(*ao_ok(n))
                for b in range(4):
                    last = mm(Bk[2][:, 0:D], aoT[:, b, :], wo[:, b, :], start=(b == 0), stop=(b == 3))
                last.then_inc(xo_ps.sem, 1)

            def b_y2T(n):
                pe.wait_ge(*yn(n, 2))
                for c in range(KC):
                    last = tr(Bk[3][:, c * P:(c + 1) * P], y2[:, c * P:(c + 1) * P], ident)
                last.then_inc(y2T_ps.sem, 1)

            def b_h(n):
                pe.wait_ge(*y2T_ok(n))
                for c in range(KC):
                    last = mm(Bk[0][:, 0:P], w1[:, c, :], y2T[:, c, :], start=(c == 0), stop=(c == KC - 1))
                last.then_inc(hg_ps.sem, 1)
                for c in range(KC):
                    mm(Bk[1][:, 0:NCOL], y2T[:, c, :], cenT[:, c, :], start=(c == 0), stop=(c == KC - 1))

            def columns(n, half):
                for b in range(4):
                    o = (4 * half + b) * P
                    for c in range(KC):
                        last = mm(Bk[2 + half][:, b * P:(b + 1) * P], wc[:, c, o:o + P], y2T[:, c, :],
                                  start=(c == 0), stop=(c == KC - 1))
                last.then_inc(c_ps.sem, 1)

            def b_lg(n):
                pe.wait_ge(*hT_ok(n))
                mm(Bk[1][:, 32:32 + NCOL], hT[:, :], w2[:, :], start=True, stop=True).then_inc(lg_ps.sem, 1)

            def b_wT(n):
                pe.wait_ge(*lchain(n, 5))
                tr(Bk[0][0:NCOL, 0:P], onehot[:, :], ident).then_inc(wT_ps.sem, 1)

            def b_spread(n):
                pe.wait_ge(*wT_ok(n))
                for half in range(2):
                    for b in range(4):
                        o = (4 * half + b) * P
                        last = mm(Bk[half][:, b * P:(b + 1) * P], spread_bf[:, o:o + P], wT[:, :], start=True, stop=True)
                    last.then_inc(wb_ps.sem, 1)

            def mix(n, half):
                pe.wait_ge(*gcw_ok(n, 1 + half))
                for b in range(4 * half, 4 * half + 4):
                    last = mm(Bk[2][:, 0:D], gcw[:, b, :], wp[:, b, :], start=(b == 0), stop=(b == 7))
                if half == 1:
                    last.then_inc(pj_ps.sem, 1)

            pe.wait_ge(w_a.sem, W_A)
            pe.wait_ge(filled.sem, FILLS)
            pe.wait_ge(prep.sem, PREP_A)
            pe.wait_ge(cen_ok.sem, 1)
            for c in range(KC):
                last = tr(Bk[1][:, c * P:c * P + NCOL], cen[:, c * P:(c + 1) * P], const[0:NCOL, 0:NCOL])
            last.then_inc(ce_ps.sem, 1)
            pe.wait_ge(w_b.sem, W_B)
            pe.wait_ge(prep.sem, PREP_B)
            steps = dict(a_xT=a_xT, a_ba=a_ba, a_ss=a_ss, a_kk=a_kk, a_qk=a_qk, b_cT=b_cT, b_v=b_v, b_x2T=b_x2T,
                         b_router=b_router, b_k=b_k, b_y1T=b_y1T, b_q=b_q, b_pv=b_pv, b_xo=b_xo, b_y2T=b_y2T, b_h=b_h,
                         b_lg=b_lg, b_wT=b_wT, b_spread=b_spread)
            for name, f in (("a_z", zgate), ("a_vT", values), ("a_dec", exponents), ("a_sT", scores_T),
                            ("a_r", solve_r), ("a_n", solve_n), ("a_o", read), ("a_cT", core_T), ("a_w", project),
                            ("b_aT", act_T), ("b_dn", down), ("b_c", columns), ("b_pj", mix)):
                for half in range(2):
                    steps[f"{name}{half}"] = lambda n, f=f, half=half: f(n, half)
            for name, f in (("a_qkv", qkv), ("a_la", level_a), ("a_lb", level_b), ("b_gu", gate_up), ("b_s", scores),
                            ("b_pT", prob_T)):
                for i in range(4):
                    steps[f"{name}{i}"] = lambda n, f=f, i=i: f(n, i)
            for k in range(3):
                for half in range(2):
                    steps[f"a_step{k}{half}"] = lambda n, k=k, half=half: horner(n, k, half)
            run(steps, ORDER["pe"], pe)

        @block.scalar
        def _(act):
            fn = nc.scalar.activation

            def a_sum(n):
                act.wait_ge(*x_loaded(n))
                fn(junk_a[:, :], xin[:, :], ACT.Square, accum_out=st_a[:, 0:1]).then_inc(x_sumsq.sem, 1)

            def a_xT(n):
                act.wait_ge(*xnT_ps(n))
                fn(xnT[:, :, :], A[0][:, 0:D], ACT.Copy).then_inc(xnT_ok.sem, 1)

            def qkv(n, g):
                bank = (1, 2, 3, 0)[g]
                act.wait_ge(*qkv_ps(n, g + 1))
                fn(ypad[:, 4 * g:4 * g + 4, TAPS - 1:], quad(A[bank]), ACT.Copy).then_inc(y_ok.sem, 1)
                for b in range(4):
                    c = 4 * g + b
                    fn(acc[:, c, :], A[bank][:, b * P:(b + 1) * P], ACT.Copy, scale=convw[:, c, TAPS - 1:TAPS])\
                        .then_inc(tap_last.sem, 1)

            def zgate(n, half):
                act.wait_ge(*z_ps(n, 1 + half))
                fn(heads(zs, half), quad(A[1 + half]), ACT.Silu).then_inc(zs_ok.sem, 1)

            def a_ba(n):
                act.wait_ge(*ba_ps(n))
                fn(ba[:, :], A[3][:, 0:2 * HV], ACT.Copy).then_inc(ba_ok.sem, 1)
                act.wait_ge(*ba_ok(n))
                fn(gate[:, TB, :], ba[:, 0:HV], ACT.Tanh, scale=0.5).then_inc(tb_ok.sem, 1)

            def silu(n, g):
                act.wait_ge(*conv(n, 12 * g + 12))
                fn(mixed[:, 4 * g:4 * g + 4, :], acc[:, 4 * g:4 * g + 4, :], ACT.Silu).then_inc(mixed_ok.sem, 1)

            def a_sq(n):
                act.wait_ge(*mixed_ok(n, 2))
                fn(sqk[:, :, :], mixed[:, 0:QK_BLOCKS, :], ACT.Square).then_inc(sq_ok.sem, 1)

            def a_ln(n):
                act.wait_ge(*gates(n, 4))
                fn(gate[:, EABS, :], gate[:, NABS, :], ACT.Exp).then_inc(eln.sem, 1)
                act.wait_ge(*eln(n, 1))
                fn(gate[:, LNP, :], gate[:, EABS, :], ACT.Ln, bias=ones[:, 0:1]).then_inc(eln.sem, 1)

            def exponents(n, half):
                act.wait_ge(*decay_ps(n, 1 + half))
                fn(heads(decay, half), quad(A[(0, 3)[half]]), ACT.Exp).then_inc(decay_ok.sem, 1)

            def a_diag(n):
                act.wait_ge(*lower_ok(n))
                for b in range(NBLK):
                    r = slice(BLK * b, BLK * (b + 1))
                    last = fn(diag[r, :, :], lower[r, :, r], ACT.Copy)
                last.then_inc(diag_ok.sem, 1)

            def scores_T(n, half):
                act.wait_ge(*scoreT_ps(n, half + 1))
                fn(heads(scoreT, half), quad(A[1 + half]), ACT.Copy).then_inc(scoreT_ok.sem, 1)

            def a_zf(n):
                act.wait_ge(*z_ok(n, 5))
                for b in range(NBLK):
                    r = slice(BLK * b, BLK * (b + 1))
                    last = fn(zfull[r, :, r], zblk[r, :, :], ACT.Copy)
                last.then_inc(zfull_ok.sem, 1)

            def solve_r(n, half):
                act.wait_ge(*r_ps(n, 1 + half))
                fn(heads(rsol, half), quad(A[1 + half]), ACT.Copy).then_inc(r_ok.sem, 1)

            def read(n, half):
                act.wait_ge(*o_ps(n, 1 + half))
                for h in range(4 * half, 4 * half + 4):
                    last = fn(junk_o[:, h, :], A[1 + half][:, (h % 4) * P:(h % 4 + 1) * P], ACT.Square,
                              accum_out=ostat[:, OSS, h:h + 1])
                last.then_inc(o_sumsq.sem, 1)

            def core_T(n, half):
                act.wait_ge(*coreT_ps(n, 1 + half))
                fn(heads(coreT, half), quad(A[(0, 3)[half]]), ACT.Copy).then_inc(coreT_ok.sem, 1)

            def b_cT(n):
                act.wait_ge(*cT_ps(n))
                fn(cT[:, :, :], Bk[0][:, 0:D], ACT.Copy).then_inc(cT_ok.sem, 1)

            def b_sum(n):
                act.wait_ge(*h_ok(n))
                fn(junk_b[:, :], hmid[:, :], ACT.Square, accum_out=st_b[:, 0:1]).then_inc(h_sumsq.sem, 1)

            def b_x2T(n):
                act.wait_ge(*x2T_ps(n))
                fn(x2T[:, :, :], Bk[3][:, 0:D], ACT.Copy).then_inc(x2T_ok.sem, 1)

            def b_rl(n):
                act.wait_ge(*rl_ps(n))
                fn(rl[:, :], Bk[0][:, 0:NEXP], ACT.Copy).then_inc(rl_ok.sem, 1)

            def expert_silu(n, half):
                act.wait_ge(*gu_ps(n, 1 + 2 * half))
                fn(heads(sg, half), quad(Bk[(1, 3)[half]]), ACT.Silu).then_inc(sg_ok.sem, 1)

            def b_rt(n):
                act.wait_ge(*routing(n, 1))
                fn(rmix[:, 1:2], rmix[:, 0:1], ACT.Tanh, scale=0.5).then_inc(rtanh.sem, 1)

            def act_T(n, half):
                act.wait_ge(*actT_ps(n, 1 + half))
                fn(heads(actT, half), quad(Bk[(1, 3)[half]]), ACT.Copy).then_inc(actT_ok.sem, 1)

            def b_y1T(n):
                act.wait_ge(*y1T_ps(n))
                fn(y1T[:, :, :], Bk[0][:, 0:D], ACT.Copy).then_inc(y1T_ok.sem, 1)

            def b_q(n):
                act.wait_ge(*q_ps(n))
                for b in range(4):
                    last = fn(qT[:, b, :], Bk[1][:, b * P:(b + 1) * P], ACT.Identity, bias=bq[:, b:b + 1])
                last.then_inc(q_ok.sem, 1)

            def exps(n, b):
                act.wait_ge(*nmax_ok(n, b + 1))
                for j in range(4):
                    last = fn(prob[:, b, j, :], Bk[b][:, j * P:(j + 1) * P], ACT.Exp, scale=HD ** -0.5,
                              bias=nmax[:, 4 * b + j:4 * b + j + 1])
                last.then_inc(prob_ok.sem, 1)

            def prob_T(n, i):
                act.wait_ge(*probT_ps(n, 2 * i + 1))
                fn(probT[:, 2 * i, :, :], quad(Bk[2 * i]), ACT.Copy).then_inc(pTa_ok.sem, 1)

            def b_y2T(n):
                act.wait_ge(*y2T_ps(n))
                fn(y2T[:, :, :], Bk[3][:, 0:D], ACT.Copy).then_inc(y2T_ok.sem, 1)

            def b_h(n):
                act.wait_ge(*hg_ps(n))
                fn(hT[:, :], Bk[0][:, 0:P], ACT.Gelu, bias=b1[:, 0:1]).then_inc(hT_ok.sem, 1)

            def columns(n, half):
                act.wait_ge(*c_ps(n, 1 + half))
                for b in range(4):
                    last = fn(gc[:, 4 * half + b, :], Bk[2 + half][:, b * P:(b + 1) * P], ACT.Gelu,
                              bias=bc[:, 4 * half + b:4 * half + b + 1])
                last.then_inc(gc_ok.sem, 1)

            def b_lt(n):
                act.wait_ge(*lb_ok(n))
                fn(lg[:, LTANH, :], lg[:, LBIAS, :], ACT.Tanh, scale=0.5).then_inc(ltanh.sem, 1)

            def b_te(n):
                act.wait_ge(*lchain(n, 6))
                fn(lg[:, LTE, :], lg[:, LOGIT, :], ACT.Tanh, scale=0.5, bias=lsm[:, 1:2]).then_inc(ltanh.sem, 1)

            def b_wT(n):
                act.wait_ge(*wT_ps(n))
                fn(wT[:, :], Bk[0][0:NCOL, 0:P], ACT.Copy).then_inc(wT_ok.sem, 1)

            act.wait_ge(w_b.sem, W_B)
            fn(ce_junk[:, :], ce[:, :], ACT.Square, accum_out=ce_stat[:, 0:1]).then_inc(ce_sumsq.sem, 1)
            act.wait_ge(w_a.sem, W_A)
            fn(negA[:, :], negA[:, :], ACT.Exp).then_inc(alog_exp.sem, 1)
            act.wait_ge(filled.sem, FILLS)
            steps = dict(a_sum=a_sum, a_xT=a_xT, a_ba=a_ba, a_sq=a_sq, a_ln=a_ln, a_diag=a_diag, a_zf=a_zf, b_cT=b_cT,
                         b_sum=b_sum, b_x2T=b_x2T, b_rl=b_rl, b_rt=b_rt, b_y1T=b_y1T, b_q=b_q, b_y2T=b_y2T, b_h=b_h,
                         b_lt=b_lt, b_te=b_te, b_wT=b_wT)
            for name, f in (("a_z", zgate), ("a_dec", exponents), ("a_sT", scores_T), ("a_r", solve_r), ("a_o", read),
                            ("a_cT", core_T), ("b_sg", expert_silu), ("b_aT", act_T), ("b_pT", prob_T),
                            ("b_c", columns)):
                for half in range(2):
                    steps[f"{name}{half}"] = lambda n, f=f, half=half: f(n, half)
            for name, f in (("a_qkv", qkv), ("a_mix", silu), ("b_exp", exps)):
                for i in range(4):
                    steps[f"{name}{i}"] = lambda n, f=f, i=i: f(n, i)
            run(steps, ORDER["act"], act)

        @block.vector
        def _(dve):
            tt, ts, stt = nc.vector.tensor_tensor, nc.vector.tensor_scalar, nc.vector.scalar_tensor_tensor

            def a_xn(n):
                dve.wait_ge(*x_rstd(n))
                dve.wait_ge(*x_loaded(n))
                ts(xn[:, :], xin[:, :], st_a[:, 2:3], None, ALU.mult).then_inc(x_norm.sem, 1)

            def taps(n, g):
                dve.wait_ge(*y_ok(n, g + 1))
                for k in range(TAPS - 1):
                    for b in range(4):
                        c = 4 * g + b
                        if k == 0:
                            dve.wait_ge(*tap_last(n, c + 1))
                        else:
                            dve.wait_ge(*conv(n, 12 * g + 4 * (k - 1) + b + 1))
                        stt(acc[:, c, :], ypad[:, c, k:k + P], convw[:, c, k:k + 1], acc[:, c, :],
                            ALU.mult, ALU.add).then_inc(conv.sem, 1)

            def a_ss(n):
                dve.wait_ge(*ss_ps(n))
                ts(sse[:, :], A[3][:, 16:16 + QK_BLOCKS], EPS_RMS, None, ALU.add).then_inc(sse_ok.sem, 1)

            def values(n, half):
                dve.wait_ge(*kscale(n, 1))
                dve.wait_ge(*vT_ps(n, 1 + half))
                tt(heads(u, half), quad(A[1 + half]), cols(krb[:, 4 * half:4 * half + 4], P), ALU.mult)\
                    .then_inc(u_ok.sem, 1)

            def a_lower(n):
                dve.wait_ge(*kk_ps(n))
                dve.wait_ge(*decay_ok(n))
                dve.wait_ge(*kscale(n, 2))
                for h in range(HV):
                    last = stt(lower[:, h, :], A[1][:, (h // 2) * P:(h // 2 + 1) * P], ckk[:, h:h + 1], decay[:, h, :],
                               ALU.mult, ALU.mult)
                last.then_inc(lower_ok.sem, 1)

            def a_score(n):
                dve.wait_ge(*qk_ps(n))
                tt(scoreqk[:, :, :].rearrange("p (a b) f -> p a b f", b=2),
                   quad(A[2]).unsqueeze(2).to_broadcast([P, 4, 2, P]),
                   decay[:, :, :].rearrange("p (a b) f -> p a b f", b=2), ALU.mult).then_inc(score_ok.sem, 1)

            def a_init(n):
                dve.wait_ge(*diag_ok(n))
                nc.vector.transpose(diagT[:, :, :], diag[:, :, :]).then_inc(init_ok.sem, 1)
                dve.wait_ge(*init_ok(n, 1))
                tt(zinit[:, :, :], diagT[:, :, :], con("level1").unsqueeze(1).to_broadcast([P, HV, BLK]), ALU.mult)\
                    .then_inc(init_ok.sem, 1)
                dve.wait_ge(*init_ok(n, 2))
                tt(zblk[:, :, :], zinit[:, :, :], con("eye_blocks").unsqueeze(1).to_broadcast([P, HV, BLK]), ALU.add)\
                    .then_inc(z_ok.sem, 1)
                dve.wait_ge(*z_ok(n, 1))
                nc.vector.transpose(xblk[:, :, :], zblk[:, :, :]).then_inc(x_ok.sem, 1)

            def level_a(n, k):
                o = CONST["levels"][0] + BLK * k
                dve.wait_ge(*la_ps(n, k + 1))
                tt(ablk[:, :, :], A[0][:, 0:HV * BLK].rearrange("p (h c) -> p h c", c=BLK),
                   const[:, o:o + BLK].unsqueeze(1).to_broadcast([P, HV, BLK]), ALU.mult).then_inc(a_ok.sem, 1)

            def level_b(n, k):
                dve.wait_ge(*lb_ps(n, k + 1))
                tt(zblk[:, :, :], zblk[:, :, :], A[3][:, 0:HV * BLK].rearrange("p (h c) -> p h c", c=BLK),
                   ALU.subtract).then_inc(z_ok.sem, 1)
                if k < 3:
                    dve.wait_ge(*z_ok(n, k + 2))
                    nc.vector.transpose(xblk[:, :, :], zblk[:, :, :]).then_inc(x_ok.sem, 1)

            def solve_n(n, half):
                dve.wait_ge(*n_ps(n, 1 + half))
                tt(heads(nT, half), quad(A[(0, 3)[half]]), con("outside").unsqueeze(1).to_broadcast([P, 4, P]),
                   ALU.mult).then_inc(n_ok.sem, 1)

            def horner(n, k, half):
                dve.wait_ge(*step_ps(n, 2 * k + 1 + half))
                if k == 0:
                    dve.wait_ge(*r_ok(n, 1 + half))
                tt(heads(tsol[k % 2], half), heads(rsol, half), quad(A[(0, 3)[half]]), ALU.add)\
                    .then_inc(step_ok.sem, 1)

            def core_(n, half):
                dve.wait_ge(*o_scale(n))
                for h in range(4 * half, 4 * half + 4):
                    last = stt(core[:, h, :], A[1 + half][:, (h % 4) * P:(h % 4 + 1) * P], ostat[:, OSC, h:h + 1],
                               zs[:, h, :], ALU.mult, ALU.mult)
                last.then_inc(core_ok.sem, 1)

            def a_h(n):
                dve.wait_ge(*out_ps(n))
                dve.wait_ge(*x_res(n))
                tt(hmid[:, :], xres[:, :], A[1][:, 0:D], ALU.add).then_inc(h_ok.sem, 1)

            def stats(n, k, y):
                nc.vector.bn_stats(bn[:, k, :], y[:, :]).then_inc(ln_bn.sem, 1)
                dve.wait_ge(*ln_bn(n, 2 * k + 1)).then_inc(dve_passed.sem, 1)
                nc.vector.bn_aggr(mv[:, k, :], bn[:, k, :]).then_inc(ln_bn.sem, 1)

            def normalize(n, k, out, y):
                dve.wait_ge(*ln_rstd(n, 2 * k + 2))
                return ts(out[:, :], y[:, :], mv[:, k, 0:1], lnv[:, k, 1:2], ALU.subtract, ALU.mult)

            def b_v(n):
                dve.wait_ge(*v_ps(n))
                tt(vpad[:, :, 0:HD], Bk[2][:, 0:D].rearrange("p (h d) -> p h d", d=HD),
                   rows[:, BV, :].rearrange("p (h d) -> p h d", d=HD), ALU.add).then_inc(v_ok.sem, 1)

            def b_x2(n):
                dve.wait_ge(*h_rstd(n))
                ts(x2[:, :], hmid[:, :], st_b[:, 2:3], None, ALU.mult).then_inc(x2_ok.sem, 1)

            def b_top(n):
                dve.wait_ge(*rl_ok(n)).then_inc(dve_passed.sem, 1)
                nc.vector.max(top8[:, :], rl[:, :]).then_inc(top_ok.sem, 1)
                dve.wait_ge(*top_ok(n, 1)).then_inc(dve_passed.sem, 1)
                nc.vector.max_index(idx8[:, :], top8[:, :], rl[:, :]).then_inc(top_ok.sem, 1)
                dve.wait_ge(*top_ok(n, 2))
                nc.vector.tensor_copy(idxf[:, :], idx8[:, 0:2]).then_inc(top_ok.sem, 1)

            def routed(n, half):
                dve.wait_ge(*routing(n))
                dve.wait_ge(*gu_ps(n, 2 + 2 * half))
                dve.wait_ge(*sg_ok(n, 1 + half))
                for b in range(4):
                    e = 4 * half + b
                    last = stt(act_[:, e, :], Bk[(2, 0)[half]][:, b * P:(b + 1) * P], route[:, e:e + 1], sg[:, e, :],
                               ALU.mult, ALU.mult)
                last.then_inc(act_ok.sem, 1)

            def b_sum1(n):
                dve.wait_ge(*down_ps(n))
                dve.wait_ge(*xh_ok(n))
                tt(y1p[:, :], xh[:, :], Bk[2][:, 0:D], ALU.add).then_inc(ysum.sem, 1)
                dve.wait_ge(*ysum(n, 1))
                stats(n, 0, y1p)

            def b_k(n):
                dve.wait_ge(*k_ps(n))
                dve.wait_ge(*madj_ok(n))
                for b in range(4):
                    last = stt(keys[:, b, :, :], Bk[3][:, b * P:(b + 1) * P].unsqueeze(1).to_broadcast([P, 4, P]),
                               bk[:, b:b + 1], madj[:, :, :], ALU.add, ALU.mult)
                last.then_inc(k_ok.sem, 1)

            def b_y1(n):
                normalize(n, 0, y1, y1p).then_inc(yn.sem, 1)

            def smaxes(n, b):
                dve.wait_ge(*s_ps(n, b + 1))
                nc.vector.tensor_reduce(smax[:, 4 * b:4 * b + 4], quad(Bk[b]), AX_X, ALU.max).then_inc(smax_ok.sem, 1)
                dve.wait_ge(*smax_ok(n, b + 1))
                ts(nmax[:, 4 * b:4 * b + 4], smax[:, 4 * b:4 * b + 4], -HD ** -0.5, None, ALU.mult)\
                    .then_inc(nmax_ok.sem, 1)

            def prob_T(n, i):
                dve.wait_ge(*probT_ps(n, 2 * i + 2))
                nc.vector.tensor_copy(probT[:, 2 * i + 1, :, :], quad(Bk[2 * i + 1])).then_inc(pTv_ok.sem, 1)

            def b_ao(n):
                dve.wait_ge(*sum_ps(n))
                nc.vector.reciprocal(rsum, quad(Bk[1])).then_inc(rsum_ok.sem, 1)
                dve.wait_ge(*rsum_ok(n))
                dve.wait_ge(*pv_ps(n))
                tt(aoT, rsum, quad(Bk[0]), ALU.mult).then_inc(ao_ok.sem, 1)

            def b_sum2(n):
                dve.wait_ge(*xo_ps(n))
                dve.wait_ge(*y1b_ok(n))
                tt(y2p[:, :], y1b[:, :], Bk[2][:, 0:D], ALU.add).then_inc(ysum.sem, 1)
                dve.wait_ge(*ysum(n, 2))
                stats(n, 1, y2p)

            def b_y2(n):
                normalize(n, 1, y2, y2p).then_inc(yn.sem, 1)

            def b_lb(n):
                dve.wait_ge(*lg_ps(n))
                tt(lg[:, LBIAS, :], Bk[1][:, 32:32 + NCOL], b2[:, :], ALU.add).then_inc(lb_ok.sem, 1)

            def b_route(n):
                dve.wait_ge(*lsig(n))
                dve.wait_ge(*rx_ok(n))
                stt(lg[:, LOGIT, :], Bk[1][:, 0:NCOL], rx[:, 2:3], lg[:, LSIG, :], ALU.mult, ALU.add)\
                    .then_inc(lchain.sem, 1)
                dve.wait_ge(*lchain(n, 1)).then_inc(dve_passed.sem, 1)
                nc.vector.max(lmax[:, :], lg[:, LOGIT, :]).then_inc(lchain.sem, 1)
                dve.wait_ge(*lchain(n, 2)).then_inc(dve_passed.sem, 1)
                nc.vector.max_index(lidx[:, :], lmax[:, :], lg[:, LOGIT, :]).then_inc(lchain.sem, 1)
                dve.wait_ge(*lchain(n, 3))
                nc.vector.tensor_copy(lsm[:, 0:1], lidx[:, 0:1]).then_inc(lchain.sem, 1)
                dve.wait_ge(*lchain(n, 4))
                ts(onehot[:, :], con("iota"), lsm[:, 0:1], None, ALU.is_equal).then_inc(lchain.sem, 1)
                ts(lsm[:, 1:2], lmax[:, 0:1], -0.5, None, ALU.mult).then_inc(lchain.sem, 1)

            def b_weight(n):
                dve.wait_ge(*ltanh(n, 2))
                ts(lg[:, LNUM, :], lg[:, LTE, :], 1.0, None, ALU.add).then_inc(lchain.sem, 1)
                ts(lg[:, LDEN, :], lg[:, LTE, :], -1.0, 1.0, ALU.mult, ALU.add).then_inc(lchain.sem, 1)
                dve.wait_ge(*lchain(n, 8))
                nc.vector.reciprocal(lrec[:, :], lg[:, LDEN, :]).then_inc(lchain.sem, 1)
                dve.wait_ge(*lchain(n, 9))
                nc.vector.tensor_tensor_reduce(out=lg[:, LEXP, :], in0=lg[:, LNUM, :], in1=lrec[:, :], scale=1.0,
                                               scalar=0.0, op0=ALU.mult, op1=ALU.add, accum_out=lsm[:, 2:3])\
                    .then_inc(lchain.sem, 1)
                dve.wait_ge(*lchain(n, 10))
                nc.vector.reciprocal(lsm[:, 3:4], lsm[:, 2:3]).then_inc(lchain.sem, 1)

            def gated(n, half):
                dve.wait_ge(*wb_ps(n, 1 + half))
                dve.wait_ge(*gc_ok(n, 1 + half))
                tt(heads(gcw, half), heads(gc, half), quad(Bk[half]), ALU.mult).then_inc(gcw_ok.sem, 1)

            def b_sum3(n):
                dve.wait_ge(*pj_ps(n))
                dve.wait_ge(*y2b_ok(n))
                dve.wait_ge(*lchain(n, 11))
                stt(y3p[:, :], Bk[2][:, 0:D], lsm[:, 3:4], y2pb[:, :], ALU.mult, ALU.add).then_inc(ysum.sem, 1)
                dve.wait_ge(*ysum(n, 3))
                stats(n, 2, y3p)

            def b_y3(n):
                normalize(n, 2, y3, y3p).then_inc(yn.sem, 1)
                dve.wait_ge(*yn(n, 3))
                tt(y3g[:, :], y3[:, :], rows[:, LG, :], ALU.mult).then_inc(y3_ok.sem, 1)
                dve.wait_ge(*y3_ok(n, 1))
                tt(y4[:, :], y3g[:, :], y2lb[:, :], ALU.add).then_inc(y3_ok.sem, 1)
                dve.wait_ge(*y3_ok(n, 2))
                stats(n, 3, y4)

            def b_y4(n):
                if not first(n):
                    dve.wait_ge(*stored(n - 1))
                normalize(n, 3, yout, y4).then_inc(y_out.sem, 1)

            dve.wait_ge(w_a.sem, W_A)
            dve.wait_ge(filled.sem, FILLS)
            ts(ln12[:, :, :], ln12[:, :, :], 1.0, None, ALU.add).then_inc(prep.sem, 1)
            nc.vector.tensor_copy(ident_bf[:, :], ident).then_inc(prep.sem, 1)
            nc.vector.tensor_copy(quad(above_bf), con("above").unsqueeze(1).to_broadcast([P, 4, P])).then_inc(prep.sem, 1)
            ts(wout[:, :, :], wout[:, :, :], gnw[:, 0:1], None, ALU.mult).then_inc(prep.sem, 1)
            dve.wait_ge(prep.sem, 4)
            for c in range(KC):
                ts(wqkvz[:, c, :], wqkvz[:, c, :], ln12[:, 0, c:c + 1], None, ALU.mult).then_inc(prep.sem, 1)
                ts(wba[:, c, :], wba[:, c, :], ln12[:, 0, c:c + 1], None, ALU.mult).then_inc(prep.sem, 1)
            dve.wait_ge(alog_exp.sem, 1)
            ts(negA[:, :], negA[:, :], -1.0, None, ALU.mult).then_inc(prep.sem, 1)
            dve.wait_ge(w_b.sem, W_B)
            for c in range(KC):
                ts(wr[:, c, :], wr[:, c, :], ln12[:, 1, c:c + 1], None, ALU.mult)
                ts(wg[:, c, :], wg[:, c, :], ln12[:, 1, c:c + 1], None, ALU.mult)
                ts(wu[:, c, :], wu[:, c, :], ln12[:, 1, c:c + 1], None, ALU.mult).then_inc(prep.sem, 1)
            nc.vector.tensor_copy(spread_bf[:, :], spread_in).then_inc(prep.sem, 1)
            dve.wait_ge(ce_rnorm.sem, 2)
            ts(cen[:, :], ce[:, :], ce_stat[:, 2:3], None, ALU.mult).then_inc(cen_ok.sem, 1)
            dve.wait_ge(ce_ps.sem, 1)
            for c in range(KC):
                nc.vector.tensor_copy(cenT[:, c, :], Bk[1][:, c * P:c * P + NCOL]).then_inc(prep.sem, 1)
            steps = dict(a_xn=a_xn, a_ss=a_ss, a_lower=a_lower, a_score=a_score, a_init=a_init, a_h=a_h, b_v=b_v,
                         b_x2=b_x2, b_top=b_top, b_sum1=b_sum1, b_k=b_k, b_y1=b_y1, b_ao=b_ao, b_sum2=b_sum2,
                         b_y2=b_y2, b_lb=b_lb, b_route=b_route, b_weight=b_weight, b_sum3=b_sum3, b_y3=b_y3,
                         b_y4=b_y4)
            for name, f in (("a_u", values), ("a_n", solve_n), ("a_core", core_), ("b_act", routed), ("b_pT", prob_T),
                            ("b_gc", gated)):
                for half in range(2):
                    steps[f"{name}{half}"] = lambda n, f=f, half=half: f(n, half)
            for name, f in (("a_conv", taps), ("a_la", level_a), ("a_lb", level_b), ("b_max", smaxes)):
                for i in range(4):
                    steps[f"{name}{i}"] = lambda n, f=f, i=i: f(n, i)
            for k in range(3):
                for half in range(2):
                    steps[f"a_step{k}{half}"] = lambda n, k=k, half=half: horner(n, k, half)
            run(steps, ORDER["dve"], dve)

        @block.gpsimd
        def _(pool):
            tt, ts = nc.gpsimd.tensor_tensor, nc.gpsimd.tensor_scalar

            def power(out, base):
                return tt(out, base, nhalf[:, 0:base.shape[-1]], ALU.pow)

            def a_x(n):
                pool.wait_ge(*x_loaded(n))
                pool.wait_ge(*x_sumsq(n)).then_inc(pool_passed.sem, 1)
                ts(st_a[:, 1:2], st_a[:, 0:1], 1.0 / D, EPS_RMS, ALU.mult, ALU.add).then_inc(x_rstd.sem, 1)
                pool.wait_ge(*x_rstd(n, 1))
                power(st_a[:, 2:3], st_a[:, 1:2]).then_inc(x_rstd.sem, 1)
                ts(xres[:, :], xin[:, :], 1.0, 0.0, ALU.mult, ALU.add).then_inc(x_res.sem, 1)

            def a_ga(n):
                pool.wait_ge(*ba_ok(n))
                tt(gate[:, ADT, :], ba[:, HV:2 * HV], dtb[:, :], ALU.add).then_inc(gates.sem, 1)
                pool.wait_ge(*gates(n, 1)).then_inc(pool_passed.sem, 1)
                ts(gate[:, SPM, :], gate[:, ADT, :], 0.0, 0.0, ALU.max, ALU.add).then_inc(gates.sem, 1)
                ts(gate[:, MINA, :], gate[:, ADT, :], 0.0, 0.0, ALU.min, ALU.add).then_inc(gates.sem, 1)
                pool.wait_ge(*gates(n, 3))
                tt(gate[:, NABS, :], gate[:, MINA, :], gate[:, SPM, :], ALU.subtract).then_inc(gates.sem, 1)

            def pairs(ap):
                return ap.rearrange("p (a b) -> p a b", b=HV // HK)

            def a_sc(n):
                pool.wait_ge(*tb_ok(n)).then_inc(pool_passed.sem, 1)
                ts(gate[:, BETA, :], gate[:, TB, :], 0.5, 0.5, ALU.mult, ALU.add).then_inc(gates.sem, 1)
                pool.wait_ge(*sse_ok(n))
                power(rqk[:, :], sse[:, :]).then_inc(rqk_ok.sem, 1)
                pool.wait_ge(*rqk_ok(n))
                pool.wait_ge(*gates(n, 5))
                rk = cols(rqk[:, HK:2 * HK], HV // HK)
                tt(pairs(krb[:, :]), pairs(gate[:, BETA, :]), rk, ALU.mult).then_inc(kscale.sem, 1)
                pool.wait_ge(*kscale(n, 1))
                tt(pairs(ckk[:, :]), pairs(krb[:, :]), rk, ALU.mult).then_inc(kscale.sem, 1)

            def a_g(n):
                pool.wait_ge(*eln(n))
                tt(gate[:, SP, :], gate[:, SPM, :], gate[:, LNP, :], ALU.add).then_inc(gates.sem, 1)
                pool.wait_ge(*gates(n, 6))
                tt(gate[:, G, :], gate[:, SP, :], negA[:, :], ALU.mult).then_inc(gates.sem, 1)
                pool.wait_ge(*gates(n, 7)).then_inc(pool_passed.sem, 1)
                for h in range(HV):
                    last = ts(gseg[:, h, :], con("later"), gate[:, G, h:h + 1], None, ALU.mult)
                    if h % 4 == 3:
                        last.then_inc(gseg_ok.sem, 1)

            def a_osc(n):
                ts(ostat[:, RQS, 0:HK], rqk[:, 0:HK], DK ** -0.5, 0.0, ALU.mult, ALU.add).then_inc(o_scale.sem, 1)
                pool.wait_ge(*o_scale(n, 1))
                rq = cols(ostat[:, RQS, 0:HK], HV // HK)
                tt(pairs(ostat[:, RQ2, :]), rq, rq, ALU.mult).then_inc(o_scale.sem, 1)
                pool.wait_ge(*o_scale(n, 2))
                pool.wait_ge(*o_sumsq(n))
                tt(ostat[:, OM, :], ostat[:, OSS, :], ostat[:, RQ2, :], ALU.mult).then_inc(o_scale.sem, 1)
                pool.wait_ge(*o_scale(n, 3)).then_inc(pool_passed.sem, 1)
                ts(ostat[:, OV, :], ostat[:, OM, :], 1.0 / P, EPS_RMS, ALU.mult, ALU.add).then_inc(o_scale.sem, 1)
                pool.wait_ge(*o_scale(n, 4))
                power(ostat[:, OP, :], ostat[:, OV, :]).then_inc(o_scale.sem, 1)
                pool.wait_ge(*o_scale(n, 5))
                tt(pairs(ostat[:, OSC, :]), pairs(ostat[:, OP, :]), rq, ALU.mult).then_inc(o_scale.sem, 1)

            def a_xh(n):
                pool.wait_ge(*h_ok(n))
                tt(xh[:, :], hmid[:, :], xres[:, :], ALU.add).then_inc(xh_ok.sem, 1)

            def b_mask(n):
                pool.wait_ge(*m_loaded(n)).then_inc(pool_passed.sem, 1)
                q = CONST["quadrant"][0]
                for j in range(4):
                    last = ts(madj[:, j, :], m_u8[:, :], con("mask_row"), const[:, q + j:q + j + 1], ALU.add, ALU.mult)
                last.then_inc(madj_ok.sem, 1)

            def b_rs(n):
                pool.wait_ge(*h_sumsq(n)).then_inc(pool_passed.sem, 1)
                ts(st_b[:, 1:2], st_b[:, 0:1], 1.0 / D, EPS_RMS, ALU.mult, ALU.add).then_inc(h_rstd.sem, 1)
                pool.wait_ge(*h_rstd(n, 1))
                power(st_b[:, 2:3], st_b[:, 1:2]).then_inc(h_rstd.sem, 1)

            def b_rt(n):
                pool.wait_ge(*top_ok(n))
                tt(rmix[:, 0:1], top8[:, 0:1], top8[:, 1:2], ALU.subtract).then_inc(routing.sem, 1)
                pool.wait_ge(*rtanh(n)).then_inc(pool_passed.sem, 1)
                for i, sign in enumerate((0.5, -0.5)):
                    ts(rmix[:, 2 + i:3 + i], rmix[:, 1:2], sign, 0.5, ALU.mult, ALU.add).then_inc(routing.sem, 1)
                pool.wait_ge(*routing(n, 3)).then_inc(pool_passed.sem, 1)
                for i in range(2):
                    ts(r12[:, i, :], const[:, CONST["iota"][0]:CONST["iota"][0] + NEXP], idxf[:, i:i + 1],
                       rmix[:, 2 + i:3 + i], ALU.is_equal, ALU.mult).then_inc(routing.sem, 1)
                pool.wait_ge(*routing(n, 5))
                tt(route[:, :], r12[:, 0, :], r12[:, 1, :], ALU.add).then_inc(routing.sem, 1)

            def rstd(n, k):
                pool.wait_ge(*ln_bn(n, 2 * k + 2)).then_inc(pool_passed.sem, 1)
                ts(lnv[:, k, 0:1], mv[:, k, 1:2], 1.0, EPS_LN, ALU.mult, ALU.add).then_inc(ln_rstd.sem, 1)
                pool.wait_ge(*ln_rstd(n, 2 * k + 1))
                power(lnv[:, k, 1:2], lnv[:, k, 0:1]).then_inc(ln_rstd.sem, 1)

            def b_y1b(n):
                pool.wait_ge(*yn(n, 1))
                tt(y1b[:, :], y1[:, :], rows[:, BO, :], ALU.add).then_inc(y1b_ok.sem, 1)

            def b_rx(n):
                pool.wait_ge(*ln_rstd(n, 4)).then_inc(pool_passed.sem, 1)
                ts(rx[:, 0:1], mv[:, 1, 1:2], lnv[:, 1, 1:2], lnv[:, 1, 1:2], ALU.mult, ALU.mult).then_inc(rx_ok.sem, 1)
                pool.wait_ge(*rx_ok(n, 1)).then_inc(pool_passed.sem, 1)
                ts(rx[:, 1:2], rx[:, 0:1], float(D), 1e-24, ALU.mult, ALU.max).then_inc(rx_ok.sem, 1)
                pool.wait_ge(*rx_ok(n, 2))
                power(rx[:, 2:3], rx[:, 1:2]).then_inc(rx_ok.sem, 1)

            def b_y2b(n):
                pool.wait_ge(*yn(n, 2))
                for out, row in ((y2pb, BP), (y2lb, LB)):
                    tt(out[:, :], y2[:, :], rows[:, row, :], ALU.add).then_inc(y2b_ok.sem, 1)

            def b_sig(n):
                pool.wait_ge(*ltanh(n, 1)).then_inc(pool_passed.sem, 1)
                ts(lg[:, LSIG, :], lg[:, LTANH, :], 0.5, 0.5, ALU.mult, ALU.add).then_inc(lsig.sem, 1)

            nc.gpsimd.memset(nhalf[:, :], -0.5).then_inc(filled.sem, 1)
            nc.gpsimd.memset(ones[:, :], 1.0).then_inc(filled.sem, 1)
            nc.gpsimd.memset(ypad[:, :, 0:TAPS - 1], 0.0).then_inc(filled.sem, 1)
            nc.gpsimd.memset(zfull[:, :, :], 0.0).then_inc(filled.sem, 1)
            nc.gpsimd.memset(vpad[:, :, :], 0.0).then_inc(filled.sem, 1)
            pool.wait_ge(filled.sem, FILLS)
            pool.wait_ge(ce_sumsq.sem, 1)
            ts(ce_stat[:, 1:2], ce_stat[:, 0:1], 1.0, 1e-24, ALU.mult, ALU.max).then_inc(ce_rnorm.sem, 1)
            pool.wait_ge(ce_rnorm.sem, 1)
            tt(ce_stat[:, 2:3], ce_stat[:, 1:2], nhalf[0:NCOL, 0:1], ALU.pow).then_inc(ce_rnorm.sem, 1)
            pool.wait_ge(w_a.sem, W_A)
            pool.wait_ge(w_b.sem, W_B)
            pool.wait_ge(prep.sem, PREP_A)
            steps = dict(a_x=a_x, a_ga=a_ga, a_sc=a_sc, a_g=a_g, a_osc=a_osc, a_xh=a_xh, b_mask=b_mask, b_rs=b_rs,
                         b_rt=b_rt, b_y1b=b_y1b, b_rx=b_rx, b_y2b=b_y2b, b_sig=b_sig)
            for k in range(4):
                steps[f"b_ln{k}"] = lambda n, k=k: rstd(n, k)
            run(steps, ORDER["pool"], pool)


def kernel(**inputs):
    import concourse.bacc as bacc
    from concourse.bass_utils import run_bass_kernel_spmd

    a = {k.split("_", 2)[2] if k.startswith("L0") else k: np.asarray(v) for k, v in inputs.items()}

    def rows_first(w):
        return w.reshape(-1, P, w.shape[-1]).transpose(1, 0, 2)

    def experts(w):
        e, d, i = w.shape
        return w.reshape(e, KC, P, i).transpose(2, 1, 0, 3).reshape(P, KC, e * i)

    def padded_heads(w):
        out = np.zeros((4, 4, 32, D), w.dtype)
        out[:, :, :HD] = w.reshape(4, 4, HD, D)
        return out.reshape(4 * P, D)

    def head_rows(w):
        return rows_first(padded_heads(w).T)

    def head_bias(b, extra):
        out = np.zeros((4, 4, 32), b.dtype)
        out[:, :, :HD] = b.reshape(4, 4, HD)
        out[:, :, HD] = extra
        return out.transpose(1, 2, 0).reshape(P, 4)

    arrays = dict(
        x=a["x"], ctx=a["ctx_1024"], mask=a["mask_BxS2_bf1"].astype(np.uint8)[:, None, :], const=constants(), spread=spread(),
        wqkvz=rows_first(a["W_qkvz"]), wba=rows_first(a["W_ba"]),
        convw=a["conv_w"].reshape(CONV_BLOCKS, P, TAPS).transpose(1, 0, 2),
        ln12=np.stack([a["w_ln1"].reshape(KC, P).T, a["w_ln2"].reshape(KC, P).T], 1),
        dt=a["dt_bias"], alog=a["A_log"], gnw=a["gate_norm_w"][:, None], wout=rows_first(a["W_out"]),
        wr=rows_first(a["W_router"]), wg=experts(a["W_gate_e"]), wu=experts(a["W_up_e"]),
        wd=a["W_down_e"].transpose(1, 0, 2),
        wq=head_rows(a["Wq"]), wk=head_rows(a["Wk"]), wv=rows_first(a["Wv"].T), wo=rows_first(padded_heads(a["Wo"].T)),
        bq=head_bias(a["bq"], 1.0), bk=head_bias(a["bk"], FILL), bv=a["bv"], bo=a["bo"],
        ce=a["col_emb"], w1=rows_first(a["gate_w1"]), b1=a["gate_b1"][:, None], w2=a["gate_w2"], b2=a["gate_b2"],
        wc=experts(a["W_cols"]), bc=a["b_cols"].reshape(8, P).T, wp=rows_first(a["proj_w"]), bp=a["proj_b"],
        lng=a["ln_g"], lnb=a["ln_b"])
    nc = bacc.Bacc("TRN2", target_bir_lowering=False, num_devices=1)
    data, args = {}, []
    for name, v in arrays.items():
        v = np.ascontiguousarray(v)
        data[f"in_{name}_dram"] = v
        args.append(nc.dram_tensor(f"in_{name}_dram", v.shape, mybir.dt.from_np(v.dtype), kind="ExternalInput").ap())
    args.append(nc.dram_tensor("out_0_dram", a["x"].shape, F32, kind="ExternalOutput").ap())
    build(nc, *args)
    r = run_bass_kernel_spmd(nc, [data], core_ids=[0])
    return r.results[0]["out_0_dram"]
```

```python
from contextlib import ExitStack

import numpy as np

import concourse.bass as bass
import concourse.mybir as mybir

F32 = mybir.dt.float32
BF16 = mybir.dt.bfloat16
U8 = mybir.dt.uint8
U32 = mybir.dt.uint32
ALU = mybir.AluOpType
ACT = mybir.ActivationFunctionType
AX_X = mybir.AxisListType.X

P = 128
D = 256
KC = D // P
HK, HV = 4, 8
DK = 128
QK_BLOCKS = 2 * HK
CONV_BLOCKS = QK_BLOCKS + HV
TAPS = 4
CONV_DIM = CONV_BLOCKS * P
NEXP = 8
NH, HD = 16, 16
NCOL = 16
BLK = 32
NBLK = P // BLK
LEVELS = (2, 4, 8, 16)
EPS_RMS = 1e-6
EPS_LN = 1e-5
FILL = 1e8 * HD ** 0.5

CONST = {}
_at = 0
for _name, _width in (("ident", P), ("upto", P), ("later", P), ("above", P), ("outside", P),
                      ("level1", BLK), ("levels", len(LEVELS) * BLK), ("eye_blocks", BLK),
                      ("iota", NCOL), ("mask_row", 1), ("quadrant", 4)):
    CONST[_name] = (_at, _at + _width)
    _at += _width
CONST_COLS = _at


def constants():
    c = np.zeros((P, CONST_COLS), np.float32)
    p = np.arange(P)[:, None]
    f = np.arange(P)[None, :]

    def put(name, a):
        c[:a.shape[0], CONST[name][0]:CONST[name][1]] = a

    put("ident", (p == f) * 1.0)
    put("upto", (p <= f) * 1.0)
    put("later", (p > f) * 1.0)
    put("above", (f > p) * -1e30)
    put("outside", (p // BLK < f // BLK) * -1.0)
    r, q = p % BLK, np.arange(BLK)[None, :]

    def sibling(s):
        return ((r // (2 * s) == q // (2 * s)) & ((r // s) % 2 == 0) & ((q // s) % 2 == 1)) * 1.0

    put("level1", -sibling(1))
    put("levels", np.concatenate([sibling(s) for s in LEVELS], 1))
    put("eye_blocks", (r == q) * 1.0)
    put("iota", np.tile(np.arange(NCOL)[None, :], (P, 1)))
    put("mask_row", (p % 32 == HD) * -1.0)
    put("quadrant", (p // 32 == np.arange(4)[None, :]) * 1.0)
    return c


def spread():
    return ((np.arange(NCOL)[:, None] == np.arange(8 * P)[None, :] // 64) * 1.0).astype(np.float32)


class Signal:

    def __init__(self, ctx, nc, name, per=1):
        self.sem = ctx.enter_context(nc.semaphore(name))
        self.per = per

    def __call__(self, n, c=None):
        c = self.per if c is None else c
        return (self.sem, n * self.per if c == self.per else n * self.per - (self.per - c))


def first(n):
    return isinstance(n, int) and n == 1


ORDER = dict(
    pe="c_s0 c_s1 c_s2 a_xT c_s3 c_pT0 a_ba a_qkv0 c_pT1 c_pT2 c_pT3 a_qkv1 c_R c_pv a_qkv2 c_xo a_qkv3 a_z0 "
       "c_y2T a_z1 c_h c_c0 a_ss a_kk a_qk c_lg c_c1 a_dec0 c_wT a_dec1 c_spread c_pj0 c_pj1 b_oT0 b_oT1 b_w0 "
       "b_w1 b_cT a_la00 a_la01 a_lb00 b_v a_sT0 a_lb01 a_sT1 b_x2T a_la10 a_la11 b_router b_gu0 a_lb10 "
       "a_lb11 b_gu1 a_la20 a_la21 a_vT0 a_lb20 a_lb21 b_gu2 b_gu3 a_vT1 a_la30 a_la31 b_aT0 b_aT1 a_lb30 "
       "b_dn0 a_lb31 b_dn1 b_k a_r0 a_n0 a_r1 a_n1 a_step00 a_step01 a_step10 b_y1T a_step11 a_step20 "
       "a_step21 a_o0 a_o1 b_q".split(),
    act="a_sum c_exp0 a_xT c_exp1 c_exp2 c_exp3 c_pT0 a_ba c_pT1 a_qkv0 c_R a_qkv1 a_qkv2 a_qkv3 a_mix0 c_y2T "
       "a_z0 a_z1 a_mix1 a_sq a_ln c_h c_c0 c_lt a_seg c_c1 c_wT a_dec0 a_dec1 c_te a_diag b_oT0 b_oT1 b_cT "
       "b_sum b_x2T a_sT0 a_sT1 b_rl a_mix2 b_sg0 b_rt b_sg1 a_mix3 b_aT0 b_aT1 a_zf a_r0 a_r1 b_y1T a_o0 "
       "a_o1 b_q".split(),
    dve="c_max0 a_xn c_max1 c_max2 c_max3 c_pT0 c_pT1 c_rec a_conv00 c_ao a_conv01 a_conv02 a_conv10 c_sum2 "
       "a_conv11 c_y2 a_conv12 a_ss c_lb c_route c_gc0 c_gc1 a_lower c_weight a_score c_sum3 a_init c_y3 "
       "a_la00 a_la01 c_y4 b_hid a_conv20 b_v b_x2 a_lb00 a_lb01 a_conv21 a_la10 a_la11 a_conv22 a_lb10 b_top "
       "a_lb11 a_conv30 a_la20 a_la21 a_conv31 a_lb20 a_lb21 a_conv32 b_act0 b_act1 a_u0 a_la30 a_la31 a_u1 "
       "a_lb30 a_lb31 b_sum1 b_k a_n0 a_n1 a_step00 b_y1 a_step01 a_step10 a_step11 a_step20 a_step21 a_core0 "
       "a_core1".split(),
    pool="a_x a_ga c_ln1 c_rx c_y2b a_g c_sig a_sc a_rq c_ln2 c_ln3 b_rs b_xh a_xr b_rd b_rt b_mask b_ln0 "
       "a_osc0 a_osc1 b_y1b".split(),
)


def build(nc, x_d, ctx_d, mask_d, const_d, spread_d, wqkvz_d, wba_d, convw_d, ln12_d, dt_d, alog_d, gnw_d, wout_d,
          wr_d, wg_d, wu_d, wd_d, wq_d, wk_d, wv_d, wo_d, bq_d, bk_d, bv_d, bo_d, ce_d, w1_d, b1_d, w2_d, b2_d,
          wc_d, bc_d, wp_d, bp_d, lng_d, lnb_d, out_d):
    B = x_d.shape[0]
    with ExitStack() as ctx:
        def sb(name, shape, dt=F32):
            return ctx.enter_context(nc.sbuf_tensor(name, shape, dt))

        def sig(name, per=1):
            return Signal(ctx, nc, name, per)

        const = sb("const", [P, CONST_COLS])
        wqkvz = sb("wqkvz", [P, KC, CONV_DIM + HV * P])
        wba = sb("wba", [P, KC, 2 * HV])
        convw = sb("convw", [P, CONV_BLOCKS, TAPS])
        ln12 = sb("ln12", [P, 2, KC])
        dtb = sb("dtb", [P, HV])
        negA = sb("negA", [P, HV])
        gnw = sb("gnw", [P, 1])
        wout = sb("wout", [P, HV, D])
        wr = sb("wr", [P, KC, NEXP])
        wg = sb("wg", [P, KC, NEXP * P])
        wu = sb("wu", [P, KC, NEXP * P])
        wd = sb("wd", [P, NEXP, D])
        wq = sb("wq", [P, KC, 4 * P])
        wk = sb("wk", [P, KC, 4 * P])
        wv = sb("wv", [P, KC, D])
        wo = sb("wo", [P, 4, D])
        bq = sb("bq", [P, 4])
        bk = sb("bk", [P, 4])
        rows = sb("rows", [P, 5, D])
        BV, BO, BP, LG, LB = range(5)
        ce_stat = sb("ce_stat", [NCOL, 4])
        cenT = sb("cenT", [P, KC, NCOL])
        w1 = sb("w1", [P, KC, P])
        b1 = sb("b1", [P, 1])
        w2 = sb("w2", [P, NCOL])
        b2 = sb("b2", [P, NCOL])
        wc = sb("wc", [P, KC, NCOL * 64])
        bc = sb("bc", [P, 8])
        wp = sb("wp", [P, 8, D])
        ident_bf = sb("ident_bf", [P, P], BF16)
        above_bf = sb("above_bf", [P, 4 * P], BF16)
        spread_bf = sb("spread_bf", [NCOL, 8 * P], BF16)
        ones = sb("ones", [P, 32])
        nhalf = sb("nhalf", [P, NCOL])

        def con(name, rows_=P):
            a, b = CONST[name]
            return const[0:rows_, a:b]

        ident = con("ident")

        xin = sb("xin", [P, D])
        xres = sb("xres", [P, D])
        junk_a = sb("junk_a", [P, D])
        st_a = sb("st_a", [P, 4])
        xn = sb("xn", [P, D])
        xnT = sb("xnT", [P, KC, P])
        ypad = sb("ypad", [P, CONV_BLOCKS, TAPS - 1 + P])
        acc = sb("acc", [P, CONV_BLOCKS, P])
        mixed = sb("mixed", [P, CONV_BLOCKS, P])
        zs = sb("zs", [P, HV, P])
        ba = sb("ba", [P, 2 * HV])
        gate = sb("gate", [P, 10, HV])
        TB, BETA, ADT, NABS, EABS, LNP, SPM, SP, G, MINA = range(10)
        sse = sb("sse", [P, QK_BLOCKS])
        rqk = sb("rqk", [P, QK_BLOCKS])
        krb = sb("krb", [P, HV])
        ckk = sb("ckk", [P, HV])
        u = sb("u", [P, HV, P])
        gseg = sb("gseg", [P, HV, P])
        decay = sb("decay", [P, HV, P])
        lower = sb("lower", [P, HV, P])
        scoreqk = sb("scoreqk", [P, HV, P])
        scoreT = sb("scoreT", [P, HV, P])
        sqk = scoreT
        diag = sb("diag", [P, HV, BLK])
        zblk = sb("zblk", [P, HV, BLK])
        xblk = sb("xblk", [P, HV, BLK])
        ablk = sb("ablk", [P, HV, BLK])
        diagT, zinit = xblk, ablk
        zfull = sb("zfull", [P, HV, P])
        nT = gseg
        rsol = acc[:, 0:HV, :]
        tsol = [acc[:, HV:2 * HV, :], scoreqk]
        junk_o = nT
        ostat = sb("ostat", [P, 7, HV])
        OSS, RQS, RQ2, OM, OV, OP, OSC = range(7)
        core = u
        hmid = sb("hmid", [P, D])
        xh = sb("xh", [P, D])

        cin = sb("cin", [P, D])
        m_u8 = sb("m_u8", [P, P], U8)
        madj = sb("madj", [P, 4, P])
        cT = sb("cT", [P, KC, P])
        vpad = sb("vpad", [P, NH, 32])
        junk_b = sb("junk_b", [P, D])
        st_b = sb("st_b", [P, 4])
        x2 = sb("x2", [P, D])
        x2T = sb("x2T", [P, KC, P])
        rl = sb("rl", [P, NEXP])
        top8 = sb("top8", [P, 8])
        idx8 = sb("idx8", [P, 8], U32)
        idxf = sb("idxf", [P, 2])
        rmix = sb("rmix", [P, 4])
        r12 = sb("r12", [P, 2, NEXP])
        route = sb("route", [P, NEXP])
        y1p = sb("y1p", [P, D])
        y1 = sb("y1", [P, D])
        y1b = sb("y1b", [P, D])
        bn = sb("bn", [P, 4, 6])
        mv = sb("mv", [P, 4, 2])
        lnv = sb("lnv", [P, 4, 2])
        y1T = x2T
        qT = sb("qT", [P, 4, P])
        smax = sb("smax", [P, NH])
        nmax = sb("nmax", [P, NH])
        esum = sb("esum", [P, NH])
        rinv = sb("rinv", [P, NH])
        prob = sb("prob", [P, 4, 4, P])
        probT = sb("probT", [P, 4, 4, P])
        flat = prob[:, :, :, :].rearrange("p a b f -> p (a b) f")
        sg, act_ = flat[:, 0:NEXP, :], flat[:, NEXP:2 * NEXP, :]
        actT = probT[:, 0:2, :, :].rearrange("p a b f -> p (a b) f")
        keys = probT
        rsum, aoT, rexp = prob[:, 0, :, :], prob[:, 1, :, :], prob[:, 2, :, :]
        spread_in = flat[0:NCOL, 0:8, :].rearrange("p a f -> p (a f)")
        y2p = y1p
        y2 = sb("y2", [P, D])
        y2pb = y1b
        y2lb = sb("y2lb", [P, D])
        rx = sb("rx", [P, 3])
        y2T = x2T
        hT = sb("hT", [P, P])
        gc, gcw, coreT = sg, act_, sg
        lg = sb("lg", [P, 8, NCOL])
        LBIAS, LTANH, LSIG, LOGIT, LTE, LNUM, LDEN, LEXP = range(8)
        lrec = sb("lrec", [P, NCOL])
        lmax = sb("lmax", [P, 8])
        lidx = sb("lidx", [P, 8], U32)
        lsm = sb("lsm", [P, 4])
        onehot = sb("onehot", [P, NCOL])
        wT = sb("wT", [NCOL, P], BF16)
        y3p = y1p
        y3 = sb("y3", [P, D])
        y3g = x2
        y4 = sb("y4", [P, D])
        yout = sb("yout", [P, D])
        ce, ce_junk, cen = yout[0:NCOL, :], junk_b[0:NCOL, :], y4[0:NCOL, :]

        A = [ctx.enter_context(nc.psum_tensor(f"bank_a{i}", [P, 512], F32)) for i in range(4)]
        Bk = [ctx.enter_context(nc.psum_tensor(f"bank_b{i}", [P, 512], F32)) for i in range(4)]

        GROUPS = ((2, HK), (1, 0), (3, 2 * HK), (0, 3 * HK))
        A_LEVEL = (A[0], A[3])

        def quad(bank):
            return bank[:, :].rearrange("p (a b) -> p a b", b=P)

        w_a, w_b = sig("weights_a"), sig("weights_b")
        prep = sig("prep")
        filled = sig("filled")
        ce_sumsq, alog_exp, ce_rnorm, cen_ok = sig("ce_sumsq"), sig("alog_exp"), sig("ce_rnorm", 2), sig("cen_ok")
        ce_ps = sig("ce_ps")
        x_loaded, c_loaded, m_loaded = sig("x_loaded", 16), sig("c_loaded", 16), sig("m_loaded", 16)
        stored = sig("stored", 16)
        pe_passed, dve_passed, pool_passed = sig("pe_passed"), sig("dve_passed"), sig("pool_passed")
        x_sumsq, x_rstd, x_res, x_norm = sig("x_sumsq"), sig("x_rstd", 2), sig("x_res"), sig("x_norm")
        xnT_ps, xnT_ok = sig("xnT_ps"), sig("xnT_ok")
        qkv_ps, y_ok, tap_last, conv = sig("qkv_ps", 4), sig("y_ok", 4), sig("tap_last", 16), sig("conv", 48)
        mixed_ok = sig("mixed_ok", 4)
        z_ps, ba_ps, zs_ok, ba_ok = sig("z_ps", 2), sig("ba_ps"), sig("zs_ok", 2), sig("ba_ok")
        tb_ok, eln, gates = sig("tb_ok"), sig("exp_ln", 2), sig("gates", 7)
        sq_ok, ss_ps, sse_ok, rqk_ok, kscale = sig("sq_ok"), sig("ss_ps"), sig("sse_ok"), sig("rqk_ok"), sig("kscale", 2)
        vT_ps, u_ok = sig("vT_ps", 2), sig("u_ok", 2)
        gseg_ok, decay_ps, decay_ok = sig("gseg_ok"), sig("decay_ps", 2), sig("decay_ok", 2)
        gsegb_ok, rinv_ok, rexp_ok = sig("gsegb_ok"), sig("rinv_ok"), sig("rexp_ok")
        kk_ps, qk_ps, lower_ok, score_ok = sig("kk_ps"), sig("qk_ps"), sig("lower_ok"), sig("score_ok")
        diag_ok, init_ok = sig("diag_ok"), sig("init_ok", 2)
        z_ok, x_ok = sig("z_ok", 10), sig("x_ok", 8)
        la_ps, a_ok, lb_ps = sig("la_ps", 8), sig("a_ok", 8), sig("lb_ps", 8)
        scoreT_ps, scoreT_ok = sig("scoreT_ps", 2), sig("scoreT_ok", 2)
        zfull_ok, r_ps, r_ok, n_ps, n_ok = sig("zfull_ok"), sig("r_ps", 2), sig("r_ok", 2), sig("n_ps", 2), sig("n_ok", 2)
        step_ps, step_ok = sig("step_ps", 6), sig("step_ok", 6)
        o_ps, o_sumsq, o_scale, core_ok = sig("o_ps", 2), sig("o_sumsq", 2), sig("o_scale", 10), sig("core_ok", 2)
        coreT_ps, coreT_ok, out_ps, h_ok, xh_ok = sig("coreT_ps", 2), sig("coreT_ok", 2), sig("out_ps"), sig("h_ok"), sig("xh_ok")

        cT_ps, cT_ok, madj_ok, k_ps, v_ps, k_ok, v_ok = (sig("cT_ps"), sig("cT_ok"), sig("madj_ok"), sig("k_ps"),
                                                         sig("v_ps"), sig("k_ok"), sig("v_ok"))
        h_sumsq, h_rstd, x2_ok, x2T_ps, x2T_ok = sig("h_sumsq"), sig("h_rstd", 2), sig("x2_ok"), sig("x2T_ps"), sig("x2T_ok")
        rl_ps, rl_ok, gu_ps, sg_ok = sig("rl_ps"), sig("rl_ok"), sig("gu_ps", 4), sig("sg_ok", 2)
        top_ok, rtanh, routing = sig("top_ok", 3), sig("rtanh"), sig("routing", 6)
        act_ok, actT_ps, actT_ok, down_ps = sig("act_ok", 2), sig("actT_ps", 2), sig("actT_ok", 2), sig("down_ps")
        ysum, ln_bn, ln_rstd, yn = sig("ysum", 3), sig("ln_bn", 8), sig("ln_rstd", 8), sig("yn", 3)
        y1b_ok, y1T_ps, y1T_ok, q_ps, q_ok = sig("y1b_ok"), sig("y1T_ps"), sig("y1T_ok"), sig("q_ps"), sig("q_ok")
        s_ps, smax_ok, nmax_ok, prob_ok = sig("s_ps", 4), sig("smax_ok", 4), sig("nmax_ok", 4), sig("prob_ok", 4)
        probT_ps, pTa_ok, pTv_ok = sig("probT_ps", 4), sig("probT_act", 2), sig("probT_dve", 2)
        sum_ps, pv_ps, rsum_ok, ao_ok, xo_ps = sig("sum_ps"), sig("pv_ps"), sig("rsum_ok"), sig("ao_ok"), sig("xo_ps")
        y2b_ok, rx_ok, y2T_ps, y2T_ok = sig("y2b_ok", 2), sig("rx_ok", 3), sig("y2T_ps"), sig("y2T_ok")
        hg_ps, hT_ok, c_ps, gc_ok, lg_ps = sig("hg_ps"), sig("hT_ok"), sig("c_ps", 2), sig("gc_ok", 2), sig("lg_ps")
        lb_ok, ltanh, lsig, lchain = sig("lb_ok"), sig("ltanh", 2), sig("lsig"), sig("lchain", 11)
        wT_ps, wT_ok, wb_ps, gcw_ok, pj_ps = sig("wT_ps"), sig("wT_ok"), sig("wb_ps", 2), sig("gcw_ok", 2), sig("pj_ps")
        y3_ok, y_out = sig("y3_ok", 2), sig("y_out")

        loads_a = [(const, const_d), (wqkvz, wqkvz_d), (wba, wba_d), (convw, convw_d), (wout, wout_d),
                   (ln12, ln12_d), (gnw, gnw_d)]
        loads_b = [(wr, wr_d), (wg, wg_d), (wu, wu_d), (wd, wd_d), (wq, wq_d), (wk, wk_d), (wv, wv_d), (wo, wo_d),
                   (bq, bq_d), (bk, bk_d), (w1, w1_d), (w2, w2_d), (wc, wc_d), (bc, bc_d), (wp, wp_d), (ce, ce_d), (b1, b1_d), (spread_in, spread_d)]

        small_a = [(dtb[:, :], dt_d.partition_broadcast(P)), (negA[:, :], alog_d.partition_broadcast(P))]
        small_b = [(rows[:, BV, :], bv_d.partition_broadcast(P)), (rows[:, BO, :], bo_d.partition_broadcast(P)),
                   (rows[:, BP, :], bp_d.partition_broadcast(P)), (rows[:, LG, :], lng_d.partition_broadcast(P)),
                   (rows[:, LB, :], lnb_d.partition_broadcast(P)), (b2[:, :], b2_d.partition_broadcast(P))]
        W_A = 16 * (len(loads_a) + len(small_a))
        W_B = 16 * (len(loads_b) + len(small_b))
        FILLS = 5
        PREP_A, PREP_B = 9, 14

        def heads(t, half):
            return t[:, 4 * half:4 * half + 4, :]

        def cols(ap, n):
            return ap.unsqueeze(2).to_broadcast([ap.shape[0], ap.shape[1], n])

        block = ctx.enter_context(nc.Block())

        def run(steps, order, engine, before_b):
            assert sorted(steps) == sorted(order)

            def go(n_a, n_b, n_c):
                for name in order:
                    n = dict(a=n_a, b=n_b, c=n_c)[name[0]]
                    if n is not None:
                        steps[name](n)
            go(1, None, None)
            before_b()
            go(2, 1, None)
            go(3, 2, 1)
            with engine.Fori(4, B + 1) as i:
                go(i, i - 1, i - 2)
            go(None, B, B - 1)
            go(None, None, B)

        @block.sync
        def _(sp):
            def load_x(n):
                if not first(n):
                    sp.wait_ge(*x_norm(n - 1))
                    sp.wait_ge(*x_res(n - 1))
                sp.dma_start(xin[:, :], x_d[n - 1, :, :]).then_inc(x_loaded.sem, 16)

            def load_ctx(n):
                if not first(n):
                    sp.wait_ge(*cT_ps(n - 1))
                    sp.wait_ge(*madj_ok(n - 1))
                sp.dma_start(cin[:, :], ctx_d[n - 1, :, :]).then_inc(c_loaded.sem, 16)
                sp.dma_start(m_u8[:, :], mask_d[n - 1, :, :].broadcast_to([P, P])).then_inc(m_loaded.sem, 16)

            def store(n):
                sp.wait_ge(*y_out(n))
                sp.dma_start(out_d[n - 1, :, :], yout[:, :]).then_inc(stored.sem, 16)

            load_x(1)
            for dst, src in loads_a:
                sp.dma_start(dst[:], src).then_inc(w_a.sem, 16)
            for dst, src in small_a:
                sp.dma_start(dst, src).then_inc(w_a.sem, 16)
            for dst, src in loads_b:
                sp.dma_start(dst if dst is spread_in else dst[:], src).then_inc(w_b.sem, 16)
            for dst, src in small_b:
                sp.dma_start(dst, src).then_inc(w_b.sem, 16)
            load_x(2)
            load_ctx(1)
            load_x(3)
            load_ctx(2)
            with sp.Fori(4, B + 1) as i:
                load_x(i)
                load_ctx(i - 1)
                store(i - 3)
            load_ctx(B)
            for n in range(B - 2, B + 1):
                store(n)
            sp.wait_ge(*stored(B))

        @block.tensor
        def _(pe):
            mm, tr = nc.tensor.matmul, nc.tensor.transpose

            def a_xT(n):
                pe.wait_ge(*x_norm(n))
                for c in range(KC):
                    last = tr(A[0][:, c * P:(c + 1) * P], xn[:, c * P:(c + 1) * P], ident)
                last.then_inc(xnT_ps.sem, 1)

            def qkv(n, g):
                bank, block = GROUPS[g]
                if g == 3:
                    pe.wait_ge(*ba_ok(n))
                for b in range(4):
                    o = (block + b) * P
                    for c in range(KC):
                        last = mm(A[bank][:, b * P:(b + 1) * P], wqkvz[:, c, o:o + P], xnT[:, c, :],
                                  start=(c == 0), stop=(c == KC - 1))
                last.then_inc(qkv_ps.sem, 1)

            def zgate(n, half):
                pe.wait_ge(*tap_last(n, (8, 4)[half]))
                for c in range(KC):
                    o = CONV_DIM + 512 * half
                    last = mm(A[1 + half][:, :], xnT[:, c, :], wqkvz[:, c, o:o + 512],
                              start=(c == 0), stop=(c == KC - 1))
                last.then_inc(z_ps.sem, 1)

            def a_ba(n):
                pe.wait_ge(*xnT_ok(n))
                for c in range(KC):
                    last = mm(A[0][:, D:D + 2 * HV], xnT[:, c, :], wba[:, c, :], start=(c == 0), stop=(c == KC - 1))
                last.then_inc(ba_ps.sem, 1)

            def a_ss(n):
                pe.wait_ge(*tap_last(n, 12))
                pe.wait_ge(*sq_ok(n))
                for b in range(QK_BLOCKS):
                    last = mm(A[3][:, b:b + 1], sqk[:, b, :], ones[:, 0:1], start=True, stop=True)
                last.then_inc(ss_ps.sem, 1)

            def values(n, half):
                pe.wait_ge(*mixed_ok(n, 3 + half))
                pe.wait_ge(*scoreT_ok(n, 1 + half))
                for b in range(4):
                    last = tr(A[1 + half][:, b * P:(b + 1) * P], mixed[:, QK_BLOCKS + 4 * half + b, :], ident)
                last.then_inc(vT_ps.sem, 1)

            def exponents(n, half):
                if half == 0:
                    pe.wait_ge(*tap_last(n, 16))
                else:
                    pe.wait_ge(*sse_ok(n))
                bank = (0, 3)[half]
                pe.wait_ge(*(gseg_ok, gsegb_ok)[half](n))
                mm(A[bank][:, :], ident_bf[:, :], above_bf[:, :], start=True, stop=False)
                mm(A[bank][:, :], con("upto"), heads(gseg, half), start=False, stop=True).then_inc(decay_ps.sem, 1)

            def a_kk(n):
                pe.wait_ge(*mixed_ok(n, 1))
                pe.wait_ge(*zs_ok(n, 1))
                for h in range(HK):
                    k = mixed[:, HK + h, :]
                    last = mm(A[1][:, h * P:(h + 1) * P], k, k, start=True, stop=True)
                last.then_inc(kk_ps.sem, 1)

            def a_qk(n):
                pe.wait_ge(*mixed_ok(n, 2))
                pe.wait_ge(*zs_ok(n, 2))
                for h in range(HK):
                    last = mm(A[2][:, h * P:(h + 1) * P], mixed[:, h, :], mixed[:, HK + h, :], start=True, stop=True)
                last.then_inc(qk_ps.sem, 1)

            def blocks(out, lhsT, rhs, half):
                for h in range(4 * half, 4 * half + 4):
                    for b in range(NBLK):
                        r = slice(BLK * b, BLK * (b + 1))
                        last = mm(out[r, BLK * h:BLK * (h + 1)], lhsT[r, h, :], rhs[r, h, :], start=True, stop=True)
                return last

            def level_a(n, k, half):
                if k == 0 and half == 0:
                    pe.wait_ge(*decay_ok(n, 2))
                pe.wait_ge(*z_ok(n, 2 * k + 1 + half)).then_inc(pe_passed.sem, 1)
                blocks(A_LEVEL[half], diag, zblk, half).then_inc(la_ps.sem, 1)

            def level_b(n, k, half):
                pe.wait_ge(*a_ok(n, 2 * k + 1 + half))
                pe.wait_ge(*x_ok(n, 2 * k + 1 + half)).then_inc(pe_passed.sem, 1)
                blocks(A_LEVEL[half], xblk, ablk, half).then_inc(lb_ps.sem, 1)

            def scores_T(n, half):
                if half == 0:
                    pe.wait_ge(*score_ok(n))
                    pe.wait_ge(*lower_ok(n))
                for b in range(4):
                    last = tr(A[1 + half][:, b * P:(b + 1) * P], scoreqk[:, 4 * half + b, :], ident)
                last.then_inc(scoreT_ps.sem, 1)

            def solve_r(n, half):
                pe.wait_ge(*zfull_ok(n))
                pe.wait_ge(*u_ok(n, 1 + half))
                for b in range(4):
                    h = 4 * half + b
                    last = mm(A[1 + half][:, b * P:(b + 1) * P], zfull[:, h, :], u[:, h, :], start=True, stop=True)
                last.then_inc(r_ps.sem, 1)

            def solve_n(n, half):
                bank = (0, 3)[half]
                pe.wait_ge(*zfull_ok(n))
                for b in range(4):
                    h = 4 * half + b
                    last = mm(A[bank][:, b * P:(b + 1) * P], lower[:, h, :], zfull[:, h, :], start=True, stop=True)
                last.then_inc(n_ps.sem, 1)

            def horner(n, k, half):
                bank = (0, 3)[half]
                if k == 0:
                    pe.wait_ge(*n_ok(n, 1 + half))
                    pe.wait_ge(*r_ok(n, 1 + half))
                else:
                    pe.wait_ge(*step_ok(n, 2 * k - 1 + half))
                src = rsol if k == 0 else tsol[(k - 1) % 2]
                for b in range(4):
                    h = 4 * half + b
                    last = mm(A[bank][:, b * P:(b + 1) * P], nT[:, h, :], src[:, h, :], start=True, stop=True)
                last.then_inc(step_ps.sem, 1)

            def read(n, half):
                pe.wait_ge(*step_ok(n, 5 + half))
                for b in range(4):
                    h = 4 * half + b
                    last = mm(A[1 + half][:, b * P:(b + 1) * P], scoreT[:, h, :], tsol[0][:, h, :],
                              start=True, stop=True)
                last.then_inc(o_ps.sem, 1)

            def core_T(n, half):
                pe.wait_ge(*core_ok(n, 1 + half))
                if not first(n):
                    pe.wait_ge(*gcw_ok(n - 1))
                for b in range(4):
                    last = tr(Bk[half][:, b * P:(b + 1) * P], core[:, 4 * half + b, :], ident)
                last.then_inc(coreT_ps.sem, 1)

            def project(n, half):
                pe.wait_ge(*coreT_ok(n, 1 + half))
                for h in range(4 * half, 4 * half + 4):
                    last = mm(Bk[3][:, 0:D], coreT[:, h, :], wout[:, h, :], start=(h == 0), stop=(h == HV - 1))
                if half == 1:
                    last.then_inc(out_ps.sem, 1)

            def b_cT(n):
                pe.wait_ge(*c_loaded(n))
                for c in range(KC):
                    last = tr(Bk[0][:, c * P:(c + 1) * P], cin[:, c * P:(c + 1) * P], ident)
                last.then_inc(cT_ps.sem, 1)

            def b_v(n):
                pe.wait_ge(*cT_ok(n))
                if not first(n):
                    pe.wait_ge(*ysum(n - 1))
                for c in range(KC):
                    last = mm(Bk[2][:, 0:D], cT[:, c, :], wv[:, c, :], start=(c == 0), stop=(c == KC - 1))
                last.then_inc(v_ps.sem, 1)

            def b_x2T(n):
                pe.wait_ge(*x2_ok(n))
                for c in range(KC):
                    last = tr(Bk[3][:, c * P:(c + 1) * P], x2[:, c * P:(c + 1) * P], ident)
                last.then_inc(x2T_ps.sem, 1)

            def b_router(n):
                pe.wait_ge(*x2T_ok(n))
                for c in range(KC):
                    last = mm(Bk[0][:, 0:NEXP], x2T[:, c, :], wr[:, c, :], start=(c == 0), stop=(c == KC - 1))
                last.then_inc(rl_ps.sem, 1)

            def gate_up(n, i):
                w, half, bank = ((wg, 0, 1), (wu, 0, 2), (wg, 1, 3), (wu, 1, 0))[i]
                if i == 1:
                    pe.wait_ge(*v_ok(n))
                if i == 3:
                    pe.wait_ge(*rl_ok(n))
                for c in range(KC):
                    last = mm(Bk[bank][:, :], x2T[:, c, :], w[:, c, 512 * half:512 * half + 512],
                              start=(c == 0), stop=(c == KC - 1))
                last.then_inc(gu_ps.sem, 1)

            def act_T(n, half):
                bank = (1, 3)[half]
                pe.wait_ge(*act_ok(n, 1 + half))
                for b in range(4):
                    last = tr(Bk[bank][:, b * P:(b + 1) * P], act_[:, 4 * half + b, :], ident)
                last.then_inc(actT_ps.sem, 1)

            def down(n, half):
                pe.wait_ge(*actT_ok(n, 1 + half))
                for e in range(4 * half, 4 * half + 4):
                    last = mm(Bk[2][:, 0:D], actT[:, e, :], wd[:, e, :], start=(e == 0), stop=(e == NEXP - 1))
                if half == 1:
                    last.then_inc(down_ps.sem, 1)

            def b_k(n):
                for b in range(4):
                    for c in range(KC):
                        last = mm(Bk[3][:, b * P:(b + 1) * P], wk[:, c, b * P:(b + 1) * P], cT[:, c, :],
                                  start=(c == 0), stop=(c == KC - 1))
                last.then_inc(k_ps.sem, 1)

            def b_y1T(n):
                pe.wait_ge(*yn(n, 1))
                for c in range(KC):
                    last = tr(Bk[0][:, c * P:(c + 1) * P], y1[:, c * P:(c + 1) * P], ident)
                last.then_inc(y1T_ps.sem, 1)

            def b_q(n):
                pe.wait_ge(*y1T_ok(n))
                for b in range(4):
                    for c in range(KC):
                        last = mm(Bk[1][:, b * P:(b + 1) * P], wq[:, c, b * P:(b + 1) * P], y1T[:, c, :],
                                  start=(c == 0), stop=(c == KC - 1))
                last.then_inc(q_ps.sem, 1)

            def scores(n, b):
                if b == 0:
                    pe.wait_ge(*q_ok(n))
                    pe.wait_ge(*k_ok(n))
                mm(Bk[b][:, :], qT[:, b, :], keys[:, b, :, :], start=True, stop=True).then_inc(s_ps.sem, 1)

            def prob_T(n, b):
                pe.wait_ge(*prob_ok(n, b + 1))
                for j in range(4):
                    last = tr(Bk[b][:, j * P:(j + 1) * P], prob[:, b, j, :], ident)
                last.then_inc(probT_ps.sem, 1)

            def c_R(n):
                pe.wait_ge(*pTv_ok(n, 1))
                pe.wait_ge(*rexp_ok(n))
                for b in range(4):
                    last = tr(Bk[1][:, b * P:(b + 1) * P], rexp[:, b, :], ident)
                last.then_inc(sum_ps.sem, 1)

            def c_pv(n):
                pe.wait_ge(*pTa_ok(n, 2))
                pe.wait_ge(*pTv_ok(n, 2)).then_inc(pe_passed.sem, 1)
                for j in range(4):
                    for b in range(4):
                        last = mm(Bk[0][32 * j:32 * j + 32, b * P:(b + 1) * P], vpad[:, 4 * b + j, :],
                                  probT[:, b, j, :], start=True, stop=True)
                last.then_inc(pv_ps.sem, 1)

            def c_xo(n):
                pe.wait_ge(*ao_ok(n))
                for b in range(4):
                    last = mm(Bk[2][:, 0:D], aoT[:, b, :], wo[:, b, :], start=(b == 0), stop=(b == 3))
                last.then_inc(xo_ps.sem, 1)

            def c_y2T(n):
                pe.wait_ge(*yn(n, 2))
                for c in range(KC):
                    last = tr(Bk[3][:, c * P:(c + 1) * P], y2[:, c * P:(c + 1) * P], ident)
                last.then_inc(y2T_ps.sem, 1)

            def c_h(n):
                pe.wait_ge(*y2T_ok(n))
                for c in range(KC):
                    last = mm(Bk[0][:, 0:P], w1[:, c, :], y2T[:, c, :], start=(c == 0), stop=(c == KC - 1))
                last.then_inc(hg_ps.sem, 1)
                for c in range(KC):
                    mm(Bk[1][:, 0:NCOL], y2T[:, c, :], cenT[:, c, :], start=(c == 0), stop=(c == KC - 1))

            def columns(n, half):
                for b in range(4):
                    o = (4 * half + b) * P
                    for c in range(KC):
                        last = mm(Bk[2 + half][:, b * P:(b + 1) * P], wc[:, c, o:o + P], y2T[:, c, :],
                                  start=(c == 0), stop=(c == KC - 1))
                last.then_inc(c_ps.sem, 1)

            def c_lg(n):
                pe.wait_ge(*hT_ok(n))
                mm(Bk[1][:, 32:32 + NCOL], hT[:, :], w2[:, :], start=True, stop=True).then_inc(lg_ps.sem, 1)

            def c_wT(n):
                pe.wait_ge(*lchain(n, 5))
                tr(Bk[0][0:NCOL, 0:P], onehot[:, :], ident).then_inc(wT_ps.sem, 1)

            def c_spread(n):
                pe.wait_ge(*wT_ok(n))
                for half in range(2):
                    for b in range(4):
                        o = (4 * half + b) * P
                        last = mm(Bk[half][:, b * P:(b + 1) * P], spread_bf[:, o:o + P], wT[:, :], start=True, stop=True)
                    last.then_inc(wb_ps.sem, 1)

            def mix(n, half):
                pe.wait_ge(*gcw_ok(n, 1 + half))
                for b in range(4 * half, 4 * half + 4):
                    last = mm(Bk[2][:, 0:D], gcw[:, b, :], wp[:, b, :], start=(b == 0), stop=(b == 7))
                if half == 1:
                    last.then_inc(pj_ps.sem, 1)

            pe.wait_ge(w_a.sem, W_A)
            pe.wait_ge(filled.sem, FILLS)
            pe.wait_ge(prep.sem, PREP_A)

            def before_b():
                pe.wait_ge(cen_ok.sem, 1)
                for c in range(KC):
                    last = tr(Bk[1][:, c * P:c * P + NCOL], cen[:, c * P:(c + 1) * P], const[0:NCOL, 0:NCOL])
                last.then_inc(ce_ps.sem, 1)
                pe.wait_ge(w_b.sem, W_B)
                pe.wait_ge(prep.sem, PREP_B)

            steps = dict(a_xT=a_xT, a_ba=a_ba, a_ss=a_ss, a_kk=a_kk, a_qk=a_qk, b_cT=b_cT, b_v=b_v, b_x2T=b_x2T,
                         b_router=b_router, b_k=b_k, b_y1T=b_y1T, b_q=b_q, c_R=c_R, c_pv=c_pv, c_xo=c_xo, c_y2T=c_y2T, c_h=c_h,
                         c_lg=c_lg, c_wT=c_wT, c_spread=c_spread)
            for name, f in (("a_z", zgate), ("a_vT", values), ("a_dec", exponents), ("a_sT", scores_T),
                            ("a_r", solve_r), ("a_n", solve_n), ("a_o", read), ("b_oT", core_T), ("b_w", project),
                            ("b_aT", act_T), ("b_dn", down), ("c_c", columns), ("c_pj", mix)):
                for half in range(2):
                    steps[f"{name}{half}"] = lambda n, f=f, half=half: f(n, half)
            for name, f in (("a_qkv", qkv), ("b_gu", gate_up), ("c_s", scores),
                            ("c_pT", prob_T)):
                for i in range(4):
                    steps[f"{name}{i}"] = lambda n, f=f, i=i: f(n, i)
            for name, count, f in (("a_step", 3, horner), ("a_la", 4, level_a), ("a_lb", 4, level_b)):
                for k in range(count):
                    for half in range(2):
                        steps[f"{name}{k}{half}"] = lambda n, f=f, k=k, half=half: f(n, k, half)
            run(steps, ORDER["pe"], pe, before_b)

        @block.scalar
        def _(act):
            fn = nc.scalar.activation

            def a_sum(n):
                act.wait_ge(*x_loaded(n))
                fn(junk_a[:, :], xin[:, :], ACT.Square, accum_out=st_a[:, 0:1]).then_inc(x_sumsq.sem, 1)

            def a_xT(n):
                act.wait_ge(*xnT_ps(n))
                fn(xnT[:, :, :], A[0][:, 0:D], ACT.Copy).then_inc(xnT_ok.sem, 1)

            def qkv(n, g):
                bank, block = GROUPS[g]
                act.wait_ge(*qkv_ps(n, g + 1))
                fn(ypad[:, block:block + 4, TAPS - 1:], quad(A[bank]), ACT.Copy).then_inc(y_ok.sem, 1)
                for b in range(4):
                    c = block + b
                    fn(acc[:, c, :], A[bank][:, b * P:(b + 1) * P], ACT.Copy, scale=convw[:, c, TAPS - 1:TAPS])\
                        .then_inc(tap_last.sem, 1)

            def zgate(n, half):
                act.wait_ge(*z_ps(n, 1 + half))
                fn(heads(zs, half), quad(A[1 + half]), ACT.Silu).then_inc(zs_ok.sem, 1)

            def a_ba(n):
                act.wait_ge(*ba_ps(n))
                fn(ba[:, :], A[0][:, D:D + 2 * HV], ACT.Copy).then_inc(ba_ok.sem, 1)
                act.wait_ge(*ba_ok(n))
                fn(gate[:, TB, :], ba[:, 0:HV], ACT.Tanh, scale=0.5).then_inc(tb_ok.sem, 1)

            def silu(n, g):
                block = GROUPS[g][1]
                act.wait_ge(*conv(n, 12 * g + 12))
                fn(mixed[:, block:block + 4, :], acc[:, block:block + 4, :], ACT.Silu).then_inc(mixed_ok.sem, 1)

            def a_sq(n):
                act.wait_ge(*mixed_ok(n, 2))
                fn(sqk[:, :, :], mixed[:, 0:QK_BLOCKS, :], ACT.Square).then_inc(sq_ok.sem, 1)

            def a_ln(n):
                act.wait_ge(*gates(n, 4))
                fn(gate[:, EABS, :], gate[:, NABS, :], ACT.Exp).then_inc(eln.sem, 1)
                act.wait_ge(*eln(n, 1))
                fn(gate[:, LNP, :], gate[:, EABS, :], ACT.Ln, bias=ones[:, 0:1]).then_inc(eln.sem, 1)

            def exponents(n, half):
                act.wait_ge(*decay_ps(n, 1 + half))
                fn(heads(decay, half), quad(A[(0, 3)[half]]), ACT.Exp).then_inc(decay_ok.sem, 1)

            def a_diag(n):
                act.wait_ge(*lower_ok(n))
                for b in range(NBLK):
                    r = slice(BLK * b, BLK * (b + 1))
                    last = fn(diag[r, :, :], lower[r, :, r], ACT.Copy)
                last.then_inc(diag_ok.sem, 1)

            def scores_T(n, half):
                act.wait_ge(*scoreT_ps(n, half + 1))
                fn(heads(scoreT, half), quad(A[1 + half]), ACT.Copy).then_inc(scoreT_ok.sem, 1)

            def a_zf(n):
                act.wait_ge(*z_ok(n))
                for b in range(NBLK):
                    r = slice(BLK * b, BLK * (b + 1))
                    last = fn(zfull[r, :, r], zblk[r, :, :], ACT.Copy)
                last.then_inc(zfull_ok.sem, 1)

            def solve_r(n, half):
                act.wait_ge(*r_ps(n, 1 + half))
                fn(heads(rsol, half), quad(A[1 + half]), ACT.Copy).then_inc(r_ok.sem, 1)

            def read(n, half):
                act.wait_ge(*o_ps(n, 1 + half))
                for h in range(4 * half, 4 * half + 4):
                    last = fn(junk_o[:, h, :], A[1 + half][:, (h % 4) * P:(h % 4 + 1) * P], ACT.Square,
                              accum_out=ostat[:, OSS, h:h + 1])
                last.then_inc(o_sumsq.sem, 1)

            def core_T(n, half):
                act.wait_ge(*coreT_ps(n, 1 + half))
                fn(heads(coreT, half), quad(Bk[half]), ACT.Copy).then_inc(coreT_ok.sem, 1)

            def b_cT(n):
                act.wait_ge(*cT_ps(n))
                fn(cT[:, :, :], Bk[0][:, 0:D], ACT.Copy).then_inc(cT_ok.sem, 1)

            def b_sum(n):
                act.wait_ge(*h_ok(n))
                fn(junk_b[:, :], hmid[:, :], ACT.Square, accum_out=st_b[:, 0:1]).then_inc(h_sumsq.sem, 1)

            def b_x2T(n):
                act.wait_ge(*x2T_ps(n))
                fn(x2T[:, :, :], Bk[3][:, 0:D], ACT.Copy).then_inc(x2T_ok.sem, 1)

            def b_rl(n):
                act.wait_ge(*rl_ps(n))
                fn(rl[:, :], Bk[0][:, 0:NEXP], ACT.Copy).then_inc(rl_ok.sem, 1)

            def expert_silu(n, half):
                act.wait_ge(*gu_ps(n, 1 + 2 * half))
                fn(heads(sg, half), quad(Bk[(1, 3)[half]]), ACT.Silu).then_inc(sg_ok.sem, 1)

            def b_rt(n):
                act.wait_ge(*routing(n, 1))
                fn(rmix[:, 1:2], rmix[:, 0:1], ACT.Tanh, scale=0.5).then_inc(rtanh.sem, 1)

            def act_T(n, half):
                act.wait_ge(*actT_ps(n, 1 + half))
                fn(heads(actT, half), quad(Bk[(1, 3)[half]]), ACT.Copy).then_inc(actT_ok.sem, 1)

            def b_y1T(n):
                act.wait_ge(*y1T_ps(n))
                fn(y1T[:, :, :], Bk[0][:, 0:D], ACT.Copy).then_inc(y1T_ok.sem, 1)

            def b_q(n):
                act.wait_ge(*q_ps(n))
                for b in range(4):
                    last = fn(qT[:, b, :], Bk[1][:, b * P:(b + 1) * P], ACT.Identity, bias=bq[:, b:b + 1])
                last.then_inc(q_ok.sem, 1)

            def exps(n, b):
                act.wait_ge(*nmax_ok(n, b + 1))
                for j in range(4):
                    last = fn(prob[:, b, j, :], Bk[b][:, j * P:(j + 1) * P], ACT.Exp, scale=HD ** -0.5,
                              bias=nmax[:, 4 * b + j:4 * b + j + 1], accum_out=esum[:, 4 * b + j:4 * b + j + 1])
                last.then_inc(prob_ok.sem, 1)

            def prob_T(n, i):
                act.wait_ge(*probT_ps(n, 2 * i + 1))
                fn(probT[:, 2 * i, :, :], quad(Bk[2 * i]), ACT.Copy).then_inc(pTa_ok.sem, 1)

            def c_R(n):
                act.wait_ge(*sum_ps(n))
                fn(rsum, quad(Bk[1]), ACT.Copy).then_inc(rsum_ok.sem, 1)

            def a_seg(n):
                act.wait_ge(*gates(n, 7))
                for h in range(4, HV):
                    last = fn(gseg[:, h, :], con("later"), ACT.Copy, scale=gate[:, G, h:h + 1])
                last.then_inc(gsegb_ok.sem, 1)

            def c_y2T(n):
                act.wait_ge(*y2T_ps(n))
                fn(y2T[:, :, :], Bk[3][:, 0:D], ACT.Copy).then_inc(y2T_ok.sem, 1)

            def c_h(n):
                act.wait_ge(*hg_ps(n))
                fn(hT[:, :], Bk[0][:, 0:P], ACT.Gelu, bias=b1[:, 0:1]).then_inc(hT_ok.sem, 1)

            def columns(n, half):
                act.wait_ge(*c_ps(n, 1 + half))
                for b in range(4):
                    last = fn(gc[:, 4 * half + b, :], Bk[2 + half][:, b * P:(b + 1) * P], ACT.Gelu,
                              bias=bc[:, 4 * half + b:4 * half + b + 1])
                last.then_inc(gc_ok.sem, 1)

            def c_lt(n):
                act.wait_ge(*lb_ok(n))
                fn(lg[:, LTANH, :], lg[:, LBIAS, :], ACT.Tanh, scale=0.5).then_inc(ltanh.sem, 1)

            def c_te(n):
                act.wait_ge(*lchain(n, 6))
                fn(lg[:, LTE, :], lg[:, LOGIT, :], ACT.Tanh, scale=0.5, bias=lsm[:, 1:2]).then_inc(ltanh.sem, 1)

            def c_wT(n):
                act.wait_ge(*wT_ps(n))
                fn(wT[:, :], Bk[0][0:NCOL, 0:P], ACT.Copy).then_inc(wT_ok.sem, 1)

            def before_b():
                act.wait_ge(w_b.sem, W_B)
                fn(ce_junk[:, :], ce[:, :], ACT.Square, accum_out=ce_stat[:, 0:1]).then_inc(ce_sumsq.sem, 1)

            act.wait_ge(w_a.sem, W_A)
            fn(negA[:, :], negA[:, :], ACT.Exp).then_inc(alog_exp.sem, 1)
            act.wait_ge(filled.sem, FILLS)
            steps = dict(a_sum=a_sum, a_xT=a_xT, a_ba=a_ba, a_sq=a_sq, a_ln=a_ln, a_diag=a_diag, a_zf=a_zf, a_seg=a_seg, c_R=c_R, b_cT=b_cT,
                         b_sum=b_sum, b_x2T=b_x2T, b_rl=b_rl, b_rt=b_rt, b_y1T=b_y1T, b_q=b_q, c_y2T=c_y2T, c_h=c_h,
                         c_lt=c_lt, c_te=c_te, c_wT=c_wT)
            for name, f in (("a_z", zgate), ("a_dec", exponents), ("a_sT", scores_T), ("a_r", solve_r), ("a_o", read),
                            ("b_oT", core_T), ("b_sg", expert_silu), ("b_aT", act_T), ("c_pT", prob_T),
                            ("c_c", columns)):
                for half in range(2):
                    steps[f"{name}{half}"] = lambda n, f=f, half=half: f(n, half)
            for name, f in (("a_qkv", qkv), ("a_mix", silu), ("c_exp", exps)):
                for i in range(4):
                    steps[f"{name}{i}"] = lambda n, f=f, i=i: f(n, i)
            run(steps, ORDER["act"], act, before_b)

        @block.vector
        def _(dve):
            tt, ts, stt = nc.vector.tensor_tensor, nc.vector.tensor_scalar, nc.vector.scalar_tensor_tensor

            def a_xn(n):
                dve.wait_ge(*x_rstd(n))
                dve.wait_ge(*x_loaded(n))
                ts(xn[:, :], xin[:, :], st_a[:, 2:3], None, ALU.mult).then_inc(x_norm.sem, 1)

            def taps(n, g, k):
                if k == 0:
                    dve.wait_ge(*y_ok(n, g + 1))
                for b in range(4):
                    c = GROUPS[g][1] + b
                    if k == 0:
                        dve.wait_ge(*tap_last(n, 4 * g + b + 1))
                    else:
                        dve.wait_ge(*conv(n, 12 * g + 4 * (k - 1) + b + 1))
                    stt(acc[:, c, :], ypad[:, c, k:k + P], convw[:, c, k:k + 1], acc[:, c, :],
                        ALU.mult, ALU.add).then_inc(conv.sem, 1)

            def a_ss(n):
                dve.wait_ge(*ss_ps(n))
                ts(sse[:, :], A[3][:, 0:QK_BLOCKS], EPS_RMS, None, ALU.add).then_inc(sse_ok.sem, 1)

            def values(n, half):
                if not first(n):
                    dve.wait_ge(*coreT_ps(n - 1))
                dve.wait_ge(*kscale(n, 1))
                dve.wait_ge(*vT_ps(n, 1 + half))
                tt(heads(u, half), quad(A[1 + half]), cols(krb[:, 4 * half:4 * half + 4], P), ALU.mult)\
                    .then_inc(u_ok.sem, 1)

            def a_lower(n):
                dve.wait_ge(*kk_ps(n))
                dve.wait_ge(*decay_ok(n))
                dve.wait_ge(*kscale(n, 2))
                for h in range(HV):
                    last = stt(lower[:, h, :], A[1][:, (h // 2) * P:(h // 2 + 1) * P], ckk[:, h:h + 1], decay[:, h, :],
                               ALU.mult, ALU.mult)
                last.then_inc(lower_ok.sem, 1)

            def a_score(n):
                dve.wait_ge(*qk_ps(n))
                tt(scoreqk[:, :, :].rearrange("p (a b) f -> p a b f", b=2),
                   quad(A[2]).unsqueeze(2).to_broadcast([P, 4, 2, P]),
                   decay[:, :, :].rearrange("p (a b) f -> p a b f", b=2), ALU.mult).then_inc(score_ok.sem, 1)

            def a_init(n):
                dve.wait_ge(*diag_ok(n))
                nc.vector.transpose(diagT[:, :, :], diag[:, :, :]).then_inc(init_ok.sem, 1)
                dve.wait_ge(*init_ok(n, 1))
                tt(zinit[:, :, :], diagT[:, :, :], con("level1").unsqueeze(1).to_broadcast([P, HV, BLK]), ALU.mult)\
                    .then_inc(init_ok.sem, 1)
                dve.wait_ge(*init_ok(n, 2))
                for half in range(2):
                    tt(heads(zblk, half), heads(zinit, half), con("eye_blocks").unsqueeze(1).to_broadcast([P, 4, BLK]),
                       ALU.add).then_inc(z_ok.sem, 1)
                for half in range(2):
                    dve.wait_ge(*z_ok(n, 1 + half))
                    nc.vector.transpose(heads(xblk, half), heads(zblk, half)).then_inc(x_ok.sem, 1)

            def product(half):
                return A_LEVEL[half][:, 4 * half * BLK:4 * (half + 1) * BLK].rearrange("p (h c) -> p h c", c=BLK)

            def level_a(n, k, half):
                o = CONST["levels"][0] + BLK * k
                dve.wait_ge(*la_ps(n, 2 * k + 1 + half))
                tt(heads(ablk, half), product(half), const[:, o:o + BLK].unsqueeze(1).to_broadcast([P, 4, BLK]),
                   ALU.mult).then_inc(a_ok.sem, 1)

            def level_b(n, k, half):
                dve.wait_ge(*lb_ps(n, 2 * k + 1 + half))
                tt(heads(zblk, half), heads(zblk, half), product(half), ALU.subtract).then_inc(z_ok.sem, 1)
                if k < 3:
                    dve.wait_ge(*z_ok(n, 2 * k + 3 + half))
                    nc.vector.transpose(heads(xblk, half), heads(zblk, half)).then_inc(x_ok.sem, 1)

            def solve_n(n, half):
                dve.wait_ge(*n_ps(n, 1 + half))
                tt(heads(nT, half), quad(A[(0, 3)[half]]), con("outside").unsqueeze(1).to_broadcast([P, 4, P]),
                   ALU.mult).then_inc(n_ok.sem, 1)

            def horner(n, k, half):
                dve.wait_ge(*step_ps(n, 2 * k + 1 + half))
                if k == 0:
                    dve.wait_ge(*r_ok(n, 1 + half))
                tt(heads(tsol[k % 2], half), heads(rsol, half), quad(A[(0, 3)[half]]), ALU.add)\
                    .then_inc(step_ok.sem, 1)

            def core_(n, half):
                dve.wait_ge(*o_scale(n, 6 + 4 * half))
                for h in range(4 * half, 4 * half + 4):
                    last = stt(core[:, h, :], A[1 + half][:, (h % 4) * P:(h % 4 + 1) * P], ostat[:, OSC, h:h + 1],
                               zs[:, h, :], ALU.mult, ALU.mult)
                last.then_inc(core_ok.sem, 1)

            def b_hid(n):
                dve.wait_ge(*out_ps(n))
                dve.wait_ge(*x_res(n))
                tt(hmid[:, :], xres[:, :], Bk[3][:, 0:D], ALU.add).then_inc(h_ok.sem, 1)

            def stats(n, k, y):
                nc.vector.bn_stats(bn[:, k, :], y[:, :]).then_inc(ln_bn.sem, 1)
                dve.wait_ge(*ln_bn(n, 2 * k + 1)).then_inc(dve_passed.sem, 1)
                nc.vector.bn_aggr(mv[:, k, :], bn[:, k, :]).then_inc(ln_bn.sem, 1)

            def normalize(n, k, out, y):
                dve.wait_ge(*ln_rstd(n, 2 * k + 2))
                return ts(out[:, :], y[:, :], mv[:, k, 0:1], lnv[:, k, 1:2], ALU.subtract, ALU.mult)

            def b_v(n):
                dve.wait_ge(*v_ps(n))
                tt(vpad[:, :, 0:HD], Bk[2][:, 0:D].rearrange("p (h d) -> p h d", d=HD),
                   rows[:, BV, :].rearrange("p (h d) -> p h d", d=HD), ALU.add).then_inc(v_ok.sem, 1)

            def b_x2(n):
                dve.wait_ge(*h_rstd(n))
                ts(x2[:, :], hmid[:, :], st_b[:, 2:3], None, ALU.mult).then_inc(x2_ok.sem, 1)

            def b_top(n):
                dve.wait_ge(*rl_ok(n)).then_inc(dve_passed.sem, 1)
                nc.vector.max(top8[:, :], rl[:, :]).then_inc(top_ok.sem, 1)
                dve.wait_ge(*top_ok(n, 1)).then_inc(dve_passed.sem, 1)
                nc.vector.max_index(idx8[:, :], top8[:, :], rl[:, :]).then_inc(top_ok.sem, 1)
                dve.wait_ge(*top_ok(n, 2))
                nc.vector.tensor_copy(idxf[:, :], idx8[:, 0:2]).then_inc(top_ok.sem, 1)

            def routed(n, half):
                dve.wait_ge(*routing(n))
                dve.wait_ge(*gu_ps(n, 2 + 2 * half))
                dve.wait_ge(*sg_ok(n, 1 + half))
                for b in range(4):
                    e = 4 * half + b
                    last = stt(act_[:, e, :], Bk[(2, 0)[half]][:, b * P:(b + 1) * P], route[:, e:e + 1], sg[:, e, :],
                               ALU.mult, ALU.mult)
                last.then_inc(act_ok.sem, 1)

            def b_sum1(n):
                dve.wait_ge(*down_ps(n))
                dve.wait_ge(*xh_ok(n))
                tt(y1p[:, :], xh[:, :], Bk[2][:, 0:D], ALU.add).then_inc(ysum.sem, 1)
                dve.wait_ge(*ysum(n, 1))
                stats(n, 0, y1p)

            def b_k(n):
                dve.wait_ge(*k_ps(n))
                dve.wait_ge(*madj_ok(n))
                for b in range(4):
                    last = stt(keys[:, b, :, :], Bk[3][:, b * P:(b + 1) * P].unsqueeze(1).to_broadcast([P, 4, P]),
                               bk[:, b:b + 1], madj[:, :, :], ALU.add, ALU.mult)
                last.then_inc(k_ok.sem, 1)

            def b_y1(n):
                normalize(n, 0, y1, y1p).then_inc(yn.sem, 1)

            def smaxes(n, b):
                dve.wait_ge(*s_ps(n, b + 1))
                nc.vector.tensor_reduce(smax[:, 4 * b:4 * b + 4], quad(Bk[b]), AX_X, ALU.max).then_inc(smax_ok.sem, 1)
                dve.wait_ge(*smax_ok(n, b + 1))
                ts(nmax[:, 4 * b:4 * b + 4], smax[:, 4 * b:4 * b + 4], -HD ** -0.5, None, ALU.mult)\
                    .then_inc(nmax_ok.sem, 1)

            def prob_T(n, i):
                dve.wait_ge(*probT_ps(n, 2 * i + 2))
                nc.vector.tensor_copy(probT[:, 2 * i + 1, :, :], quad(Bk[2 * i + 1])).then_inc(pTv_ok.sem, 1)

            def c_rec(n):
                dve.wait_ge(*prob_ok(n))
                nc.vector.reciprocal(rinv[:, :], esum[:, :]).then_inc(rinv_ok.sem, 1)
                dve.wait_ge(*rinv_ok(n))
                dve.wait_ge(*probT_ps(n))
                nc.vector.tensor_copy(rexp.rearrange("p a (j r) -> p (a j) r", r=32), cols(rinv[:, :], 32))\
                    .then_inc(rexp_ok.sem, 1)

            def c_ao(n):
                dve.wait_ge(*rsum_ok(n))
                dve.wait_ge(*pv_ps(n))
                tt(aoT, rsum, quad(Bk[0]), ALU.mult).then_inc(ao_ok.sem, 1)

            def c_sum2(n):
                dve.wait_ge(*xo_ps(n))
                dve.wait_ge(*y1b_ok(n))
                tt(y2p[:, :], y1b[:, :], Bk[2][:, 0:D], ALU.add).then_inc(ysum.sem, 1)
                dve.wait_ge(*ysum(n, 2))
                stats(n, 1, y2p)

            def c_y2(n):
                normalize(n, 1, y2, y2p).then_inc(yn.sem, 1)

            def c_lb(n):
                dve.wait_ge(*lg_ps(n))
                tt(lg[:, LBIAS, :], Bk[1][:, 32:32 + NCOL], b2[:, :], ALU.add).then_inc(lb_ok.sem, 1)

            def c_route(n):
                dve.wait_ge(*lsig(n))
                dve.wait_ge(*rx_ok(n))
                stt(lg[:, LOGIT, :], Bk[1][:, 0:NCOL], rx[:, 2:3], lg[:, LSIG, :], ALU.mult, ALU.add)\
                    .then_inc(lchain.sem, 1)
                dve.wait_ge(*lchain(n, 1)).then_inc(dve_passed.sem, 1)
                nc.vector.max(lmax[:, :], lg[:, LOGIT, :]).then_inc(lchain.sem, 1)
                dve.wait_ge(*lchain(n, 2)).then_inc(dve_passed.sem, 1)
                nc.vector.max_index(lidx[:, :], lmax[:, :], lg[:, LOGIT, :]).then_inc(lchain.sem, 1)
                dve.wait_ge(*lchain(n, 3))
                nc.vector.tensor_copy(lsm[:, 0:1], lidx[:, 0:1]).then_inc(lchain.sem, 1)
                dve.wait_ge(*lchain(n, 4))
                ts(onehot[:, :], con("iota"), lsm[:, 0:1], None, ALU.is_equal).then_inc(lchain.sem, 1)
                ts(lsm[:, 1:2], lmax[:, 0:1], -0.5, None, ALU.mult).then_inc(lchain.sem, 1)

            def c_weight(n):
                dve.wait_ge(*ltanh(n, 2))
                ts(lg[:, LNUM, :], lg[:, LTE, :], 1.0, None, ALU.add).then_inc(lchain.sem, 1)
                ts(lg[:, LDEN, :], lg[:, LTE, :], -1.0, 1.0, ALU.mult, ALU.add).then_inc(lchain.sem, 1)
                dve.wait_ge(*lchain(n, 8))
                nc.vector.reciprocal(lrec[:, :], lg[:, LDEN, :]).then_inc(lchain.sem, 1)
                dve.wait_ge(*lchain(n, 9))
                nc.vector.tensor_tensor_reduce(out=lg[:, LEXP, :], in0=lg[:, LNUM, :], in1=lrec[:, :], scale=1.0,
                                               scalar=0.0, op0=ALU.mult, op1=ALU.add, accum_out=lsm[:, 2:3])\
                    .then_inc(lchain.sem, 1)
                dve.wait_ge(*lchain(n, 10))
                nc.vector.reciprocal(lsm[:, 3:4], lsm[:, 2:3]).then_inc(lchain.sem, 1)

            def gated(n, half):
                dve.wait_ge(*wb_ps(n, 1 + half))
                dve.wait_ge(*gc_ok(n, 1 + half))
                tt(heads(gcw, half), heads(gc, half), quad(Bk[half]), ALU.mult).then_inc(gcw_ok.sem, 1)

            def c_sum3(n):
                dve.wait_ge(*pj_ps(n))
                dve.wait_ge(*y2b_ok(n))
                dve.wait_ge(*lchain(n, 11))
                stt(y3p[:, :], Bk[2][:, 0:D], lsm[:, 3:4], y2pb[:, :], ALU.mult, ALU.add).then_inc(ysum.sem, 1)
                dve.wait_ge(*ysum(n, 3))
                stats(n, 2, y3p)

            def c_y3(n):
                normalize(n, 2, y3, y3p).then_inc(yn.sem, 1)
                dve.wait_ge(*yn(n, 3))
                tt(y3g[:, :], y3[:, :], rows[:, LG, :], ALU.mult).then_inc(y3_ok.sem, 1)
                dve.wait_ge(*y3_ok(n, 1))
                tt(y4[:, :], y3g[:, :], y2lb[:, :], ALU.add).then_inc(y3_ok.sem, 1)
                dve.wait_ge(*y3_ok(n, 2))
                stats(n, 3, y4)

            def c_y4(n):
                if not first(n):
                    dve.wait_ge(*stored(n - 1))
                normalize(n, 3, yout, y4).then_inc(y_out.sem, 1)

            dve.wait_ge(w_a.sem, W_A)
            dve.wait_ge(filled.sem, FILLS)
            ts(ln12[:, :, :], ln12[:, :, :], 1.0, None, ALU.add).then_inc(prep.sem, 1)
            nc.vector.tensor_copy(ident_bf[:, :], ident).then_inc(prep.sem, 1)
            nc.vector.tensor_copy(quad(above_bf), con("above").unsqueeze(1).to_broadcast([P, 4, P])).then_inc(prep.sem, 1)
            ts(wout[:, :, :], wout[:, :, :], gnw[:, 0:1], None, ALU.mult).then_inc(prep.sem, 1)
            dve.wait_ge(prep.sem, 4)
            for c in range(KC):
                ts(wqkvz[:, c, :], wqkvz[:, c, :], ln12[:, 0, c:c + 1], None, ALU.mult).then_inc(prep.sem, 1)
                ts(wba[:, c, :], wba[:, c, :], ln12[:, 0, c:c + 1], None, ALU.mult).then_inc(prep.sem, 1)
            dve.wait_ge(alog_exp.sem, 1)
            ts(negA[:, :], negA[:, :], -1.0, None, ALU.mult).then_inc(prep.sem, 1)

            def before_b():
                dve.wait_ge(w_b.sem, W_B)
                for c in range(KC):
                    ts(wr[:, c, :], wr[:, c, :], ln12[:, 1, c:c + 1], None, ALU.mult)
                    ts(wg[:, c, :], wg[:, c, :], ln12[:, 1, c:c + 1], None, ALU.mult)
                    ts(wu[:, c, :], wu[:, c, :], ln12[:, 1, c:c + 1], None, ALU.mult).then_inc(prep.sem, 1)
                nc.vector.tensor_copy(spread_bf[:, :], spread_in).then_inc(prep.sem, 1)
                dve.wait_ge(ce_rnorm.sem, 2)
                ts(cen[:, :], ce[:, :], ce_stat[:, 2:3], None, ALU.mult).then_inc(cen_ok.sem, 1)
                dve.wait_ge(ce_ps.sem, 1)
                for c in range(KC):
                    nc.vector.tensor_copy(cenT[:, c, :], Bk[1][:, c * P:c * P + NCOL]).then_inc(prep.sem, 1)

            steps = dict(a_xn=a_xn, a_ss=a_ss, a_lower=a_lower, a_score=a_score, a_init=a_init, b_hid=b_hid, c_rec=c_rec, b_v=b_v,
                         b_x2=b_x2, b_top=b_top, b_sum1=b_sum1, b_k=b_k, b_y1=b_y1, c_ao=c_ao, c_sum2=c_sum2,
                         c_y2=c_y2, c_lb=c_lb, c_route=c_route, c_weight=c_weight, c_sum3=c_sum3, c_y3=c_y3,
                         c_y4=c_y4)
            for name, f in (("a_u", values), ("a_n", solve_n), ("a_core", core_), ("b_act", routed), ("c_pT", prob_T),
                            ("c_gc", gated)):
                for half in range(2):
                    steps[f"{name}{half}"] = lambda n, f=f, half=half: f(n, half)
            for name, f in (("c_max", smaxes),):
                for i in range(4):
                    steps[f"{name}{i}"] = lambda n, f=f, i=i: f(n, i)
            for name, count, f in (("a_step", 3, horner), ("a_la", 4, level_a), ("a_lb", 4, level_b)):
                for k in range(count):
                    for half in range(2):
                        steps[f"{name}{k}{half}"] = lambda n, f=f, k=k, half=half: f(n, k, half)
            for g in range(4):
                for k in range(TAPS - 1):
                    steps[f"a_conv{g}{k}"] = lambda n, g=g, k=k: taps(n, g, k)
            run(steps, ORDER["dve"], dve, before_b)

        @block.gpsimd
        def _(pool):
            tt, ts = nc.gpsimd.tensor_tensor, nc.gpsimd.tensor_scalar

            def power(out, base):
                return tt(out, base, nhalf[:, 0:base.shape[-1]], ALU.pow)

            def a_x(n):
                pool.wait_ge(*x_loaded(n))
                pool.wait_ge(*x_sumsq(n)).then_inc(pool_passed.sem, 1)
                ts(st_a[:, 1:2], st_a[:, 0:1], 1.0 / D, EPS_RMS, ALU.mult, ALU.add).then_inc(x_rstd.sem, 1)
                pool.wait_ge(*x_rstd(n, 1))
                power(st_a[:, 2:3], st_a[:, 1:2]).then_inc(x_rstd.sem, 1)

            def a_xr(n):
                if not first(n):
                    pool.wait_ge(*xh_ok(n - 1)).then_inc(pool_passed.sem, 1)
                ts(xres[:, :], xin[:, :], 1.0, 0.0, ALU.mult, ALU.add).then_inc(x_res.sem, 1)

            def a_ga(n):
                pool.wait_ge(*ba_ok(n))
                tt(gate[:, ADT, :], ba[:, HV:2 * HV], dtb[:, :], ALU.add).then_inc(gates.sem, 1)
                pool.wait_ge(*gates(n, 1)).then_inc(pool_passed.sem, 1)
                ts(gate[:, SPM, :], gate[:, ADT, :], 0.0, 0.0, ALU.max, ALU.add).then_inc(gates.sem, 1)
                ts(gate[:, MINA, :], gate[:, ADT, :], 0.0, 0.0, ALU.min, ALU.add).then_inc(gates.sem, 1)
                pool.wait_ge(*gates(n, 3))
                tt(gate[:, NABS, :], gate[:, MINA, :], gate[:, SPM, :], ALU.subtract).then_inc(gates.sem, 1)
                pool.wait_ge(*tb_ok(n)).then_inc(pool_passed.sem, 1)
                ts(gate[:, BETA, :], gate[:, TB, :], 0.5, 0.5, ALU.mult, ALU.add).then_inc(gates.sem, 1)

            def pairs(ap):
                return ap.rearrange("p (a b) -> p a b", b=HV // HK)

            def a_sc(n):
                pool.wait_ge(*sse_ok(n))
                power(rqk[:, :], sse[:, :]).then_inc(rqk_ok.sem, 1)
                pool.wait_ge(*rqk_ok(n))
                pool.wait_ge(*gates(n, 5))
                rk = cols(rqk[:, HK:2 * HK], HV // HK)
                tt(pairs(krb[:, :]), pairs(gate[:, BETA, :]), rk, ALU.mult).then_inc(kscale.sem, 1)
                pool.wait_ge(*kscale(n, 1))
                tt(pairs(ckk[:, :]), pairs(krb[:, :]), rk, ALU.mult).then_inc(kscale.sem, 1)

            def a_g(n):
                pool.wait_ge(*eln(n))
                tt(gate[:, SP, :], gate[:, SPM, :], gate[:, LNP, :], ALU.add).then_inc(gates.sem, 1)
                pool.wait_ge(*gates(n, 6))
                tt(gate[:, G, :], gate[:, SP, :], negA[:, :], ALU.mult).then_inc(gates.sem, 1)
                pool.wait_ge(*gates(n, 7)).then_inc(pool_passed.sem, 1)
                for h in range(4):
                    last = ts(gseg[:, h, :], con("later"), gate[:, G, h:h + 1], None, ALU.mult)
                last.then_inc(gseg_ok.sem, 1)

            def a_rq(n):
                ts(ostat[:, RQS, 0:HK], rqk[:, 0:HK], DK ** -0.5, 0.0, ALU.mult, ALU.add).then_inc(o_scale.sem, 1)
                pool.wait_ge(*o_scale(n, 1))
                rq = cols(ostat[:, RQS, 0:HK], HV // HK)
                tt(pairs(ostat[:, RQ2, :]), rq, rq, ALU.mult).then_inc(o_scale.sem, 1)

            def out_scale(n, half):
                h, done = slice(4 * half, 4 * half + 4), 2 + 4 * half
                pool.wait_ge(*o_scale(n, done))
                pool.wait_ge(*o_sumsq(n, 1 + half))
                tt(ostat[:, OM, h], ostat[:, OSS, h], ostat[:, RQ2, h], ALU.mult).then_inc(o_scale.sem, 1)
                pool.wait_ge(*o_scale(n, done + 1)).then_inc(pool_passed.sem, 1)
                ts(ostat[:, OV, h], ostat[:, OM, h], 1.0 / P, EPS_RMS, ALU.mult, ALU.add).then_inc(o_scale.sem, 1)
                pool.wait_ge(*o_scale(n, done + 2))
                power(ostat[:, OP, h], ostat[:, OV, h]).then_inc(o_scale.sem, 1)
                pool.wait_ge(*o_scale(n, done + 3))
                tt(pairs(ostat[:, OSC, h]), pairs(ostat[:, OP, h]), cols(ostat[:, RQS, 2 * half:2 * half + 2], 2),
                   ALU.mult).then_inc(o_scale.sem, 1)

            def b_xh(n):
                pool.wait_ge(*h_ok(n))
                tt(xh[:, :], hmid[:, :], xres[:, :], ALU.add).then_inc(xh_ok.sem, 1)

            def b_mask(n):
                pool.wait_ge(*m_loaded(n)).then_inc(pool_passed.sem, 1)
                q = CONST["quadrant"][0]
                for j in range(4):
                    last = ts(madj[:, j, :], m_u8[:, :], con("mask_row"), const[:, q + j:q + j + 1], ALU.add, ALU.mult)
                last.then_inc(madj_ok.sem, 1)

            def b_rs(n):
                pool.wait_ge(*h_sumsq(n)).then_inc(pool_passed.sem, 1)
                ts(st_b[:, 1:2], st_b[:, 0:1], 1.0 / D, EPS_RMS, ALU.mult, ALU.add).then_inc(h_rstd.sem, 1)
                pool.wait_ge(*h_rstd(n, 1))
                power(st_b[:, 2:3], st_b[:, 1:2]).then_inc(h_rstd.sem, 1)

            def b_rd(n):
                pool.wait_ge(*top_ok(n))
                tt(rmix[:, 0:1], top8[:, 0:1], top8[:, 1:2], ALU.subtract).then_inc(routing.sem, 1)

            def b_rt(n):
                pool.wait_ge(*rtanh(n)).then_inc(pool_passed.sem, 1)
                for i, sign in enumerate((0.5, -0.5)):
                    ts(rmix[:, 2 + i:3 + i], rmix[:, 1:2], sign, 0.5, ALU.mult, ALU.add).then_inc(routing.sem, 1)
                pool.wait_ge(*routing(n, 3)).then_inc(pool_passed.sem, 1)
                for i in range(2):
                    ts(r12[:, i, :], const[:, CONST["iota"][0]:CONST["iota"][0] + NEXP], idxf[:, i:i + 1],
                       rmix[:, 2 + i:3 + i], ALU.is_equal, ALU.mult).then_inc(routing.sem, 1)
                pool.wait_ge(*routing(n, 5))
                tt(route[:, :], r12[:, 0, :], r12[:, 1, :], ALU.add).then_inc(routing.sem, 1)

            def rstd(n, k):
                pool.wait_ge(*ln_bn(n, 2 * k + 2)).then_inc(pool_passed.sem, 1)
                ts(lnv[:, k, 0:1], mv[:, k, 1:2], 1.0, EPS_LN, ALU.mult, ALU.add).then_inc(ln_rstd.sem, 1)
                pool.wait_ge(*ln_rstd(n, 2 * k + 1))
                power(lnv[:, k, 1:2], lnv[:, k, 0:1]).then_inc(ln_rstd.sem, 1)

            def b_y1b(n):
                pool.wait_ge(*yn(n, 1))
                tt(y1b[:, :], y1[:, :], rows[:, BO, :], ALU.add).then_inc(y1b_ok.sem, 1)

            def c_rx(n):
                pool.wait_ge(*ln_rstd(n, 4)).then_inc(pool_passed.sem, 1)
                ts(rx[:, 0:1], mv[:, 1, 1:2], lnv[:, 1, 1:2], lnv[:, 1, 1:2], ALU.mult, ALU.mult).then_inc(rx_ok.sem, 1)
                pool.wait_ge(*rx_ok(n, 1)).then_inc(pool_passed.sem, 1)
                ts(rx[:, 1:2], rx[:, 0:1], float(D), 1e-24, ALU.mult, ALU.max).then_inc(rx_ok.sem, 1)
                pool.wait_ge(*rx_ok(n, 2))
                power(rx[:, 2:3], rx[:, 1:2]).then_inc(rx_ok.sem, 1)

            def c_y2b(n):
                pool.wait_ge(*yn(n, 2))
                for out, row in ((y2pb, BP), (y2lb, LB)):
                    tt(out[:, :], y2[:, :], rows[:, row, :], ALU.add).then_inc(y2b_ok.sem, 1)

            def c_sig(n):
                pool.wait_ge(*ltanh(n, 1)).then_inc(pool_passed.sem, 1)
                ts(lg[:, LSIG, :], lg[:, LTANH, :], 0.5, 0.5, ALU.mult, ALU.add).then_inc(lsig.sem, 1)

            nc.gpsimd.memset(nhalf[:, :], -0.5).then_inc(filled.sem, 1)
            nc.gpsimd.memset(ones[:, :], 1.0).then_inc(filled.sem, 1)
            nc.gpsimd.memset(ypad[:, :, 0:TAPS - 1], 0.0).then_inc(filled.sem, 1)
            nc.gpsimd.memset(zfull[:, :, :], 0.0).then_inc(filled.sem, 1)
            nc.gpsimd.memset(vpad[:, :, :], 0.0).then_inc(filled.sem, 1)
            pool.wait_ge(filled.sem, FILLS)
            def before_b():
                pool.wait_ge(ce_sumsq.sem, 1)
                ts(ce_stat[:, 1:2], ce_stat[:, 0:1], 1.0, 1e-24, ALU.mult, ALU.max).then_inc(ce_rnorm.sem, 1)
                pool.wait_ge(ce_rnorm.sem, 1)
                tt(ce_stat[:, 2:3], ce_stat[:, 1:2], nhalf[0:NCOL, 0:1], ALU.pow).then_inc(ce_rnorm.sem, 1)
                pool.wait_ge(w_b.sem, W_B)

            pool.wait_ge(w_a.sem, W_A)
            pool.wait_ge(prep.sem, PREP_A)
            steps = dict(a_x=a_x, a_ga=a_ga, a_sc=a_sc, a_g=a_g, a_rq=a_rq, a_osc0=lambda n: out_scale(n, 0),
                         a_osc1=lambda n: out_scale(n, 1), a_xr=a_xr, b_xh=b_xh, b_mask=b_mask, b_rs=b_rs, b_rd=b_rd,
                         b_rt=b_rt, b_y1b=b_y1b, c_rx=c_rx, c_y2b=c_y2b, c_sig=c_sig)
            for k, name in enumerate(("b_ln0", "c_ln1", "c_ln2", "c_ln3")):
                steps[name] = lambda n, k=k: rstd(n, k)
            run(steps, ORDER["pool"], pool, before_b)


def kernel(**inputs):
    import concourse.bacc as bacc
    from concourse.bass_utils import run_bass_kernel_spmd

    a = {k.split("_", 2)[2] if k.startswith("L0") else k: np.asarray(v) for k, v in inputs.items()}

    def rows_first(w):
        return w.reshape(-1, P, w.shape[-1]).transpose(1, 0, 2)

    def experts(w):
        e, d, i = w.shape
        return w.reshape(e, KC, P, i).transpose(2, 1, 0, 3).reshape(P, KC, e * i)

    def padded_heads(w):
        out = np.zeros((4, 4, 32, D), w.dtype)
        out[:, :, :HD] = w.reshape(4, 4, HD, D)
        return out.reshape(4 * P, D)

    def head_rows(w):
        return rows_first(padded_heads(w).T)

    def head_bias(b, extra):
        out = np.zeros((4, 4, 32), b.dtype)
        out[:, :, :HD] = b.reshape(4, 4, HD)
        out[:, :, HD] = extra
        return out.transpose(1, 2, 0).reshape(P, 4)

    arrays = dict(
        x=a["x"], ctx=a["ctx_1024"], mask=a["mask_BxS2_bf1"].astype(np.uint8)[:, None, :], const=constants(), spread=spread(),
        wqkvz=rows_first(a["W_qkvz"]), wba=rows_first(a["W_ba"]),
        convw=a["conv_w"].reshape(CONV_BLOCKS, P, TAPS).transpose(1, 0, 2),
        ln12=np.stack([a["w_ln1"].reshape(KC, P).T, a["w_ln2"].reshape(KC, P).T], 1),
        dt=a["dt_bias"], alog=a["A_log"], gnw=a["gate_norm_w"][:, None], wout=rows_first(a["W_out"]),
        wr=rows_first(a["W_router"]), wg=experts(a["W_gate_e"]), wu=experts(a["W_up_e"]),
        wd=a["W_down_e"].transpose(1, 0, 2),
        wq=head_rows(a["Wq"]), wk=head_rows(a["Wk"]), wv=rows_first(a["Wv"].T), wo=rows_first(padded_heads(a["Wo"].T)),
        bq=head_bias(a["bq"], 1.0), bk=head_bias(a["bk"], FILL), bv=a["bv"], bo=a["bo"],
        ce=a["col_emb"], w1=rows_first(a["gate_w1"]), b1=a["gate_b1"][:, None], w2=a["gate_w2"], b2=a["gate_b2"],
        wc=experts(a["W_cols"]), bc=a["b_cols"].reshape(8, P).T, wp=rows_first(a["proj_w"]), bp=a["proj_b"],
        lng=a["ln_g"], lnb=a["ln_b"])
    nc = bacc.Bacc("TRN2", target_bir_lowering=False, num_devices=1)
    data, args = {}, []
    for name, v in arrays.items():
        v = np.ascontiguousarray(v)
        data[f"in_{name}_dram"] = v
        args.append(nc.dram_tensor(f"in_{name}_dram", v.shape, mybir.dt.from_np(v.dtype), kind="ExternalInput").ap())
    args.append(nc.dram_tensor("out_0_dram", a["x"].shape, F32, kind="ExternalOutput").ap())
    build(nc, *args)
    r = run_bass_kernel_spmd(nc, [data], core_ids=[0])
    return r.results[0]["out_0_dram"]
```
